# Optimizing a Trainium2 kernel written in Bass

```python
import numpy as np
import jax
import jax.numpy as jnp

def _softmax(x, axis=-1):
    return jax.nn.softmax(x, axis=axis)

def _gelu(x):
    return jax.nn.gelu(x, approximate=True)

def _silu(x):
    return jax.nn.silu(x)

def _sigmoid(x):
    return jax.nn.sigmoid(x)

def _layernorm(x, axis=-1, eps=1e-05):
    m = jnp.mean(x, axis=axis, keepdims=True)
    v = jnp.var(x, axis=axis, keepdims=True)
    return (x - m) / jnp.sqrt(v + eps)

def _scatter_add(tgt, idx, src, axis=0):
    return tgt.at[idx].add(src)

def _segment_sum(src, seg, n):
    return jax.ops.segment_sum(src, seg, n)
kernel_name = 'mk_prb_d2_jaxref_r8_509bee'

def setup_inputs(seed: int=0):
    np.random.seed(seed)
    _w = jnp.asarray

    def _L0_attn_setup():
        import jax, jax.numpy as jnp
        import numpy as np
        import math
        B, N, D, H = (1, 512, 128, 16)
        HS = D // H
        NEG_INF = -10000.0
        key = jax.random.key(seed)
        k1, k2, k3, k4, k5 = jax.random.split(key, 5)
        return {'encodings': jax.random.normal(k1, (B, N, D), dtype=jnp.float32), 'attn_W': jax.random.normal(k2, (D, 3 * D), dtype=jnp.float32) * 0.02, 'attn_b': jax.random.normal(k3, (3 * D,), dtype=jnp.float32) * 0.02, 'out_W': jax.random.normal(k4, (D, D), dtype=jnp.float32) * 0.02, 'out_b': jax.random.normal(k5, (D,), dtype=jnp.float32) * 0.02}
    _L0_attn_in = _L0_attn_setup()

    def _L0_ffn_setup():
        import jax, jax.numpy as jnp
        import numpy as np
        TOP_K = 2
        key = jax.random.key(seed)
        ks = jax.random.split(key, 6)
        B, T, D, H, E = (4, 256, 128, 512, 8)
        s = 0.02
        return {'x': jax.random.normal(ks[0], (B, T, D), dtype=jnp.float32), 'Wg': jax.random.normal(ks[1], (E, D), dtype=jnp.float32) * s, 'W1': jax.random.normal(ks[2], (E, H, D), dtype=jnp.float32) * s, 'b1': jax.random.normal(ks[3], (E, H), dtype=jnp.float32) * s, 'W2': jax.random.normal(ks[4], (E, D, H), dtype=jnp.float32) * s, 'b2': jax.random.normal(ks[5], (E, D), dtype=jnp.float32) * s}
    _L0_ffn_in = _L0_ffn_setup()

    def _L1_attn_setup():
        import jax, jax.numpy as jnp
        import numpy as np
        DIM = 128
        key = jax.random.key(seed)
        kx, kw = jax.random.split(key)
        x = jax.random.normal(kx, (4, 256, DIM), dtype=jnp.float32)
        W_qkv = jax.random.normal(kw, (3 * DIM, DIM), dtype=jnp.float32) * DIM ** (-0.5)
        return {'x': x, 'W_qkv': W_qkv}
    _L1_attn_in = _L1_attn_setup()

    def _L1_ffn_setup():
        import jax, jax.numpy as jnp
        import numpy as np
        H = 128
        DFF = 512
        E_ROUTED = 7
        TOP_K = 2

        def _swiglu(flat, gate_w, up_w, down_w):
            g = flat @ gate_w.T
            up = flat @ up_w.T
            return jax.nn.silu(g) * up @ down_w.T
        key = jax.random.key(seed)
        ks = jax.random.split(key, 8)
        s = 0.02
        return {'x': jax.random.normal(ks[0], (4, 256, H), jnp.float32), 'shared_up': jax.random.normal(ks[1], (DFF, H), jnp.float32) * s, 'shared_gate': jax.random.normal(ks[2], (DFF, H), jnp.float32) * s, 'shared_down': jax.random.normal(ks[3], (H, DFF), jnp.float32) * s, 'routed_up': jax.random.normal(ks[4], (E_ROUTED, DFF, H), jnp.float32) * s, 'routed_gate': jax.random.normal(ks[5], (E_ROUTED, DFF, H), jnp.float32) * s, 'routed_down': jax.random.normal(ks[6], (E_ROUTED, H, DFF), jnp.float32) * s, 'router_w': jax.random.normal(ks[7], (E_ROUTED, H), jnp.float32) * 0.02}
    _L1_ffn_in = _L1_ffn_setup()
    _d = {'L0_attn_encodings': _L0_attn_in['encodings'], 'L0_attn_attn_W': _L0_attn_in['attn_W'], 'L0_attn_attn_b': _L0_attn_in['attn_b'], 'L0_attn_out_W': _L0_attn_in['out_W'], 'L0_attn_out_b': _L0_attn_in['out_b'], 'L0_ffn_Wg': _L0_ffn_in['Wg'], 'L0_ffn_W1': _L0_ffn_in['W1'], 'L0_ffn_b1': _L0_ffn_in['b1'], 'L0_ffn_W2': _L0_ffn_in['W2'], 'L0_ffn_b2': _L0_ffn_in['b2'], 'L1_attn_W_qkv': _L1_attn_in['W_qkv'], 'L1_ffn_shared_up': _L1_ffn_in['shared_up'], 'L1_ffn_shared_gate': _L1_ffn_in['shared_gate'], 'L1_ffn_shared_down': _L1_ffn_in['shared_down'], 'L1_ffn_routed_up': _L1_ffn_in['routed_up'], 'L1_ffn_routed_gate': _L1_ffn_in['routed_gate'], 'L1_ffn_routed_down': _L1_ffn_in['routed_down'], 'L1_ffn_router_w': _L1_ffn_in['router_w']}
    _x0 = _d['L0_attn_encodings']
    _d['L0_attn_encodings'] = jax.random.normal(jax.random.fold_in(jax.random.key(seed), 1), (32, 256, 128), dtype=_x0.dtype)
    del _x0
    return _d

def reference(L0_attn_encodings, L0_attn_attn_W, L0_attn_attn_b, L0_attn_out_W, L0_attn_out_b, L0_ffn_Wg, L0_ffn_W1, L0_ffn_b1, L0_ffn_W2, L0_ffn_b2, L1_attn_W_qkv, L1_ffn_shared_up, L1_ffn_shared_gate, L1_ffn_shared_down, L1_ffn_routed_up, L1_ffn_routed_gate, L1_ffn_routed_down, L1_ffn_router_w):

    def _L0_attn_ref(encodings, attn_W, attn_b, out_W, out_b):
        import jax, jax.numpy as jnp
        import numpy as np
        import math
        B, N, D, H = (1, 512, 128, 16)
        HS = D // H
        NEG_INF = -10000.0
        b, n, d = encodings.shape
        qkv = encodings @ attn_W + attn_b
        qkv = qkv.reshape(b, n, H, 3 * HS).transpose(0, 2, 1, 3)
        q, k, v = jnp.split(qkv, 3, axis=-1)
        scores = jnp.einsum('bhki,bhqi->bhkq', k, q) / math.sqrt(HS)
        mask = jnp.arange(n)[:, None] <= jnp.arange(n)[None, :]
        scores = jnp.where(mask, scores, jnp.float32(NEG_INF))
        prob = jax.nn.softmax(scores, axis=2)
        combined = jnp.einsum('bhkq,bhkl->bhql', prob, v)
        out = combined.transpose(0, 2, 1, 3).reshape(b, n, d)
        return out @ out_W + out_b

    def _L0_ffn_ref(x, Wg, W1, b1, W2, b2):
        import jax, jax.numpy as jnp
        import numpy as np
        TOP_K = 2
        B, T, D = x.shape
        N = B * T
        xf = x.reshape(N, D)
        logits = jnp.einsum('nd,ed->ne', xf, Wg)
        top_logits, top_idx = jax.lax.top_k(logits, TOP_K)
        top_w = jax.nn.softmax(top_logits, axis=-1)
        h = jax.nn.gelu(jnp.einsum('nd,ehd->neh', xf, W1) + b1[None], approximate=False)
        all_out = jnp.einsum('neh,edh->ned', h, W2) + b2[None]
        selected = jnp.take_along_axis(all_out, top_idx[:, :, None], axis=1)
        out = jnp.sum(selected * top_w[:, :, None], axis=1)
        return out.reshape(B, T, D)

    def _L1_attn_ref(x, W_qkv):
        import jax, jax.numpy as jnp
        import numpy as np
        DIM = 128
        qkv = jnp.einsum('bnd,ed->bne', x, W_qkv)
        B, N, _ = qkv.shape
        qkv = qkv.reshape(B, N, 3, DIM).transpose(2, 0, 1, 3)
        q, k, v = (qkv[0], qkv[1], qkv[2])
        scale = DIM ** (-0.5)
        attn = jnp.einsum('bnd,bmd->bnm', q * scale, k)
        attn = jax.nn.softmax(attn, axis=-1)
        out = jnp.einsum('bnm,bmd->bnd', attn, v)
        return out

    def _L1_ffn_ref(x, shared_up, shared_gate, shared_down, routed_up, routed_gate, routed_down, router_w):
        import jax, jax.numpy as jnp
        import numpy as np
        H = 128
        DFF = 512
        E_ROUTED = 7
        TOP_K = 2

        def _swiglu(flat, gate_w, up_w, down_w):
            g = flat @ gate_w.T
            up = flat @ up_w.T
            return jax.nn.silu(g) * up @ down_w.T
        orig_shape = x.shape
        flat = x.reshape(-1, H)
        out = _swiglu(flat, shared_gate, shared_up, shared_down)
        logits = flat @ router_w.T
        probs = jax.nn.softmax(logits, axis=-1)
        top_vals, top_idx = jax.lax.top_k(probs, TOP_K)
        top_vals = top_vals / (top_vals.sum(-1, keepdims=True) + 1e-09)
        combine = jnp.sum(jax.nn.one_hot(top_idx, E_ROUTED, dtype=flat.dtype) * top_vals[..., None], axis=1)
        routed = jnp.zeros_like(flat)
        for e in range(E_ROUTED):
            eo = _swiglu(flat, routed_gate[e], routed_up[e], routed_down[e])
            routed = routed + combine[:, e:e + 1] * eo
        return (out + routed).reshape(orig_shape)
    x = L0_attn_encodings
    xn = _layernorm(x, axis=-1)
    x = x + _L0_attn_ref(xn, L0_attn_attn_W, L0_attn_attn_b, L0_attn_out_W, L0_attn_out_b) + _L0_ffn_ref(xn, L0_ffn_Wg, L0_ffn_W1, L0_ffn_b1, L0_ffn_W2, L0_ffn_b2)
    xn = _layernorm(x, axis=-1)
    x = x + _L1_attn_ref(xn, L1_attn_W_qkv) + _L1_ffn_ref(xn, L1_ffn_shared_up, L1_ffn_shared_gate, L1_ffn_shared_down, L1_ffn_routed_up, L1_ffn_routed_gate, L1_ffn_routed_down, L1_ffn_router_w)
    return x

_drawn_inputs = setup_inputs


def setup_inputs(seed=0):
    import zlib

    import numpy as np

    out = dict(_drawn_inputs(seed))
    spreads = {}
    factors = {'L0_attn_attn_W': 6.237,
     'L0_attn_attn_b': 8.0,
     'L0_attn_out_W': 5.272,
     'L0_ffn_b1': 8.0,
     'L0_ffn_b2': 3.639,
     'L1_ffn_shared_up': 4.884,
     'L1_ffn_shared_gate': 4.876,
     'L1_ffn_shared_down': 4.838,
     'L1_ffn_routed_up': 6.899,
     'L1_ffn_routed_gate': 6.948,
     'L1_ffn_routed_down': 6.907,
     'L1_ffn_router_w': 8.0}
    for name, (base, spread) in spreads.items():
        noise = np.random.default_rng([zlib.crc32(name.encode()), seed]).standard_normal(out[name].shape)
        drawn = base * np.exp(spread * noise) if base else spread * noise
        out[name] = jnp.asarray(drawn.astype(out[name].dtype))
    for name, factor in factors.items():
        out[name] = (out[name] * factor).astype(out[name].dtype)
    return out
```

```python
from contextlib import ExitStack

import numpy as np
import concourse.bass as bass
from concourse import mybir
from concourse.alu_op_type import AluOpType as ALU

F32 = mybir.dt.float32
F32R = mybir.dt.float32r
BF16 = mybir.dt.bfloat16
I32 = mybir.dt.int32
ACT = mybir.ActivationFunctionType
AX = mybir.AxisListType

P = 128
D = 128
BATCH, SEQ = 32, 256
TOKENS = BATCH * SEQ
TILES = TOKENS // P
GROUP = 4
GROUPS = TILES // GROUP
H, HS = 16, D // 16
HG, HM = 4, 4
HID = 512
CH = HID // P
E0, E1 = 8, 7
TOP = 2
FT = 256
NT0 = TOP * TOKENS // FT + E0
NT1 = NT0
NEG = -1.0e30
EPS = 1e-5

C_ID, C_TRI, C_ONE, C_MB, C_RM, C_SEL, C_REV, C_TB = 0, 128, 256, 384, 512, 516, 1028, 1036
C_ALL = C_TB + NT0


def shape_constants():
    p = np.arange(P)
    c = np.zeros((P, C_ALL), np.float32)
    c[:, C_ID:C_ID + P] = np.eye(P)
    c[:, C_TRI:C_TRI + P] = p[:, None] < p[None, :]
    c[:, C_ONE:C_ONE + P] = 1.0
    c[:, C_MB:C_MB + P] = np.where(p[None, :] > p[:, None], NEG, 0.0)
    c[:, C_RM:C_RM + HM] = (p[:, None] % 32) // HS == np.arange(HM)[None]
    for m in range(HM):
        c[m, C_SEL + m * P:C_SEL + (m + 1) * P] = 1.0
        c[HM + m, C_SEL + m * P:C_SEL + (m + 1) * P] = 1.0
    c[:, C_REV:C_REV + 8] = 8 - np.arange(8)
    c[:, C_TB:C_TB + NT0] = FT * np.arange(NT0)
    return c


class Routing:

    def __init__(self, ctx, nc, name, experts, tiles):
        sb = lambda n, s, d: ctx.enter_context(nc.sbuf_tensor(f"{name}_{n}", s, d))
        self.experts, self.tiles = experts, tiles
        self.weight = [sb(f"weight{k}", [P, TILES], F32) for k in range(TOP)]
        self.slot = [sb(f"slot{k}", [P, TILES], I32) for k in range(TOP)]
        self.expert_of_tile = sb("expert_of_tile", [1, tiles], I32)


def norm_and_route(nc, layer, x, xn, xnT, const, const_bf, gateT, routing, gated_softmax):
    E = routing.experts
    ident = const[:, C_ID:C_ID + P]
    with ExitStack() as ctx:
        sb = lambda n, s, d=F32: ctx.enter_context(nc.sbuf_tensor(f"{layer}_{n}", s, d))
        pb = lambda n, s, d=F32: ctx.enter_context(nc.psum_tensor(f"{layer}_{n}", s, d))
        sem = lambda n: ctx.enter_context(nc.semaphore(f"{layer}_{n}"))
        stats = sb("stats", [P, TILES, 6])
        dmean, mean, var, rstd, shift = (sb(n, [P, TILES]) for n in ("dmean", "mean", "var", "rstd", "shift"))
        logits = sb("logits", [P, TILES, E])
        score, hot1, hot2, base = (sb(n, [P, TILES, E]) for n in ("score", "hot1", "hot2", "base"))
        hits = sb("hits", [P, TILES, E], BF16)
        top1, top2, first, t1, t2, t3 = (sb(n, [P, TILES]) for n in ("top1", "top2", "first", "t1", "t2", "t3"))
        upto = sb("upto", [P, TILES, E])
        padded_i = sb("padded_i", [P, E], I32)
        total, padded, ends, starts = (sb(n, [P, E]) for n in ("total", "padded", "ends", "starts"))
        passed = sb("passed", [1, routing.tiles, E])
        expert_f = sb("expert_f", [1, routing.tiles])
        xn_now = [sb(f"xn_now{i}", [P, GROUP, P]) for i in range(2)]
        xnT_now = [sb(f"xnT_now{i}", [P, GROUP * P]) for i in range(2)]
        xn_kept = [sem(f"xn_kept{i}") for i in range(2)]
        xnT_kept = [sem(f"xnT_kept{i}") for i in range(2)]
        turned = [pb(f"turned{i}", [P, GROUP * P]) for i in range(2)]
        logit_ps = [pb(f"logit_ps{i}", [P, GROUP, E]) for i in range(2)]
        within = pb("within", [P, TILES * E])
        in_tile = pb("in_tile", [P, TILES * E])
        stats_ready, xn_ready, turned_ready, xnT_ready = (sem(n) for n in ("stats_ready", "xn_ready", "turned_ready", "xnT_ready"))
        logit_ready, logit_read, hits_ready, counts_ready = (sem(n) for n in ("logit_ready", "logit_read", "hits_ready", "counts_ready"))
        exp_asked, exp_ready, step = (sem(n) for n in ("exp_asked", "exp_ready", "step"))
        var_ready, root_ready = sem("var_ready"), sem("root_ready")
        block = ctx.enter_context(nc.Block())

        @block.vector
        def _(dve):
            done = [0]

            def chained(ins):
                done[0] += 1
                ins.then_inc(step, 1)
                dve.wait_ge(step, done[0])

            with dve.Fori(0, TILES - 1) as t:
                nc.vector.bn_stats(stats[:, bass.ds(t, 1), :], x[:, bass.ds(t, 1), :])
            chained(nc.vector.bn_stats(stats[:, TILES - 1, :], x[:, TILES - 1, :]))
            m_even, q_even, m_odd, q_odd = (stats[:, :, i] for i in (1, 2, 4, 5))
            chained(nc.vector.tensor_tensor(mean[:], m_even, m_odd, ALU.add))
            chained(nc.vector.tensor_tensor(dmean[:], m_even, m_odd, ALU.subtract))
            chained(nc.vector.tensor_scalar(mean[:], mean[:], 0.5, None, ALU.mult))
            chained(nc.vector.tensor_tensor(dmean[:], dmean[:], dmean[:], ALU.mult))
            chained(nc.vector.tensor_tensor(var[:], q_even, q_odd, ALU.add))
            chained(nc.vector.tensor_scalar(var[:], var[:], 1.0 / D, None, ALU.mult))
            chained(nc.vector.scalar_tensor_tensor(var[:], dmean[:], 0.25, var[:], ALU.mult, ALU.add))
            nc.vector.tensor_scalar(var[:], var[:], EPS, None, ALU.add).then_inc(var_ready, 1)
            dve.wait_ge(root_ready, 1)
            chained(nc.vector.reciprocal(rstd[:], rstd[:]))
            chained(nc.vector.tensor_tensor(t1[:], rstd[:], rstd[:], ALU.mult))
            chained(nc.vector.tensor_tensor(t1[:], t1[:], var[:], ALU.mult))
            chained(nc.vector.tensor_scalar(t1[:], t1[:], -0.5, 1.5, ALU.mult, ALU.add))
            chained(nc.vector.tensor_tensor(rstd[:], rstd[:], t1[:], ALU.mult))
            nc.vector.scalar_tensor_tensor(shift[:], mean[:], -1.0, rstd[:], ALU.mult, ALU.mult).then_inc(stats_ready, 1)

            with dve.Fori(0, GROUPS // 2) as g2:
                for i in range(2):
                    dve.wait_ge(logit_ready, 2 * g2 + i + 1)
                    nc.vector.tensor_copy(logits[:, bass.ds(GROUP * (2 * g2 + i), GROUP), :], logit_ps[i][:]).then_inc(logit_read, 1)
            dve.wait_ge(logit_read, GROUPS)

            wide = lambda a: a[:].unsqueeze(2).to_broadcast([P, TILES, E])
            rev = const[:, C_REV:C_REV + E].unsqueeze(1).to_broadcast([P, TILES, E])
            for top, hot in ((top1, hot1), (top2, hot2)):
                src = logits if hot is hot1 else base
                chained(nc.vector.reduce_max(top[:], src[:], AX.X))
                chained(nc.vector.tensor_tensor(score[:], src[:], wide(top), ALU.is_ge))
                chained(nc.vector.tensor_tensor(score[:], score[:], rev, ALU.mult))
                chained(nc.vector.reduce_max(first[:], score[:], AX.X))
                chained(nc.vector.tensor_tensor(hot[:], score[:], wide(first), ALU.is_equal))
                if hot is hot1:
                    chained(nc.vector.scalar_tensor_tensor(base[:], hot1[:], -3.0e38, logits[:], ALU.mult, ALU.add))
            nc.vector.tensor_tensor(hits[:], hot1[:], hot2[:], ALU.add).then_inc(hits_ready, 1)

            if gated_softmax:
                chained(nc.vector.tensor_tensor(base[:], logits[:], wide(top1), ALU.subtract))
                nc.vector.tensor_tensor(t1[:], top2[:], top1[:], ALU.subtract).then_inc(exp_asked, 1)
                dve.wait_ge(exp_ready, 1)
                chained(nc.vector.reduce_sum(t2[:], score[:], AX.X))
                chained(nc.vector.reciprocal(t2[:], t2[:]))
                chained(nc.vector.tensor_tensor(t3[:], t1[:], t2[:], ALU.mult))
                chained(nc.vector.tensor_tensor(first[:], t2[:], t3[:], ALU.add))
                chained(nc.vector.tensor_scalar(first[:], first[:], 1e-9, None, ALU.add))
                chained(nc.vector.reciprocal(first[:], first[:]))
                nc.vector.tensor_tensor(routing.weight[0][:], t2[:], first[:], ALU.mult)
                chained(nc.vector.tensor_tensor(routing.weight[1][:], t3[:], first[:], ALU.mult))
            else:
                nc.vector.tensor_tensor(t1[:], top2[:], top1[:], ALU.subtract).then_inc(exp_asked, 1)
                dve.wait_ge(exp_ready, 1)
                chained(nc.vector.tensor_scalar(t2[:], t1[:], 1.0, None, ALU.add))
                chained(nc.vector.reciprocal(routing.weight[0][:], t2[:]))
                chained(nc.vector.tensor_tensor(routing.weight[1][:], t1[:], routing.weight[0][:], ALU.mult))

            dve.wait_ge(counts_ready, 1)
            here = in_tile[:].rearrange("p (t e) -> p t e", e=E)
            before = within[:].rearrange("p (t e) -> p t e", e=E)
            ones = const[:, C_ONE:C_ONE + TILES]
            for e in range(E):
                last = nc.vector.tensor_tensor_scan(upto[:, :, e], ones, here[:, :, e], 0.0, ALU.mult, ALU.add)
            chained(last)
            chained(nc.vector.tensor_scalar(padded_i[:], upto[:, TILES - 1, :], float(FT - 1), None, ALU.add))
            chained(nc.vector.tensor_scalar(padded_i[:], padded_i[:], FT.bit_length() - 1, FT.bit_length() - 1,
                                            ALU.arith_shift_right, ALU.arith_shift_left))
            chained(nc.vector.tensor_copy(padded[:], padded_i[:]))
            chained(nc.vector.tensor_tensor_scan(ends[:], const[:, C_ONE:C_ONE + E], padded[:], 0.0, ALU.mult, ALU.add))
            chained(nc.vector.tensor_tensor(starts[:], ends[:], padded[:], ALU.subtract))
            chained(nc.vector.tensor_tensor(upto[:], upto[:], here, ALU.subtract))
            chained(nc.vector.tensor_tensor(upto[:], upto[:], before, ALU.add))
            chained(nc.vector.tensor_tensor(base[:], upto[:], starts[:].unsqueeze(1).to_broadcast([P, TILES, E]), ALU.add))
            for k, hot in enumerate((hot1, hot2)):
                chained(nc.vector.tensor_tensor(score[:], base[:], hot[:], ALU.mult))
                chained(nc.vector.reduce_sum(first[:], score[:], AX.X))
                chained(nc.vector.tensor_copy(routing.slot[k][:], first[:]))
            n = routing.tiles
            chained(nc.vector.tensor_tensor(
                passed[:], const[0:1, C_TB:C_TB + n].unsqueeze(2).to_broadcast([1, n, E]),
                ends[0:1, :].unsqueeze(1).to_broadcast([1, n, E]), ALU.is_ge))
            chained(nc.vector.reduce_sum(expert_f[:], passed[:], AX.X))
            chained(nc.vector.tensor_scalar(expert_f[:], expert_f[:], float(E - 1), None, ALU.min))
            chained(nc.vector.tensor_copy(routing.expert_of_tile[:], expert_f[:]))

        @block.sync
        def _(sp):
            def keep(g2, i):
                g = 2 * g2 + i
                sp.wait_ge(xn_ready, g + 1)
                sp.dma_start(xn[:, bass.ds(GROUP * g, GROUP), :], xn_now[i][:]).then_inc(xn_kept[i], 16)
                sp.wait_ge(xnT_ready, g + 1)
                sp.dma_start(xnT[:, bass.ds(GROUP * P * g, GROUP * P)], xnT_now[i][:]).then_inc(xnT_kept[i], 16)

            with sp.Fori(0, GROUPS // 2) as g2:
                for i in range(2):
                    keep(g2, i)
            for i in range(2):
                sp.wait_ge(xn_kept[i], 16 * (GROUPS // 2))
                sp.wait_ge(xnT_kept[i], 16 * (GROUPS // 2))

        @block.scalar
        def _(act):
            def normalise(g2, i):
                g = 2 * g2 + i
                if not isinstance(g2, int) or g2 > 0:
                    act.wait_ge(turned_ready, g - 1)
                    act.wait_ge(xn_kept[i], 16 * g2)
                for t in range(GROUP):
                    at = bass.ds(GROUP * g + t, 1)
                    last = nc.scalar.activation(xn_now[i][:, t:t + 1, :], x[:, at, :], ACT.Identity,
                                                bias=shift[:, at], scale=rstd[:, at])
                last.then_inc(xn_ready, 1)

            def take_turned(g2, i):
                g = 2 * g2 + i
                act.wait_ge(turned_ready, g + 1)
                if not isinstance(g2, int) or g2 > 0:
                    act.wait_ge(logit_ready, g - 1)
                    act.wait_ge(xnT_kept[i], 16 * g2)
                nc.scalar.activation(xnT_now[i][:], turned[i][:], ACT.Copy).then_inc(xnT_ready, 1)

            act.wait_ge(var_ready, 1)
            nc.scalar.activation(rstd[:], var[:], ACT.Sqrt).then_inc(root_ready, 1)
            act.wait_ge(stats_ready, 1)
            for i in range(2):
                normalise(0, i)
            for i in range(2):
                take_turned(0, i)
            with act.Fori(1, GROUPS // 2) as g2:
                for i in range(2):
                    normalise(g2, i)
                for i in range(2):
                    take_turned(g2, i)
            act.wait_ge(exp_asked, 1)
            if gated_softmax:
                nc.scalar.activation(score[:], base[:], ACT.Exp)
            nc.scalar.activation(t1[:], t1[:], ACT.Exp).then_inc(exp_ready, 1)

        @block.tensor
        def _(pe):
            def turn(g2, i):
                g = 2 * g2 + i
                pe.wait_ge(xn_ready, g + 1)
                if not isinstance(g2, int) or g2 > 0:
                    pe.wait_ge(xnT_ready, g - 1)
                for t in range(GROUP):
                    last = nc.tensor.transpose(turned[i][:, t * P:(t + 1) * P], xn_now[i][:, t, :], ident)
                last.then_inc(turned_ready, 1)

            def score_experts(g2, i):
                g = 2 * g2 + i
                pe.wait_ge(xnT_ready, g + 1)
                if not isinstance(g2, int) or g2 > 0:
                    pe.wait_ge(logit_read, g - 1)
                for t in range(GROUP):
                    last = nc.tensor.matmul(logit_ps[i][:, t, :], xnT_now[i][:, t * P:(t + 1) * P], gateT[:, 0:E],
                                            start=(t == 0), stop=(t == GROUP - 1), skip_group_check=True)
                last.then_inc(logit_ready, 1)

            def both(g2):
                for i in range(2):
                    turn(g2, i)
                for i in range(2):
                    score_experts(g2, i)

            both(0)
            with pe.Fori(1, GROUPS // 2) as g2:
                both(g2)
            pe.wait_ge(hits_ready, 1)
            flat = hits[:].rearrange("p t e -> p (t e)")
            nc.tensor.matmul(within[:], const_bf[:, C_TRI:C_TRI + P], flat, start=True, stop=True)
            nc.tensor.matmul(in_tile[:], const_bf[:, C_ONE:C_ONE + P], flat, start=True, stop=True).then_inc(counts_ready, 1)


START = 16
NB = 3
UNROLL = 6


class Tile:

    def __init__(self, turn, place):
        self.turn, self.place = turn + place // UNROLL, place % UNROLL

    @property
    def i(self):
        return UNROLL * self.turn + self.place

    def back(self, n):
        return Tile(self.turn, self.place - n)

    def loaded(self):
        return START + 16 * (UNROLL // NB) * self.turn + 16 * (self.place // NB + 1)


def over_tiles(eng, first, end, body):
    turns = (end - first) // UNROLL
    if turns > 1:
        with eng.Fori(0, turns) as r:
            for u in range(UNROLL):
                body(Tile(r, first + u))
        first += turns * UNROLL
    for i in range(first, end):
        body(Tile(0, i))


def pack_cols(gated):
    return 3 * HID if gated else 2 * HID + CH + D


def expert_tiles(nc, layer, tiles, const, packs, gated, routed, x=None, xnT=None, rows_in=None, rows_out=None,
                 expert_of_tile=None):
    ident = const[:, C_ID:C_ID + P]
    W = pack_cols(gated)
    S = FT // P
    with ExitStack() as ctx:
        sb = lambda n, s, d=F32: ctx.enter_context(nc.sbuf_tensor(f"{layer}_{n}", s, d))
        pb = lambda n, s, d=F32: ctx.enter_context(nc.psum_tensor(f"{layer}_{n}", s, d))
        sem = lambda n: ctx.enter_context(nc.semaphore(f"{layer}_{n}"))
        pack = [sb(f"pack{i}", [P, W]) for i in range(NB if routed else 1)]
        tok = [sb(f"tok{i}", [P, S, D]) for i in range(NB)] if routed else None
        xT = [sb(f"xT{i}", [P, FT]) for i in range(2)]
        hT = [sb(f"hT{i}", [P, CH, FT]) for i in range(2)]
        y = [sb(f"y{i}", [P, S, D]) for i in range(2)]
        turned = pb("turned", [P, FT])
        silu = [sb(f"silu{i}", [P, 2, FT]) for i in range(2)] if gated else None
        hid_ps = [pb(f"hid_ps{i}", [P, 2, FT]) for i in range(4)]
        y_ps = [pb(f"y_ps{i}", [P, S, D]) for i in range(2)]
        tok_in, pack_in, y_out = ([sem(f"{n}{i}") for i in range(NB)] for n in ("tok_in", "pack_in", "y_out"))
        turned_ready, xT_ready, hid_ready, silu_ready, hT_ready, y_ready, y_kept = (
            sem(n) for n in ("turned_ready", "xT_ready", "hid_ready", "silu_ready", "hT_ready", "y_ready", "y_kept"))
        block = ctx.enter_context(nc.Block())
        wp = lambda j: pack[j % NB] if routed else pack[0]

        @block.sync
        def _(sp):
            def load(tile):
                i, j = tile.i, tile.place
                sp.wait_ge(turned_ready, START + i - (NB - 1))
                sp.dma_start(tok[j % NB][:], rows_in[bass.ds(i * FT, FT), :].rearrange("(s p) d -> p s d", p=P)).then_inc(tok_in[j % NB], 16)
                sp.wait_ge(y_kept, START + i - (NB - 1))
                e = sp.value_load(expert_of_tile[0:1, bass.ds(i, 1)], min_val=0, max_val=packs.shape[0] - 1)
                sp.dma_start(pack[j % NB][:], packs[bass.ds(e, 1), :, :].rearrange("e p w -> (e p) w")).then_inc(pack_in[j % NB], 16)

            def store(tile):
                i, j = tile.i, tile.place
                sp.wait_ge(y_kept, START + i + 1)
                sp.dma_start(rows_out[bass.ds(i * FT, FT), :].rearrange("(s p) d -> p s d", p=P), y[j % 2][:]).then_inc(y_out[j % NB], 16)

            if not routed:
                sp.dma_start(pack[0][:], packs[0, :, :]).then_inc(pack_in[0], 16)
                sp.wait_ge(pack_in[0], 16)
                return
            for q in range(NB):
                sp.sem_inc(tok_in[q], START)
                sp.sem_inc(pack_in[q], START)
                sp.sem_inc(y_out[q], START)
            over_tiles(sp, 0, 2, load)

            def step(tile):
                load(tile)
                store(tile.back(2))

            over_tiles(sp, 2, tiles, step)
            for i in range(tiles - 2, tiles):
                store(Tile(0, i))
            for i in range(tiles - NB, tiles):
                sp.wait_ge(y_out[i % NB], Tile(0, i).loaded())

        @block.tensor
        def _(pe):
            def turn(tile):
                i, j = tile.i, tile.place
                pe.wait_ge(tok_in[j % NB], tile.loaded())
                pe.wait_ge(xT_ready, START + i)
                for s in range(S):
                    last = nc.tensor.transpose(turned[:, s * P:(s + 1) * P], tok[j % NB][:, s, :], ident)
                last.then_inc(turned_ready, 1)

            def hidden(tile):
                i, j = tile.i, tile.place
                if routed:
                    pe.wait_ge(xT_ready, START + i + 1)
                    pe.wait_ge(pack_in[j % NB], tile.loaded())
                    src = xT[j % 2][:]
                else:
                    src = xnT[:, bass.ds(i * FT, FT)]
                for half in range(2):
                    if gated:
                        pe.wait_ge(hT_ready, START + 2 * i - 1 + half)
                        into = [hid_ps[2 * half], hid_ps[2 * half + 1]]
                    else:
                        pe.wait_ge(hT_ready, START + 2 * i - 3 + half)
                        into = [hid_ps[2 * (j % 2) + half]]
                    for k, bank in enumerate(into):
                        for c in range(2):
                            o = k * HID + (2 * half + c) * P
                            last = nc.tensor.matmul(bank[:, c, :], wp(j)[:, o:o + P], src, start=(c == 0), stop=(c == 1),
                                                    skip_group_check=True)
                        last.then_inc(hid_ready, 1)

            def down(tile):
                i, j = tile.i, tile.place
                pe.wait_ge(hT_ready, START + 2 * i + 2)
                pe.wait_ge(y_kept, START + i - 1)
                o = (2 if gated else 1) * HID
                for s in range(S):
                    for c in range(CH):
                        last = nc.tensor.matmul(y_ps[j % 2][:, s, :], hT[j % 2][:, c, s * P:(s + 1) * P],
                                                wp(j)[:, o + c * D:o + (c + 1) * D], start=(c == 0), stop=(c == CH - 1))
                last.then_inc(y_ready, 1)

            pe.sem_inc(turned_ready, START)
            pe.sem_inc(y_ready, START)
            pe.sem_inc(hid_ready, START)
            if not routed:
                pe.wait_ge(pack_in[0], 16)
            if routed:
                turn(Tile(0, 0))
            hidden(Tile(0, 0))

            def step(tile):
                if routed:
                    turn(tile)
                hidden(tile)
                down(tile.back(1))

            over_tiles(pe, 1, tiles, step)
            down(Tile(0, tiles - 1))

        @block.scalar
        def _(act):
            def step(tile):
                i, j = tile.i, tile.place
                if gated:
                    for half in range(2):
                        act.wait_ge(hid_ready, START + 4 * i + 2 * half + 1)
                        act.wait_ge(hT_ready, START + 2 * i - 1 + half)
                        nc.scalar.activation(silu[half][:], hid_ps[2 * half][:], ACT.Silu).then_inc(silu_ready, 1)
                else:
                    act.wait_ge(y_ready, START + i - 1)
                    for half in range(2):
                        act.wait_ge(hid_ready, START + 2 * i + half + 1)
                        for c in range(2):
                            b = 2 * HID + 2 * half + c
                            last = nc.scalar.activation(hT[j % 2][:, 2 * half + c, :], hid_ps[2 * (j % 2) + half][:, c, :],
                                                        ACT.Gelu, bias=wp(j)[:, b:b + 1])
                        last.then_inc(hT_ready, 1)

            if not gated:
                act.sem_inc(hT_ready, START)
            over_tiles(act, 0, tiles, step)

        @block.vector
        def _(dve):
            def take_turned(tile):
                i, j = tile.i, tile.place
                dve.wait_ge(turned_ready, START + i + 1)
                per = 4 if gated else 2
                dve.wait_ge(hid_ready, START + per * (i - 1))
                nc.vector.tensor_copy(xT[j % 2][:], turned[:]).then_inc(xT_ready, 1)

            def multiply(tile):
                i, j = tile.i, tile.place
                dve.wait_ge(y_ready, START + i - 1)
                for half in range(2):
                    dve.wait_ge(hid_ready, START + 4 * i + 2 * half + 2)
                    dve.wait_ge(silu_ready, 2 * i + half + 1)
                    nc.vector.tensor_tensor(hT[j % 2][:, 2 * half:2 * half + 2, :], hid_ps[2 * half + 1][:], silu[half][:],
                                            ALU.mult).then_inc(hT_ready, 1)

            def take_y(tile):
                i, j = tile.i, tile.place
                dve.wait_ge(y_ready, START + i + 1)
                if not routed:
                    at = x[:, bass.ds(S * i, S), :]
                    nc.vector.tensor_tensor(at, at, y_ps[j % 2][:], ALU.add).then_inc(y_kept, 1)
                    return
                dve.wait_ge(y_out[(j - 2) % NB], tile.back(2).loaded())
                if gated:
                    nc.vector.tensor_copy(y[j % 2][:], y_ps[j % 2][:]).then_inc(y_kept, 1)
                else:
                    b = 2 * HID + CH
                    bias = wp(j)[:, b:b + D].unsqueeze(1).to_broadcast([P, S, D])
                    nc.vector.tensor_tensor(y[j % 2][:], y_ps[j % 2][:], bias, ALU.add).then_inc(y_kept, 1)

            dve.sem_inc(xT_ready, START)
            dve.sem_inc(y_kept, START)
            if gated:
                dve.sem_inc(hT_ready, START)
            if routed:
                take_turned(Tile(0, 0))
            if gated:
                multiply(Tile(0, 0))

            def step(tile):
                if routed:
                    take_turned(tile)
                if gated:
                    multiply(tile)
                take_y(tile.back(1))

            over_tiles(dve, 1, tiles, step)
            take_y(Tile(0, tiles - 1))


def scatter_of(nc, xn, rows, routing, scattered):
    def scatter(pool, first, end):
        for t in range(first, end):
            for k in range(TOP):
                at = bass.IndirectOffsetOnAxis(ap=routing.slot[k][:, t:t + 1], axis=0)
                nc.gpsimd.indirect_dma_start(rows, at, xn[:, t, :], None).then_inc(scattered, 16)

    def wait_for_all(pool):
        pool.wait_ge(scattered, 16 * TOP * TILES)

    return scatter, wait_for_all


RING = 8


def combine(nc, layer, x, rows, routing, out=None):
    with ExitStack() as ctx:
        sb = lambda n, s, d=F32: ctx.enter_context(nc.sbuf_tensor(f"{layer}_{n}", s, d))
        sem = lambda n: ctx.enter_context(nc.semaphore(f"{layer}_{n}"))
        got = [[sb(f"got{r}_{k}", [P, D]) for k in range(TOP)] for r in range(RING)]
        gathered = [sem(f"gathered{r}") for r in range(RING)]
        half_added, added, written = sem("half_added"), sem("added"), sem("written")
        block = ctx.enter_context(nc.Block())

        @block.gpsimd
        def _(pool):
            for t in range(TILES):
                if t >= RING:
                    pool.wait_ge(added, t - RING + 1)
                for k in range(TOP):
                    at = bass.IndirectOffsetOnAxis(ap=routing.slot[k][:, t:t + 1], axis=0)
                    nc.gpsimd.indirect_dma_start(got[t % RING][k][:], None, rows, at).then_inc(gathered[t % RING], 16)

        @block.vector
        def _(dve):
            with dve.Fori(0, TILES // RING) as g:
                for r in range(RING):
                    t = RING * g + r
                    dve.wait_ge(gathered[r], 16 * TOP * g + 16 * TOP)
                    for k in range(TOP):
                        if k:
                            dve.wait_ge(half_added, t + 1)
                        nc.vector.scalar_tensor_tensor(x[:, bass.ds(t, 1), :].squeeze(1), got[r][k][:],
                                                       routing.weight[k][:, bass.ds(t, 1)], x[:, bass.ds(t, 1), :].squeeze(1),
                                                       ALU.mult, ALU.add).then_inc((half_added, added)[k], 1)

        if out is not None:
            @block.sync
            def _(sp):
                rows_of = out.rearrange("(t p) d -> p t d", p=P)
                with sp.Fori(0, TILES // RING) as g:
                    sp.wait_ge(added, RING * g + RING)
                    sp.dma_start(rows_of[:, bass.ds(RING * g, RING), :], x[:, bass.ds(RING * g, RING), :]).then_inc(written, 16)
                sp.wait_ge(written, 16 * (TILES // RING))


def causal_attention(nc, x, xnT, const, const_bf, w_q, w_k, w_v, b_qk, b_v, w_out, b_out, scatter,
                     scattered_all):
    ident = const[:, C_ID:C_ID + P]
    ident_bf = const_bf[:, C_ID:C_ID + P]
    causal = const_bf[:, C_MB:C_MB + P].unsqueeze(1).to_broadcast([P, 2, P])
    with ExitStack() as ctx:
        sb = lambda n, s, d=F32: ctx.enter_context(nc.sbuf_tensor(f"att_{n}", s, d))
        pb = lambda n, s, d=F32: ctx.enter_context(nc.psum_tensor(f"att_{n}", s, d))
        sem = lambda n: ctx.enter_context(nc.semaphore(f"att_{n}"))
        xT = [sb(f"xT{i}", [P, SEQ]) for i in range(2)]
        full = [sb(f"{n}_full", [P, HG, SEQ]) for n in "qk"]
        q_rows = sb("q_rows", [P, HG, SEQ], F32R)
        q_member = [sb(f"q_member{i}", [P, HG, HM, SEQ], F32R) for i in range(2)]
        k_rows = [sb(f"k_rows{i}", [P, HG, SEQ], F32R) for i in range(2)]
        v_ones = [sb(f"v_ones{i}", [P, 2, H, 32]) for i in range(2)]
        maxima = sb("maxima", [P, 2, H])
        minus_max = sb("minus_max", [P, 2, HG, 2, HM], BF16)
        max_rows = sb("max_rows", [P, HG, SEQ], BF16)
        probs_a = [sb(f"probs_a{i}", [P, HM, SEQ]) for i in range(2)]
        probs_b = [sb(f"probs_b{i}", [P, HM, P]) for i in range(2)]
        oT = sb("oT", [P, HG, SEQ])
        inv = sb("inv", [P, H])
        o_tok = [sb(f"o_tok{i}", [P, H, HS]) for i in range(2)]
        o_cols = sb("o_cols", [P, SEQ])
        with_bias = sb("with_bias", [P, 2, D])

        bank_s = [pb(f"bank_s{i}", [P, 2, SEQ]) for i in range(2)]
        bank_a = pb("bank_a", [P, HM, SEQ])
        bank_b = pb("bank_b", [P, HM, P])
        bank_m = [pb(f"bank_m{i}", [P, 512]) for i in range(3)]

        PER = (4, 3, 4)
        filled = [sem(f"filled{i}") for i in range(3)]
        xT_in = [sem(f"xT_in{i}") for i in range(2)]
        (constants_set, biased, q_high, k_high, q_halves, k_halves, q_ready, v_ready, s_ready, max_ready, minus_high, minus_ready,
         rows_ready, a_ready, b_ready, exp_a, exp_b, probs_ready, weighed, oT_ready, inv_ready, otok_ready, cols_ready,
         out_taken, x_added, step) = (
            sem(n) for n in ("constants_set", "biased", "q_high", "k_high", "q_halves", "k_halves", "q_ready", "v_ready",
                             "s_ready", "max_ready", "minus_high", "minus_ready", "rows_ready", "a_ready", "b_ready",
                             "exp_a", "exp_b", "probs_ready", "weighed", "oT_ready", "inv_ready", "otok_ready", "cols_ready",
                             "out_taken", "x_added", "step"))
        block = ctx.enter_context(nc.Block())

        def wait(eng, semaphore, value):
            if not isinstance(value, int) or value > 0:
                eng.wait_ge(semaphore, value)

        def steps(eng, new, old, both):
            new(0, 0)
            both(1, 1)
            with eng.Fori(0, BATCH // 2 - 1) as r:
                both(2 * r + 2, 0)
                both(2 * r + 3, 1)
            old(BATCH - 1, 1)

        @block.tensor
        def _(pe):
            def project(s, p, which, half):
                bank = half
                if which == 0:
                    pe.wait_ge(xT_in[p], 8 * (s - p) + 16)
                    wait(pe, rows_ready, 2 * s - 1 + half)
                else:
                    pe.wait_ge(biased, 4 * s + 1 + half)
                w = (w_q, w_k)[which]
                for g in range(2):
                    last = nc.tensor.matmul(bank_m[bank][:, g * SEQ:(g + 1) * SEQ], w[:, (2 * half + g) * P:(2 * half + g + 1) * P],
                                            xT[p][:], start=(g == 0), stop=(g == 1), skip_group_check=True)
                last.then_inc(filled[bank], 1)

            def project_v(s, p):
                pe.wait_ge(biased, 4 * s + 3)
                for t in range(2):
                    last = nc.tensor.matmul(bank_m[0][:, t * D:(t + 1) * D], xT[p][:, t * P:(t + 1) * P], w_v[:],
                                            start=(t == 0), stop=(t == 1), skip_group_check=True)
                last.then_inc(filled[0], 1)

            def scores(s, p, g):
                if g == 0:
                    pe.wait_ge(q_ready, HM * (s + 1))
                    pe.wait_ge(k_halves, s + 1)
                for t in range(2):
                    for pair in range(2):
                        u = 4 * g + 2 * t + pair
                        bank = bank_s[u % 2]
                        wait(pe, max_ready, 16 * s + (u - 1))
                        for k in range(2):
                            nc.tensor.matmul(bank[:, k, :], q_member[p][:, g, 2 * pair + k, t * P:(t + 1) * P], k_rows[p][:, g, :],
                                             start=(k == 0), stop=False, skip_group_check=True)
                        nc.tensor.matmul(bank[:, :, t * P:(t + 1) * P], ident_bf, causal,
                                         start=False, stop=True, skip_group_check=True).then_inc(s_ready, 1)

            def turn_maxima(s, half):
                pe.wait_ge(minus_ready, s + 1)
                if half == 0:
                    pe.wait_ge(v_ready, s + 1)
                else:
                    pe.wait_ge(biased, 4 * s + 4)
                for g in range(2):
                    for t in range(2):
                        last = nc.tensor.matmul(bank_m[half][0:2 * HM, g * SEQ + t * P:g * SEQ + (t + 1) * P],
                                                minus_max[:, t, 2 * half + g, :, :].rearrange("p a m -> p (a m)"), ident_bf,
                                                start=(g + t == 0), stop=(g + t == 2), skip_group_check=True)
                last.then_inc(filled[half], 1)

            def shifted(s, p, g):
                if g == 0:
                    pe.wait_ge(rows_ready, 2 * s + 2)
                wait(pe, exp_a, 4 * s + g)
                for m in range(HM):
                    nc.tensor.matmul(bank_a[:, m, :], k_rows[p][:, g, 0:P], q_member[p][:, g, m, :],
                                     start=(m % 2 == 0), stop=False, skip_group_check=True)
                for m in range(HM):
                    last = nc.tensor.matmul(bank_a[:, m, :], const_bf[:, C_SEL + m * P:C_SEL + (m + 1) * P], max_rows[:, g, :],
                                            start=False, stop=True, skip_group_check=True)
                last.then_inc(a_ready, 1)
                wait(pe, exp_b, 4 * s + g)
                for m in range(0, HM, 2):
                    nc.tensor.matmul(bank_b[:, m:m + 2, :], k_rows[p][:, g, P:2 * P], q_member[p][:, g, m:m + 2, P:2 * P],
                                     start=(m == 0), stop=False, skip_group_check=True)
                for m in range(HM):
                    last = nc.tensor.matmul(bank_b[:, m, :], const_bf[:, C_SEL + m * P:C_SEL + (m + 1) * P], max_rows[:, g, P:2 * P],
                                            start=False, stop=True, skip_group_check=True)
                last.then_inc(b_ready, 1)

            def weigh(s, p, g):
                pe.wait_ge(probs_ready, 8 * s + 2 * g + 2)
                if g == 0:
                    wait(pe, out_taken, s)
                if g == 2:
                    pe.wait_ge(oT_ready, 2 * s + 1)
                at = (g % 2) * SEQ
                for m in range(HM):
                    nc.tensor.matmul(bank_m[2][32 * m:32 * m + 32, at:at + SEQ], v_ones[p][:, 0, HM * g + m, :], probs_a[g % 2][:, m, :],
                                     start=True, stop=False, skip_group_check=True)
                for m in range(HM):
                    last = nc.tensor.matmul(bank_m[2][32 * m:32 * m + 32, at + P:at + SEQ], v_ones[p][:, 1, HM * g + m, :],
                                            probs_b[g % 2][:, m, :], start=False, stop=True, skip_group_check=True)
                last.then_inc(weighed, 1)

            def turn_back(s, t):
                pe.wait_ge(oT_ready, 2 * s + 2)
                if t == 1:
                    pe.wait_ge(otok_ready, 2 * s + 1)
                for g in range(HG):
                    last = nc.tensor.transpose(bank_m[2][:, g * P:(g + 1) * P], oT[:, g, t * P:(t + 1) * P], ident)
                last.then_inc(filled[2], 1)

            def to_columns(s):
                pe.wait_ge(otok_ready, 2 * s + 2)
                for t in range(2):
                    last = nc.tensor.transpose(bank_m[2][:, t * P:(t + 1) * P], o_tok[t][:].rearrange("p h d -> p (h d)"), ident)
                last.then_inc(filled[2], 1)

            def project_out(s):
                pe.wait_ge(cols_ready, s + 1)
                for t in range(2):
                    last = nc.tensor.matmul(bank_m[2][:, t * D:(t + 1) * D], o_cols[:, t * P:(t + 1) * P], w_out[:],
                                            start=(t == 0), stop=(t == 1), skip_group_check=True)
                last.then_inc(filled[2], 1)

            def new(s, p):
                for half, which in ((0, 0), (1, 0), (0, 1), (1, 1)):
                    project(s, p, which, half)
                project_v(s, p)
                for g in range(HG):
                    scores(s, p, g)
                turn_maxima(s, 0)
                turn_maxima(s, 1)

            def old(s, p):
                for g in range(HG):
                    shifted(s, p, g)
                    if g:
                        weigh(s, p, g - 1)
                weigh(s, p, HG - 1)
                turn_back(s, 0)
                turn_back(s, 1)
                to_columns(s)
                project_out(s)

            def both(s, p):
                o, q = s - 1, 1 - p
                project(s, p, 0, 0)
                shifted(o, q, 0)
                project(s, p, 0, 1)
                project(s, p, 1, 0)
                shifted(o, q, 1)
                weigh(o, q, 0)
                project(s, p, 1, 1)
                project_v(s, p)
                shifted(o, q, 2)
                weigh(o, q, 1)
                scores(s, p, 0)
                shifted(o, q, 3)
                weigh(o, q, 2)
                scores(s, p, 1)
                weigh(o, q, 3)
                scores(s, p, 2)
                turn_back(o, 0)
                scores(s, p, 3)
                turn_back(o, 1)
                turn_maxima(s, 0)
                turn_maxima(s, 1)
                to_columns(o)
                project_out(o)

            pe.wait_ge(constants_set, 1)
            steps(pe, new, old, both)

        @block.sync
        def _(sp):
            def load(s, p):
                wait(sp, v_ready, s - 1)
                sp.dma_start(xT[p][:], xnT[:, bass.ds(s * SEQ, SEQ)]).then_inc(xT_in[p], 16)

            for s in range(2):
                load(s, s)
            with sp.Fori(0, BATCH // 2 - 1) as r:
                for p in range(2):
                    load(2 * r + (2 + p), p)
            for p in range(2):
                sp.wait_ge(xT_in[p], 8 * BATCH)

        @block.scalar
        def _(act):
            def add_bias(s, which, half):
                act.wait_ge(filled[half], PER[half] * s + which + 1)
                wait(act, (q_halves, k_halves)[which], s)
                for g in range(2):
                    grp = 2 * half + g
                    last = nc.scalar.activation(full[which][:, grp, :], bank_m[half][:, g * SEQ:(g + 1) * SEQ], ACT.Identity,
                                                bias=b_qk[:, HG * which + grp:HG * which + grp + 1])
                last.then_inc(biased, 1)

            def exponentials(s, g):
                act.wait_ge(a_ready, 4 * s + g + 1)
                wait(act, weighed, 4 * s + (g - 1))
                nc.scalar.activation(probs_a[g % 2][:], bank_a[:], ACT.Exp, scale=HS ** -0.5).then_inc(exp_a, 1)
                act.wait_ge(b_ready, 4 * s + g + 1)
                nc.scalar.activation(probs_b[g % 2][:], bank_b[:], ACT.Exp, scale=HS ** -0.5).then_inc(exp_b, 1)

            def keep_maxima(s, half):
                act.wait_ge(filled[half], PER[half] * (s + 1))
                nc.scalar.activation(max_rows[0:2 * HM, 2 * half:2 * half + 2, :],
                                     bank_m[half][0:2 * HM, :].rearrange("p (g q) -> p g q", g=2), ACT.Copy).then_inc(rows_ready, 1)

            def keep_oT(s, half):
                act.wait_ge(weighed, 4 * s + 2 * half + 2)
                nc.scalar.activation(oT[:, 2 * half:2 * half + 2, :], bank_m[2][:].rearrange("p (g q) -> p g q", g=2),
                                     ACT.Copy).then_inc(oT_ready, 1)

            def keep_cols(s):
                act.wait_ge(filled[2], 4 * s + 3)
                nc.scalar.activation(o_cols[:], bank_m[2][:, 0:SEQ], ACT.Copy).then_inc(cols_ready, 1)

            def new(s, p):
                for which, half in ((0, 0), (0, 1), (1, 0), (1, 1)):
                    add_bias(s, which, half)
                keep_maxima(s, 0)
                keep_maxima(s, 1)

            def old(s, p):
                for g in range(HG):
                    exponentials(s, g)
                    if g == 2:
                        keep_oT(s, 0)
                keep_oT(s, 1)
                keep_cols(s)

            def both(s, p):
                o = s - 1
                add_bias(s, 0, 0)
                exponentials(o, 0)
                add_bias(s, 0, 1)
                add_bias(s, 1, 0)
                exponentials(o, 1)
                add_bias(s, 1, 1)
                exponentials(o, 2)
                keep_oT(o, 0)
                exponentials(o, 3)
                keep_oT(o, 1)
                keep_maxima(s, 0)
                keep_maxima(s, 1)
                keep_cols(o)

            steps(act, new, old, both)

        @block.vector
        def _(dve):
            def split_q(s, p):
                dve.wait_ge(biased, 4 * s + 2)
                wait(dve, q_ready, HM * s)
                nc.vector.tensor_copy(q_rows[:], full[0][:]).then_inc(q_high, 1)
                dve.wait_ge(q_high, s + 1)
                low = slice(64, 128)
                nc.vector.tensor_tensor(q_rows[low, :, :], full[0][low, :, :], q_rows[low, :, :].bitcast(F32),
                                        ALU.subtract).then_inc(q_halves, 1)

            def split_k(s, p):
                dve.wait_ge(biased, 4 * s + 4)
                wait(dve, b_ready, 4 * s - 4)
                nc.vector.tensor_copy(k_rows[p][:], full[1][:]).then_inc(k_high, 1)
                dve.wait_ge(k_high, s + 1)
                for low in (slice(32, 64), slice(96, 128)):
                    last = nc.vector.tensor_tensor(k_rows[p][low, :, :], full[1][low, :, :], k_rows[p][low, :, :].bitcast(F32),
                                                   ALU.subtract)
                last.then_inc(k_halves, 1)

            def keep_v(s, p):
                dve.wait_ge(filled[0], 4 * s + 3)
                wait(dve, weighed, 4 * s - 4)
                nc.vector.tensor_tensor(v_ones[p][:, :, :, 0:HS], bank_m[0][:, 0:2 * D].rearrange("p (t h d) -> p t h d", t=2, h=H),
                                        b_v[:].rearrange("p (h d) -> p h d", h=H).unsqueeze(1).to_broadcast([P, 2, H, HS]),
                                        ALU.add).then_inc(v_ready, 1)

            def reduce(s, g):
                for t in range(2):
                    for pair in range(2):
                        u = 4 * g + 2 * t + pair
                        dve.wait_ge(s_ready, 16 * s + u + 1)
                        h = HM * g + 2 * pair
                        nc.vector.reduce_max(maxima[:, t, h:h + 2], bank_s[u % 2][:, :, 0:(t + 1) * P], AX.X).then_inc(max_ready, 1)

            def split_maxima(s):
                dve.wait_ge(max_ready, 16 * (s + 1))
                wait(dve, filled[1], 3 * s)
                high, low = (minus_max[:, :, :, a, :].rearrange("p t g m -> p (t g) m") for a in range(2))
                src = maxima[:].rearrange("p t (g m) -> p (t g) m", m=HM)
                nc.vector.tensor_scalar(high, src, -1.0, None, ALU.mult).then_inc(minus_high, 1)
                dve.wait_ge(minus_high, s + 1)
                nc.vector.scalar_tensor_tensor(low, src, -1.0, high, ALU.mult, ALU.subtract).then_inc(minus_ready, 1)

            def normalise(s, t):
                dve.wait_ge(filled[2], 4 * s + t + 1)
                heads = bank_m[2][:].rearrange("p (h c) -> p h c", c=32)
                nc.vector.reciprocal(inv[:], heads[:, :, HS]).then_inc(inv_ready, 1)
                dve.wait_ge(inv_ready, 2 * s + t + 1)
                nc.vector.tensor_tensor(o_tok[t][:], heads[:, :, 0:HS], inv[:].unsqueeze(2).to_broadcast([P, H, HS]),
                                        ALU.mult).then_inc(otok_ready, 1)

            def add_out(s):
                dve.wait_ge(filled[2], 4 * s + 4)
                nc.vector.tensor_tensor(with_bias[:], bank_m[2][:, 0:2 * D].rearrange("p (t d) -> p t d", t=2),
                                        b_out[:].unsqueeze(1).to_broadcast([P, 2, D]), ALU.add).then_inc(out_taken, 1)
                dve.wait_ge(out_taken, s + 1)
                at = x[:, bass.ds(2 * s, 2), :]
                nc.vector.tensor_tensor(at, at, with_bias[:], ALU.add).then_inc(x_added, 1)

            def new(s, p):
                split_q(s, p)
                split_k(s, p)
                keep_v(s, p)
                for g in range(HG):
                    reduce(s, g)
                split_maxima(s)

            def old(s, p):
                normalise(s, 0)
                normalise(s, 1)
                add_out(s)

            def both(s, p):
                o = s - 1
                split_q(s, p)
                split_k(s, p)
                keep_v(s, p)
                reduce(s, 0)
                reduce(s, 1)
                reduce(s, 2)
                normalise(o, 0)
                reduce(s, 3)
                split_maxima(s)
                normalise(o, 1)
                add_out(o)

            for p in range(2):
                nc.vector.memset(v_ones[p][:], 0.0)
            nc.vector.memset(max_rows[:], 0.0).then_inc(step, 1)
            dve.wait_ge(step, 1)
            for p in range(2):
                last = nc.vector.memset(v_ones[p][:, :, :, HS:HS + 1], 1.0)
            last.then_inc(constants_set, 1)
            dve.wait_ge(constants_set, 1)
            steps(dve, new, old, both)

        @block.gpsimd
        def _(pool):
            def member_queries(s):
                pool.wait_ge(q_halves, s + 1)
                wait(pool, b_ready, 4 * s - 4)
                for m in range(HM):
                    nc.gpsimd.tensor_scalar(q_member[s % 2][:, :, m, :], q_rows[:].bitcast(F32), const[:, C_RM + m:C_RM + m + 1], 1.0,
                                            ALU.mult, ALU.mult).then_inc(q_ready, 1)

            def keep_causal(s, g):
                for ready, block_of in ((exp_a, probs_a[g % 2][:, :, 0:P]), (exp_b, probs_b[g % 2][:])):
                    pool.wait_ge(ready, 4 * s + g + 1)
                    nc.gpsimd.affine_select(out=block_of, in_=block_of, pattern=[[0, HM], [1, P]], compare_op=ALU.is_ge,
                                            fill=0.0, base=0, channel_multiplier=-1).then_inc(probs_ready, 1)

            for s in range(BATCH + 1):
                for g in range(HG):
                    if s > 0:
                        keep_causal(s - 1, g)
                    if g == 1 and s < BATCH:
                        member_queries(s)
                if s < BATCH:
                    scatter(pool, 2 * s, 2 * s + 2)
            scattered_all(pool)


def attention(nc, x, xnT, const, w_q, w_k, w_v, scatter, scattered_all):
    ident = const[:, C_ID:C_ID + P]
    with ExitStack() as ctx:
        sb = lambda n, s, d=F32: ctx.enter_context(nc.sbuf_tensor(f"att1_{n}", s, d))
        pb = lambda n, s, d=F32: ctx.enter_context(nc.psum_tensor(f"att1_{n}", s, d))
        sem = lambda n: ctx.enter_context(nc.semaphore(f"att1_{n}"))
        xT = [sb(f"xT{i}", [P, SEQ]) for i in range(2)]
        qT, kT = sb("qT", [P, SEQ]), sb("kT", [P, SEQ])
        v = [sb(f"v{i}", [P, 2, D]) for i in range(2)]
        top = sb("top", [P, 2])
        minus_top = [sb(f"minus_top{i}", [P, 2]) for i in range(2)]
        total = [sb(f"total{i}", [P, 2]) for i in range(2)]
        inv = sb("inv", [P, 2])
        probs = [sb(f"probs{i}", [P, 2, SEQ]) for i in range(2)]
        probsT = sb("probsT", [P, 2, 2, P])
        qk_ps, v_ps, turned, o_ps = pb("qk_ps", [P, 2, SEQ]), pb("v_ps", [P, 2, D]), pb("turned", [P, 2, 2, P]), pb("o_ps", [P, 2, D])
        s_ps = [pb(f"s_ps{i}", [P, 2, SEQ]) for i in range(2)]
        xT_in = [sem(f"xT_in{i}") for i in range(2)]
        names = ("qk_ready", "qk_taken", "v_ready", "v_taken", "s_ready", "top_ready", "minus_ready", "probs_ready",
                 "turned_ready", "probsT_ready", "o_ready", "inv_ready", "x_added")
        (qk_ready, qk_taken, v_ready, v_taken, s_ready, top_ready, minus_ready, probs_ready,
         turned_ready, probsT_ready, o_ready, inv_ready, x_added) = (sem(n) for n in names)
        block = ctx.enter_context(nc.Block())

        def wait(eng, semaphore, value):
            if not isinstance(value, int) or value > 0:
                eng.wait_ge(semaphore, value)

        def steps(eng, new, old, both):
            new(0, 0)
            both(1, 1)
            with eng.Fori(0, BATCH // 2 - 1) as r:
                both(2 * r + 2, 0)
                both(2 * r + 3, 1)
            old(BATCH - 1, 1)

        @block.tensor
        def _(pe):
            def project(s, p):
                pe.wait_ge(xT_in[p], 8 * (s - p) + 16)
                wait(pe, qk_taken, 2 * s)
                for which, w in enumerate((w_q, w_k)):
                    last = nc.tensor.matmul(qk_ps[:, which, :], w[:], xT[p][:], start=(which == 0), stop=(which == 1),
                                            skip_group_check=True)
                last.then_inc(qk_ready, 1)

            def project_v(s, p):
                wait(pe, v_taken, s)
                for t in range(2):
                    last = nc.tensor.matmul(v_ps[:, t, :], xT[p][:, t * P:(t + 1) * P], w_v[:], start=(t == 0), stop=(t == 1),
                                            skip_group_check=True)
                last.then_inc(v_ready, 1)

            def scores(s, p):
                pe.wait_ge(qk_taken, 2 * s + 2)
                wait(pe, probs_ready, 2 * s - 2)
                for t in range(2):
                    last = nc.tensor.matmul(s_ps[p][:, t, :], qT[:, t * P:(t + 1) * P], kT[:], start=(t == 0), stop=(t == 1),
                                            skip_group_check=True)
                last.then_inc(s_ready, 1)

            def turn(s, p):
                pe.wait_ge(probs_ready, 2 * s + 2)
                wait(pe, probsT_ready, s)
                for k in range(2):
                    for t in range(2):
                        last = nc.tensor.transpose(turned[:, k, t, :], probs[p][:, t, k * P:(k + 1) * P], ident)
                last.then_inc(turned_ready, 1)

            def weigh(s, p):
                pe.wait_ge(probsT_ready, s + 1)
                pe.wait_ge(v_taken, s + 1)
                wait(pe, x_added, s)
                for t in range(2):
                    for k in range(2):
                        last = nc.tensor.matmul(o_ps[:, t, :], probsT[:, k, t, :], v[p][:, k, :], start=(k == 0), stop=(k == 1))
                last.then_inc(o_ready, 1)

            def new(s, p):
                project(s, p)
                project_v(s, p)
                scores(s, p)

            def old(s, p):
                turn(s, p)
                weigh(s, p)

            def both(s, p):
                project(s, p)
                turn(s - 1, 1 - p)
                project_v(s, p)
                scores(s, p)
                weigh(s - 1, 1 - p)

            steps(pe, new, old, both)

        @block.sync
        def _(sp):
            def load(s, p):
                wait(sp, v_ready, s - 1)
                sp.dma_start(xT[p][:], xnT[:, bass.ds(s * SEQ, SEQ)]).then_inc(xT_in[p], 16)

            for s in range(2):
                load(s, s)
            with sp.Fori(0, BATCH // 2 - 1) as r:
                for p in range(2):
                    load(2 * r + (2 + p), p)
            for p in range(2):
                sp.wait_ge(xT_in[p], 8 * BATCH)

        @block.scalar
        def _(act):
            def take_qk(s):
                act.wait_ge(qk_ready, s + 1)
                wait(act, s_ready, s)
                nc.scalar.activation(qT[:], qk_ps[:, 0, :], ACT.Copy, scale=D ** -0.5).then_inc(qk_taken, 1)
                nc.scalar.activation(kT[:], qk_ps[:, 1, :], ACT.Copy).then_inc(qk_taken, 1)

            def exponentials(s, p):
                act.wait_ge(minus_ready, s + 1)
                wait(act, turned_ready, s - 1)
                wait(act, x_added, s - 1)
                for t in range(2):
                    nc.scalar.activation(probs[p][:, t, :], s_ps[p][:, t, :], ACT.Exp, bias=minus_top[p][:, t:t + 1],
                                         accum_out=total[p][:, t:t + 1]).then_inc(probs_ready, 1)

            def take_turned(s):
                act.wait_ge(turned_ready, s + 1)
                wait(act, o_ready, s)
                nc.scalar.activation(probsT[:], turned[:], ACT.Copy).then_inc(probsT_ready, 1)

            def new(s, p):
                take_qk(s)
                exponentials(s, p)

            def old(s, p):
                take_turned(s)

            def both(s, p):
                take_qk(s)
                take_turned(s - 1)
                exponentials(s, p)

            steps(act, new, old, both)

        @block.vector
        def _(dve):
            def take_v(s, p):
                dve.wait_ge(v_ready, s + 1)
                wait(dve, o_ready, s - 1)
                nc.vector.tensor_copy(v[p][:], v_ps[:]).then_inc(v_taken, 1)

            def maxima(s, p):
                dve.wait_ge(s_ready, s + 1)
                nc.vector.reduce_max(top[:], s_ps[p][:], AX.X).then_inc(top_ready, 1)
                dve.wait_ge(top_ready, s + 1)
                wait(dve, probs_ready, 2 * s - 2)
                nc.vector.tensor_scalar(minus_top[p][:], top[:], -1.0, None, ALU.mult).then_inc(minus_ready, 1)

            def add_out(s, p):
                dve.wait_ge(probs_ready, 2 * s + 2)
                wait(dve, x_added, s)
                nc.vector.reciprocal(inv[:], total[p][:]).then_inc(inv_ready, 1)
                dve.wait_ge(inv_ready, s + 1)
                dve.wait_ge(o_ready, s + 1)
                for t in range(2):
                    at = x[:, bass.ds(2 * s + t, 1), :].squeeze(1)
                    last = nc.vector.scalar_tensor_tensor(at, o_ps[:, t, :], inv[:, t:t + 1], at, ALU.mult, ALU.add)
                last.then_inc(x_added, 1)

            def new(s, p):
                take_v(s, p)
                maxima(s, p)

            def old(s, p):
                add_out(s, p)

            def both(s, p):
                take_v(s, p)
                maxima(s, p)
                add_out(s - 1, 1 - p)

            steps(dve, new, old, both)

        @block.gpsimd
        def _(pool):
            scatter(pool, 0, TILES)
            scattered_all(pool)


def program(nc, x_in, constants, gate0, gate1, att0, att1, packs0, packs1, out):
    rows_in = [nc.dram_tensor(f"rows_in{l}", [n * FT, D], F32, kind="Internal").ap() for l, n in enumerate((NT0, NT1))]
    rows_out = [nc.dram_tensor(f"rows_out{l}", [n * FT, D], F32, kind="Internal").ap() for l, n in enumerate((NT0, NT1))]
    with ExitStack() as ctx:
        def sb(name, shape, dt=F32):
            return ctx.enter_context(nc.sbuf_tensor(name, shape, dt))

        x, xn, xnT = sb("x", [P, TILES, D]), sb("xn", [P, TILES, D]), sb("xnT", [P, TOKENS])
        const = sb("const", [P, C_ALL])
        const_bf = sb("const_bf", [P, C_REV], BF16)
        gates = [sb("gate0", [P, E0]), sb("gate1", [P, E1])]
        routing = [Routing(ctx, nc, f"routing{l}", e, n) for l, (e, n) in enumerate(((E0, NT0), (E1, NT1)))]
        weights_in, zero_set, rows_zeroed = (ctx.enter_context(nc.semaphore(n)) for n in ("weights_in", "zero_set", "rows_zeroed"))
        scattered = [ctx.enter_context(nc.semaphore(f"scattered{l}")) for l in range(2)]
        scatters = [scatter_of(nc, xn, rows_in[l], routing[l], scattered[l]) for l in range(2)]

        with ExitStack() as first:
            zero = first.enter_context(nc.sbuf_tensor("zero", [P, 2048], F32))
            block = first.enter_context(nc.Block())

            @block.sync
            def _(sp):
                for dst, src in ((x[:], x_in.rearrange("(t p) d -> p t d", p=P)), (const[:], constants),
                                 (gates[0][:], gate0), (gates[1][:], gate1)):
                    sp.dma_start(dst, src).then_inc(weights_in, 16)
                sp.wait_ge(weights_in, 64)
                sp.wait_ge(zero_set, 1)
                step = 16 * P
                for rows in rows_in:
                    for r in range(0, rows.shape[0], step):
                        sp.dma_start(rows[r:r + step, :].rearrange("(p t) d -> p (t d)", p=P), zero[:]).then_inc(rows_zeroed, 16)
                sp.wait_ge(rows_zeroed, 16 * sum(rows.shape[0] // step for rows in rows_in))

            @block.vector
            def _(dve):
                nc.vector.memset(zero[:], 0.0).then_inc(zero_set, 1)
                dve.wait_ge(weights_in, 64)
                nc.vector.tensor_copy(const_bf[:], const[:, 0:C_REV])

        norm_and_route(nc, "route0", x, xn, xnT, const, const_bf, gates[0], routing[0], False)
        with ExitStack() as layer:
            parts = [layer.enter_context(nc.sbuf_tensor(f"att0_w{i}", list(a.shape), F32)) for i, a in enumerate(att0)]
            load_all(nc, layer, "att0_in", parts, att0)
            causal_attention(nc, x, xnT, const, const_bf, *parts, *scatters[0])
        expert_tiles(nc, "experts0", NT0, const, packs0, False, True, rows_in=rows_in[0], rows_out=rows_out[0],
                     expert_of_tile=routing[0].expert_of_tile)
        combine(nc, "combine0", x, rows_out[0], routing[0])
        norm_and_route(nc, "route1", x, xn, xnT, const, const_bf, gates[1], routing[1], True)
        with ExitStack() as layer:
            parts = [layer.enter_context(nc.sbuf_tensor(f"att1_w{i}", list(a.shape), F32)) for i, a in enumerate(att1)]
            load_all(nc, layer, "att1_in", parts, att1)
            attention(nc, x, xnT, const, *parts, *scatters[1])
        expert_tiles(nc, "experts1", NT1, const, packs1[0:E1], True, True, rows_in=rows_in[1], rows_out=rows_out[1],
                     expert_of_tile=routing[1].expert_of_tile)
        expert_tiles(nc, "shared", TOKENS // FT, const, packs1[E1:E1 + 1], True, False, x=x, xnT=xnT)
        combine(nc, "combine1", x, rows_out[1], routing[1], out)


def load_all(nc, ctx, name, tiles, arrays):
    loaded = ctx.enter_context(nc.semaphore(name))
    with nc.Block() as block:
        @block.sync
        def _(sp):
            for dst, src in zip(tiles, arrays):
                sp.dma_start(dst[:], src).then_inc(loaded, 16)
            sp.wait_ge(loaded, 16 * len(arrays))


def kernel(L0_attn_encodings, L0_attn_attn_W, L0_attn_attn_b, L0_attn_out_W, L0_attn_out_b, L0_ffn_Wg, L0_ffn_W1, L0_ffn_b1,
           L0_ffn_W2, L0_ffn_b2, L1_attn_W_qkv, L1_ffn_shared_up, L1_ffn_shared_gate, L1_ffn_shared_down, L1_ffn_routed_up,
           L1_ffn_routed_gate, L1_ffn_routed_down, L1_ffn_router_w):
    import concourse.bacc as bacc
    from concourse.bass_utils import run_bass_kernel_spmd

    host = np.asarray

    def down_rows(w):
        return w.transpose(0, 2, 1).reshape(-1, CH, P, D).transpose(0, 2, 1, 3).reshape(-1, P, CH * D)

    w = host(L0_attn_attn_W).reshape(D, HG, HM, 3, HS)
    b = host(L0_attn_attn_b).reshape(HG, HM, 3, HS)
    rows = lambda k: np.broadcast_to(w[:, :, None, :, k], (D, HG, 4, HM, HS)).reshape(D, HG * P)
    bias = lambda k: np.broadcast_to(b[:, None, :, k], (HG, 4, HM, HS)).reshape(HG, P).T
    everywhere = lambda a: np.broadcast_to(a.reshape(1, -1), (P, a.size))
    att0 = [rows(0), rows(1), w[:, :, :, 2].reshape(D, D), np.concatenate([bias(0), bias(1)], 1), everywhere(b[:, :, 2]),
            host(L0_attn_out_W), everywhere(host(L0_attn_out_b))]
    w1 = host(L1_attn_W_qkv)
    att1 = [w1[i * D:(i + 1) * D].T for i in range(3)]
    E = E0
    packs0 = np.concatenate([host(L0_ffn_W1).transpose(0, 2, 1), down_rows(host(L0_ffn_W2)),
                             host(L0_ffn_b1).reshape(E, CH, P).transpose(0, 2, 1),
                             np.broadcast_to(host(L0_ffn_b2)[:, None], (E, P, D))], 2)
    experts = lambda routed, shared: np.concatenate([host(routed), host(shared)[None]])
    packs1 = np.concatenate([experts(L1_ffn_routed_gate, L1_ffn_shared_gate).transpose(0, 2, 1),
                             experts(L1_ffn_routed_up, L1_ffn_shared_up).transpose(0, 2, 1),
                             down_rows(experts(L1_ffn_routed_down, L1_ffn_shared_down))], 2)
    arrays = {"x": host(L0_attn_encodings).reshape(TOKENS, D), "constants": shape_constants(), "gate0": host(L0_ffn_Wg).T,
              "gate1": host(L1_ffn_router_w).T, "packs0": packs0, "packs1": packs1}
    arrays |= {f"att0_{i}": a for i, a in enumerate(att0)} | {f"att1_{i}": a for i, a in enumerate(att1)}
    arrays = {n: np.ascontiguousarray(a) for n, a in arrays.items()}

    nc = bacc.Bacc("TRN2", target_bir_lowering=False, num_devices=1)
    ap = {n: nc.dram_tensor(f"in_{n}", a.shape, mybir.dt.from_np(a.dtype), kind="ExternalInput").ap() for n, a in arrays.items()}
    out = nc.dram_tensor("out", [TOKENS, D], F32, kind="ExternalOutput").ap()
    program(nc, ap["x"], ap["constants"], ap["gate0"], ap["gate1"], [ap[f"att0_{i}"] for i in range(len(att0))],
            [ap[f"att1_{i}"] for i in range(len(att1))], ap["packs0"], ap["packs1"], out)
    ran = run_bass_kernel_spmd(nc, [{f"in_{n}": a for n, a in arrays.items()}], core_ids=[0])
    return ran.results[0]["out"].reshape(BATCH, SEQ, D)
```

```python
from contextlib import ExitStack

import numpy as np
import concourse.bass as bass
from concourse import mybir
from concourse.alu_op_type import AluOpType as ALU

F32 = mybir.dt.float32
F32R = mybir.dt.float32r
BF16 = mybir.dt.bfloat16
I32 = mybir.dt.int32
ACT = mybir.ActivationFunctionType
AX = mybir.AxisListType

P = 128
D = 128
BATCH, SEQ = 32, 256
TOKENS = BATCH * SEQ
TILES = TOKENS // P
GROUP = 4
GROUPS = TILES // GROUP
H, HS = 16, D // 16
HG, HM = 4, 4
HID = 512
CH = HID // P
E0, E1 = 8, 7
TOP = 2
FT = 256
NT0, NT1 = ((TOP * TOKENS + e * (FT - 1)) // FT for e in (E0, E1))
ROWS = FT * (NT0 + 1)
ZEROED = 16 * P
NEG = -1.0e30
EPS = 1e-5

C_ID, C_TRI, C_ONE, C_MB, C_RM, C_SEL, C_REV, C_TB = 0, 128, 256, 384, 512, 516, 1028, 1036
C_ALL = C_TB + NT0


def shape_constants():
    p = np.arange(P)
    c = np.zeros((P, C_ALL), np.float32)
    c[:, C_ID:C_ID + P] = np.eye(P)
    c[:, C_TRI:C_TRI + P] = p[:, None] < p[None, :]
    c[:, C_ONE:C_ONE + P] = 1.0
    c[:, C_MB:C_MB + P] = np.where(p[None, :] > p[:, None], NEG, 0.0)
    c[:, C_RM:C_RM + HM] = (p[:, None] % 32) // HS == np.arange(HM)[None]
    for m in range(HM):
        c[m, C_SEL + m * P:C_SEL + (m + 1) * P] = 1.0
        c[HM + m, C_SEL + m * P:C_SEL + (m + 1) * P] = 1.0
    c[:, C_REV:C_REV + 8] = 8 - np.arange(8)
    c[:, C_TB:C_TB + NT0] = FT * np.arange(NT0)
    return c


class Routing:

    def __init__(self, ctx, nc, name, experts, tiles):
        sb = lambda n, s, d: ctx.enter_context(nc.sbuf_tensor(f"{name}_{n}", s, d))
        self.experts, self.tiles = experts, tiles
        self.weight = [sb(f"weight{k}", [P, TILES], F32) for k in range(TOP)]
        self.slot = [sb(f"slot{k}", [P, TILES], I32) for k in range(TOP)]
        self.expert_of_tile = sb("expert_of_tile", [1, tiles], I32)


def weighted_add(nc, x, tile, got, weight):
    at = x[:, bass.ds(tile, 1), :].squeeze(1)
    return nc.vector.scalar_tensor_tensor(at, got, weight[:, bass.ds(tile, 1)], at, ALU.mult, ALU.add)


def norm_and_route(nc, layer, x, xn, xnT, const, const_bf, gateT, routing, gated_softmax, background,
                   x_in=None, const_loaded=None, const_bf_set=None, results=None):
    E = routing.experts
    ident = const[:, C_ID:C_ID + P]
    with ExitStack() as ctx:
        sb = lambda n, s, d=F32: ctx.enter_context(nc.sbuf_tensor(f"{layer}_{n}", s, d))
        pb = lambda n, s, d=F32: ctx.enter_context(nc.psum_tensor(f"{layer}_{n}", s, d))
        sem = lambda n: ctx.enter_context(nc.semaphore(f"{layer}_{n}"))
        stats = [sb(f"stats{i}", [P, GROUP, 6]) for i in range(2)]
        dmean, mean, var, root, rstd, shift, newton = (
            [sb(f"{n}{i}", [P, GROUP]) for i in range(2)] for n in ("dmean", "mean", "var", "root", "rstd", "shift", "newton"))
        logits = sb("logits", [P, TILES, E])
        score, hot1, hot2, base = (sb(n, [P, TILES, E]) for n in ("score", "hot1", "hot2", "base"))
        hits = sb("hits", [P, TILES, E], BF16)
        top1, top2, first, t1, t2, t3 = (sb(n, [P, TILES]) for n in ("top1", "top2", "first", "t1", "t2", "t3"))
        upto = sb("upto", [P, TILES, E])
        padded_i = sb("padded_i", [P, E], I32)
        total, padded, ends, starts = (sb(n, [P, E]) for n in ("total", "padded", "ends", "starts"))
        passed = sb("passed", [1, routing.tiles, E])
        expert_f = sb("expert_f", [1, routing.tiles])
        xn_now = [sb(f"xn_now{i}", [P, GROUP, P]) for i in range(2)]
        xnT_now = [sb(f"xnT_now{i}", [P, GROUP * P]) for i in range(2)]
        got = [[[sb(f"got{i}_{t}_{k}", [P, D]) for k in range(TOP)] for t in range(GROUP)] for i in range(2)] if results else None
        xn_kept = [sem(f"xn_kept{i}") for i in range(2)]
        xnT_kept = [sem(f"xnT_kept{i}") for i in range(2)]
        group_in = [sem(f"group_in{i}") for i in range(2)]
        turned = [pb(f"turned{i}", [P, GROUP * P]) for i in range(2)]
        logit_ps = [pb(f"logit_ps{i}", [P, GROUP, E]) for i in range(2)]
        within = pb("within", [P, TILES * E])
        in_tile = pb("in_tile", [P, TILES * E])
        half_added, added, moments_ready, stats_ready, xn_ready, turned_ready, xnT_ready = (
            sem(n) for n in ("half_added", "added", "moments_ready", "stats_ready", "xn_ready", "turned_ready", "xnT_ready"))
        logit_ready, logit_read, hits_ready, counts_ready = (sem(n) for n in ("logit_ready", "logit_read", "hits_ready", "counts_ready"))
        exp_asked, exp_ready, chain = (sem(n) for n in ("exp_asked", "exp_ready", "chain"))
        var_ready, root_ready = sem("var_ready"), sem("root_ready")
        block = ctx.enter_context(nc.Block())

        def wait(eng, semaphore, value):
            if not isinstance(value, int) or value > 0:
                eng.wait_ge(semaphore, value)

        def steps(eng, step):
            for g in range(4):
                step(g, g % 2, g // 2, range(g + 1))
            with eng.Fori(0, (GROUPS - 4) // 2) as r:
                for i in range(2):
                    step(2 * r + (4 + i), i, r + 2, range(4))
            for g in range(GROUPS, GROUPS + 3):
                step(g, g % 2, g // 2, range(g - GROUPS + 1, 4))

        @block.vector
        def _(dve):
            done = [0]

            def chained(ins):
                done[0] += 1
                ins.then_inc(chain, 1)
                dve.wait_ge(chain, done[0])

            def take_group(g, i, turn):
                if results is None:
                    dve.wait_ge(group_in[i], 16 * turn + 16)
                    return
                dve.wait_ge(group_in[i], 16 * TOP * GROUP * turn + 16 * TOP * GROUP)
                for k, after in enumerate((half_added, added)):
                    if k:
                        dve.wait_ge(half_added, g + 1)
                    for t in range(GROUP):
                        last = weighted_add(nc, x, GROUP * g + t, got[i][t][k][:], results[1].weight[k])
                    last.then_inc(after, 1)
                dve.wait_ge(added, g + 1)

            def moments(g, i):
                for t in range(GROUP):
                    last = nc.vector.bn_stats(stats[i][:, t, :], x[:, bass.ds(GROUP * g + t, 1), :].squeeze(1))
                last.then_inc(moments_ready, 1)
                dve.wait_ge(moments_ready, 5 * g + 1)
                m_even, q_even, m_odd, q_odd = (stats[i][:, :, n] for n in (1, 2, 4, 5))
                nc.vector.tensor_tensor(mean[i][:], m_even, m_odd, ALU.add)
                nc.vector.tensor_tensor(dmean[i][:], m_even, m_odd, ALU.subtract).then_inc(moments_ready, 1)
                nc.vector.tensor_tensor(var[i][:], q_even, q_odd, ALU.add).then_inc(moments_ready, 1)
                dve.wait_ge(moments_ready, 5 * g + 3)
                nc.vector.tensor_tensor(dmean[i][:], dmean[i][:], dmean[i][:], ALU.mult).then_inc(moments_ready, 1)
                nc.vector.tensor_scalar(var[i][:], var[i][:], 1.0 / D, EPS, ALU.mult, ALU.add).then_inc(moments_ready, 1)
                dve.wait_ge(moments_ready, 5 * g + 5)
                nc.vector.scalar_tensor_tensor(var[i][:], dmean[i][:], 0.25, var[i][:], ALU.mult, ALU.add).then_inc(var_ready, 1)

            def inverse_root(g, i):
                dve.wait_ge(root_ready, g + 1)
                ops = (lambda: nc.vector.reciprocal(rstd[i][:], root[i][:]),
                       lambda: nc.vector.tensor_tensor(newton[i][:], rstd[i][:], rstd[i][:], ALU.mult),
                       lambda: nc.vector.tensor_tensor(newton[i][:], newton[i][:], var[i][:], ALU.mult),
                       lambda: nc.vector.tensor_scalar(newton[i][:], newton[i][:], -0.5, 1.5, ALU.mult, ALU.add),
                       lambda: nc.vector.tensor_tensor(rstd[i][:], rstd[i][:], newton[i][:], ALU.mult),
                       lambda: nc.vector.scalar_tensor_tensor(shift[i][:], mean[i][:], -0.5, rstd[i][:], ALU.mult, ALU.mult))
                for n, op in enumerate(ops):
                    op().then_inc(stats_ready, 1)
                    if n + 1 < len(ops):
                        dve.wait_ge(stats_ready, 6 * g + n + 1)

            def step(g, i, turn, stages):
                if 0 in stages:
                    take_group(g, i, turn)
                if 1 in stages:
                    inverse_root(g - 1, 1 - i)
                if 0 in stages:
                    moments(g, i)
                if 3 in stages:
                    dve.wait_ge(logit_ready, g - 2)
                    nc.vector.tensor_copy(logits[:, bass.ds(GROUP * (g - 3), GROUP), :], logit_ps[1 - i][:]).then_inc(logit_read, 1)

            steps(dve, step)
            if const_loaded is not None:
                dve.wait_ge(*const_loaded)
            dve.wait_ge(logit_read, GROUPS)

            wide = lambda a: a[:].unsqueeze(2).to_broadcast([P, TILES, E])
            rev = const[:, C_REV:C_REV + E].unsqueeze(1).to_broadcast([P, TILES, E])
            for top, hot in ((top1, hot1), (top2, hot2)):
                src = logits if hot is hot1 else base
                chained(nc.vector.reduce_max(top[:], src[:], AX.X))
                chained(nc.vector.tensor_tensor(score[:], src[:], wide(top), ALU.is_ge))
                chained(nc.vector.tensor_tensor(score[:], score[:], rev, ALU.mult))
                chained(nc.vector.reduce_max(first[:], score[:], AX.X))
                chained(nc.vector.tensor_tensor(hot[:], score[:], wide(first), ALU.is_equal))
                if hot is hot1:
                    chained(nc.vector.scalar_tensor_tensor(base[:], hot1[:], -3.0e38, logits[:], ALU.mult, ALU.add))
            nc.vector.tensor_tensor(hits[:], hot1[:], hot2[:], ALU.add).then_inc(hits_ready, 1)

            if gated_softmax:
                chained(nc.vector.tensor_tensor(base[:], logits[:], wide(top1), ALU.subtract))
                nc.vector.tensor_tensor(t1[:], top2[:], top1[:], ALU.subtract).then_inc(exp_asked, 1)
                dve.wait_ge(exp_ready, 1)
                chained(nc.vector.reduce_sum(t2[:], score[:], AX.X))
                chained(nc.vector.reciprocal(t2[:], t2[:]))
                chained(nc.vector.tensor_tensor(t3[:], t1[:], t2[:], ALU.mult))
                chained(nc.vector.tensor_tensor(first[:], t2[:], t3[:], ALU.add))
                chained(nc.vector.tensor_scalar(first[:], first[:], 1e-9, None, ALU.add))
                chained(nc.vector.reciprocal(first[:], first[:]))
                nc.vector.tensor_tensor(routing.weight[0][:], t2[:], first[:], ALU.mult)
                chained(nc.vector.tensor_tensor(routing.weight[1][:], t3[:], first[:], ALU.mult))
            else:
                nc.vector.tensor_tensor(t1[:], top2[:], top1[:], ALU.subtract).then_inc(exp_asked, 1)
                dve.wait_ge(exp_ready, 1)
                chained(nc.vector.tensor_scalar(t2[:], t1[:], 1.0, None, ALU.add))
                chained(nc.vector.reciprocal(routing.weight[0][:], t2[:]))
                chained(nc.vector.tensor_tensor(routing.weight[1][:], t1[:], routing.weight[0][:], ALU.mult))

            dve.wait_ge(counts_ready, 1)
            here = in_tile[:].rearrange("p (t e) -> p t e", e=E)
            before = within[:].rearrange("p (t e) -> p t e", e=E)
            ones = const[:, C_ONE:C_ONE + TILES]
            for e in range(E):
                last = nc.vector.tensor_tensor_scan(upto[:, :, e], ones, here[:, :, e], 0.0, ALU.mult, ALU.add)
            chained(last)
            chained(nc.vector.tensor_scalar(padded_i[:], upto[:, TILES - 1, :], float(FT - 1), None, ALU.add))
            chained(nc.vector.tensor_scalar(padded_i[:], padded_i[:], FT.bit_length() - 1, FT.bit_length() - 1,
                                            ALU.arith_shift_right, ALU.arith_shift_left))
            chained(nc.vector.tensor_copy(padded[:], padded_i[:]))
            chained(nc.vector.tensor_tensor_scan(ends[:], const[:, C_ONE:C_ONE + E], padded[:], 0.0, ALU.mult, ALU.add))
            chained(nc.vector.tensor_tensor(starts[:], ends[:], padded[:], ALU.subtract))
            chained(nc.vector.tensor_tensor(upto[:], upto[:], here, ALU.subtract))
            chained(nc.vector.tensor_tensor(upto[:], upto[:], before, ALU.add))
            chained(nc.vector.tensor_tensor(base[:], upto[:], starts[:].unsqueeze(1).to_broadcast([P, TILES, E]), ALU.add))
            for k, hot in enumerate((hot1, hot2)):
                chained(nc.vector.tensor_tensor(score[:], base[:], hot[:], ALU.mult))
                chained(nc.vector.reduce_sum(first[:], score[:], AX.X))
                chained(nc.vector.tensor_copy(routing.slot[k][:], first[:]))
            n = routing.tiles
            chained(nc.vector.tensor_tensor(
                passed[:], const[0:1, C_TB:C_TB + n].unsqueeze(2).to_broadcast([1, n, E]),
                ends[0:1, :].unsqueeze(1).to_broadcast([1, n, E]), ALU.is_ge))
            chained(nc.vector.reduce_sum(expert_f[:], passed[:], AX.X))
            chained(nc.vector.tensor_scalar(expert_f[:], expert_f[:], float(E - 1), None, ALU.min))
            chained(nc.vector.tensor_copy(routing.expert_of_tile[:], expert_f[:]))

        @block.sync
        def _(sp):
            def step(g, i, turn, stages):
                if 1 in stages:
                    sp.wait_ge(xn_ready, g)
                    sp.dma_start(xn[:, bass.ds(GROUP * (g - 1), GROUP), :], xn_now[1 - i][:]).then_inc(xn_kept[1 - i], 16)
                if 2 in stages:
                    sp.wait_ge(xnT_ready, g - 1)
                    sp.dma_start(xnT[:, bass.ds(GROUP * P * (g - 2), GROUP * P)], xnT_now[i][:]).then_inc(xnT_kept[i], 16)

            steps(sp, step)
            for i in range(2):
                sp.wait_ge(xn_kept[i], 16 * (GROUPS // 2))
                sp.wait_ge(xnT_kept[i], 16 * (GROUPS // 2))

        @block.gpsimd
        def _(pool):
            def load_group(turn, i):
                wait(pool, group_in[i], 16 * turn)
                g = 2 * turn + i
                pool.dma_start(x[:, bass.ds(GROUP * g, GROUP), :],
                               x_in[bass.ds(GROUP * P * g, GROUP * P), :].rearrange("(t p) d -> p t d", p=P)).then_inc(group_in[i], 16)

            if results is None:
                for i in range(2):
                    load_group(0, i)
                with pool.Fori(1, GROUPS // 2) as turn:
                    for i in range(2):
                        load_group(turn, i)
            else:
                for t in range(TILES):
                    g, i = t // GROUP, t // GROUP % 2
                    if g > 1 and t % GROUP == 0:
                        pool.wait_ge(added, g - 1)
                    for k in range(TOP):
                        at = bass.IndirectOffsetOnAxis(ap=results[1].slot[k][:, t:t + 1], axis=0)
                        nc.gpsimd.indirect_dma_start(got[i][t % GROUP][k][:], None, results[0], at).then_inc(group_in[i], 16)
            background(pool, xnT_ready, GROUPS)

        @block.scalar
        def _(act):
            def normalise(g, i, turn):
                act.wait_ge(stats_ready, 6 * g + 6)
                wait(act, turned_ready, g - 1)
                wait(act, xn_kept[i], 16 * turn)
                for t in range(GROUP):
                    last = nc.scalar.activation(xn_now[i][:, t:t + 1, :], x[:, bass.ds(GROUP * g + t, 1), :], ACT.Identity,
                                                bias=shift[i][:, t:t + 1], scale=rstd[i][:, t:t + 1])
                last.then_inc(xn_ready, 1)

            def take_turned(g, i, turn):
                act.wait_ge(turned_ready, g + 1)
                wait(act, logit_ready, g - 1)
                wait(act, xnT_kept[i], 16 * turn)
                nc.scalar.activation(xnT_now[i][:], turned[i][:], ACT.Copy).then_inc(xnT_ready, 1)

            def step(g, i, turn, stages):
                if 0 in stages:
                    act.wait_ge(var_ready, g + 1)
                    wait(act, stats_ready, 6 * (g - 1))
                    nc.scalar.activation(root[i][:], var[i][:], ACT.Sqrt).then_inc(root_ready, 1)
                if 1 in stages:
                    normalise(g - 1, 1 - i, turn - 1 + i)
                if 2 in stages:
                    take_turned(g - 2, i, turn - 1)

            steps(act, step)
            act.wait_ge(exp_asked, 1)
            if gated_softmax:
                nc.scalar.activation(score[:], base[:], ACT.Exp)
            nc.scalar.activation(t1[:], t1[:], ACT.Exp).then_inc(exp_ready, 1)

        @block.tensor
        def _(pe):
            def turn_group(g, i):
                pe.wait_ge(xn_ready, g + 1)
                wait(pe, xnT_ready, g - 1)
                for t in range(GROUP):
                    last = nc.tensor.transpose(turned[i][:, t * P:(t + 1) * P], xn_now[i][:, t, :], ident)
                last.then_inc(turned_ready, 1)

            def score_experts(g, i):
                pe.wait_ge(xnT_ready, g + 1)
                wait(pe, logit_read, g - 1)
                for t in range(GROUP):
                    last = nc.tensor.matmul(logit_ps[i][:, t, :], xnT_now[i][:, t * P:(t + 1) * P], gateT[:, 0:E],
                                            start=(t == 0), stop=(t == GROUP - 1), skip_group_check=True)
                last.then_inc(logit_ready, 1)

            def step(g, i, turn, stages):
                if 1 in stages:
                    turn_group(g - 1, 1 - i)
                if 2 in stages:
                    score_experts(g - 2, i)

            if const_loaded is not None:
                pe.wait_ge(*const_loaded)
            steps(pe, step)
            if const_bf_set is not None:
                pe.wait_ge(const_bf_set, 1)
            pe.wait_ge(hits_ready, 1)
            flat = hits[:].rearrange("p t e -> p (t e)")
            nc.tensor.matmul(within[:], const_bf[:, C_TRI:C_TRI + P], flat, start=True, stop=True)
            nc.tensor.matmul(in_tile[:], const_bf[:, C_ONE:C_ONE + P], flat, start=True, stop=True).then_inc(counts_ready, 1)


START = 16
UNROLL = 6
NY = 3


class Tile:

    def __init__(self, turn, place):
        self.turn, self.place = turn + place // UNROLL, place % UNROLL

    @property
    def i(self):
        return UNROLL * self.turn + self.place

    def back(self, n):
        return Tile(self.turn, self.place - n)

    def loaded(self):
        return START + 32 * self.turn + 32

    def gathered(self):
        return 16 * TOP * (FT // P) * (self.turn + 1)

    def stored(self):
        return START + 16 * (UNROLL // NY) * self.turn + 16 * (self.place // NY + 1)


def over_tiles(eng, first, end, body):
    turns = (end - first) // UNROLL
    if turns > 1:
        with eng.Fori(0, turns) as r:
            for u in range(UNROLL):
                body(Tile(r, first + u))
        first += turns * UNROLL
    for i in range(first, end):
        body(Tile(0, i))


def pack_cols(gated):
    return 3 * HID if gated else 2 * HID + CH + D


def expert_tiles(nc, layer, tiles, const, packs, gated, routed, rows_in, rows_out, routing, x=None, xnT=None, out=None):
    ident = const[:, C_ID:C_ID + P]
    W = pack_cols(gated)
    S = FT // P
    with ExitStack() as ctx:
        sb = lambda n, s, d=F32: ctx.enter_context(nc.sbuf_tensor(f"{layer}_{n}", s, d))
        pb = lambda n, s, d=F32: ctx.enter_context(nc.psum_tensor(f"{layer}_{n}", s, d))
        sem = lambda n: ctx.enter_context(nc.semaphore(f"{layer}_{n}"))
        pack = [sb(f"pack{i}", [P, W]) for i in range(UNROLL if routed else 1)]
        tok = [sb(f"tok{i}", [P, S, D]) for i in range(UNROLL)] if routed else None
        xT = [sb(f"xT{i}", [P, FT]) for i in range(2)]
        hT = [sb(f"hT{i}", [P, CH, FT]) for i in range(2)]
        y = [sb(f"y{i}", [P, S, D]) for i in range(NY)]
        turned = pb("turned", [P, FT])
        silu = [sb(f"silu{i}", [P, 2, FT]) for i in range(2)] if gated else None
        hid_ps = [pb(f"hid_ps{i}", [P, 2, FT]) for i in range(4)]
        y_ps = [pb(f"y_ps{i}", [P, S, D]) for i in range(2)]
        got = [[[sb(f"got{i}_{s}_{k}", [P, D]) for k in range(TOP)] for s in range(S)] for i in range(UNROLL)] if not routed else None
        gathered = [sem(f"gathered{i}") for i in range(UNROLL)] if not routed else None
        half_added, added, written = (sem(n) for n in ("half_added", "added", "written")) if not routed else (None,) * 3
        tile_in = [sem(f"tile_in{i}") for i in range(UNROLL if routed else 1)]
        y_out = [sem(f"y_out{i}") for i in range(NY)] if routed else None
        turned_ready, xT_ready, hid_ready, silu_ready, hT_ready, y_ready, y_kept = (
            sem(n) for n in ("turned_ready", "xT_ready", "hid_ready", "silu_ready", "hT_ready", "y_ready", "y_kept"))
        block = ctx.enter_context(nc.Block())
        wp = lambda j: pack[j] if routed else pack[0]

        @block.sync
        def _(sp):
            def load(tile):
                i, j = tile.i, tile.place
                sp.wait_ge(y_kept, START + i - (UNROLL - 1))
                sp.dma_start(tok[j][:], rows_in[bass.ds(i * FT, FT), :].rearrange("(s p) d -> p s d", p=P)).then_inc(tile_in[j], 16)
                e = sp.value_load(routing.expert_of_tile[0:1, bass.ds(i, 1)], min_val=0, max_val=packs.shape[0] - 1)
                sp.dma_start(pack[j][:], packs[bass.ds(e, 1), :, :].rearrange("e p w -> (e p) w")).then_inc(tile_in[j], 16)

            def store(tile):
                i, j = tile.i, tile.place
                sp.wait_ge(y_kept, START + i + 1)
                sp.dma_start(rows_out[bass.ds(i * FT, FT), :].rearrange("(s p) d -> p s d", p=P), y[j % NY][:]).then_inc(y_out[j % NY], 16)

            if not routed:
                sp.dma_start(pack[0][:], packs[0, :, :]).then_inc(tile_in[0], 16)
                sp.wait_ge(tile_in[0], 16)

                def write(tile):
                    sp.wait_ge(added, tile.i + 1)
                    sp.dma_start(out[bass.ds(tile.i * FT, FT), :].rearrange("(s p) d -> p s d", p=P),
                                 x[:, bass.ds(S * tile.i, S), :]).then_inc(written, 16)

                over_tiles(sp, 0, tiles, write)
                sp.wait_ge(written, 16 * tiles)
                return
            for semaphore in tile_in + y_out:
                sp.sem_inc(semaphore, START)
            over_tiles(sp, 0, UNROLL - 1, load)

            def step(tile):
                load(tile)
                store(tile.back(UNROLL - 1))

            over_tiles(sp, UNROLL - 1, tiles, step)
            for i in range(tiles - UNROLL + 1, tiles):
                store(Tile(0, i))
            for i in range(tiles - NY, tiles):
                sp.wait_ge(y_out[i % NY], Tile(0, i).stored())

        @block.tensor
        def _(pe):
            def turn(tile):
                i, j = tile.i, tile.place
                pe.wait_ge(tile_in[j], tile.loaded())
                pe.wait_ge(xT_ready, START + i)
                for s in range(S):
                    last = nc.tensor.transpose(turned[:, s * P:(s + 1) * P], tok[j][:, s, :], ident)
                last.then_inc(turned_ready, 1)

            def hidden(tile):
                i, j = tile.i, tile.place
                if routed:
                    pe.wait_ge(xT_ready, START + i + 1)
                    src = xT[j % 2][:]
                else:
                    src = xnT[:, bass.ds(i * FT, FT)]
                for half in range(2):
                    if gated:
                        pe.wait_ge(hT_ready, START + 2 * i - 1 + half)
                        into = [hid_ps[2 * half], hid_ps[2 * half + 1]]
                    else:
                        pe.wait_ge(hT_ready, START + 2 * i - 3 + half)
                        into = [hid_ps[2 * (j % 2) + half]]
                    for k, bank in enumerate(into):
                        for c in range(2):
                            o = k * HID + (2 * half + c) * P
                            last = nc.tensor.matmul(bank[:, c, :], wp(j)[:, o:o + P], src, start=(c == 0), stop=(c == 1),
                                                    skip_group_check=True)
                        last.then_inc(hid_ready, 1)

            def down(tile):
                i, j = tile.i, tile.place
                pe.wait_ge(hT_ready, START + 2 * i + 2)
                pe.wait_ge(y_kept, START + i - 1)
                o = (2 if gated else 1) * HID
                for s in range(S):
                    for c in range(CH):
                        last = nc.tensor.matmul(y_ps[j % 2][:, s, :], hT[j % 2][:, c, s * P:(s + 1) * P],
                                                wp(j)[:, o + c * D:o + (c + 1) * D], start=(c == 0), stop=(c == CH - 1))
                last.then_inc(y_ready, 1)

            pe.sem_inc(turned_ready, START)
            pe.sem_inc(y_ready, START)
            pe.sem_inc(hid_ready, START)
            if not routed:
                pe.wait_ge(tile_in[0], 16)
            def step(tile):
                if routed:
                    turn(tile.back(-1))
                hidden(tile)
                down(tile.back(1))

            if routed:
                turn(Tile(0, 0))
                turn(Tile(0, 1))
            hidden(Tile(0, 0))
            over_tiles(pe, 1, tiles - 1, step)
            hidden(Tile(0, tiles - 1))
            down(Tile(0, tiles - 2))
            down(Tile(0, tiles - 1))

        @block.scalar
        def _(act):
            def step(tile):
                i, j = tile.i, tile.place
                if gated:
                    for half in range(2):
                        act.wait_ge(hid_ready, START + 4 * i + 2 * half + 1)
                        act.wait_ge(hT_ready, START + 2 * i - 1 + half)
                        nc.scalar.activation(silu[half][:], hid_ps[2 * half][:], ACT.Silu).then_inc(silu_ready, 1)
                else:
                    act.wait_ge(y_ready, START + i - 1)
                    for half in range(2):
                        act.wait_ge(hid_ready, START + 2 * i + half + 1)
                        for c in range(2):
                            b = 2 * HID + 2 * half + c
                            last = nc.scalar.activation(hT[j % 2][:, 2 * half + c, :], hid_ps[2 * (j % 2) + half][:, c, :],
                                                        ACT.Gelu, bias=wp(j)[:, b:b + 1])
                        last.then_inc(hT_ready, 1)

            if not gated:
                act.sem_inc(hT_ready, START)
            over_tiles(act, 0, tiles, step)

        @block.vector
        def _(dve):
            def take_turned(tile):
                i, j = tile.i, tile.place
                dve.wait_ge(turned_ready, START + i + 1)
                per = 4 if gated else 2
                dve.wait_ge(hid_ready, START + per * (i - 1))
                nc.vector.tensor_copy(xT[j % 2][:], turned[:]).then_inc(xT_ready, 1)

            def multiply(tile):
                i, j = tile.i, tile.place
                dve.wait_ge(y_ready, START + i - 1)
                for half in range(2):
                    dve.wait_ge(hid_ready, START + 4 * i + 2 * half + 2)
                    dve.wait_ge(silu_ready, 2 * i + half + 1)
                    nc.vector.tensor_tensor(hT[j % 2][:, 2 * half:2 * half + 2, :], hid_ps[2 * half + 1][:], silu[half][:],
                                            ALU.mult).then_inc(hT_ready, 1)

            def take_y(tile):
                i, j = tile.i, tile.place
                dve.wait_ge(y_ready, START + i + 1)
                if not routed:
                    at = x[:, bass.ds(S * i, S), :]
                    nc.vector.tensor_tensor(at, at, y_ps[j % 2][:], ALU.add).then_inc(y_kept, 1)
                    dve.wait_ge(y_kept, START + i + 1)
                    dve.wait_ge(gathered[j], tile.gathered())
                    for k, after in enumerate((half_added, added)):
                        if k:
                            dve.wait_ge(half_added, i + 1)
                        for s in range(S):
                            last = weighted_add(nc, x, S * i + s, got[j][s][k][:], routing.weight[k])
                        last.then_inc(after, 1)
                    return
                dve.wait_ge(y_out[j % NY], tile.back(NY).stored())
                if gated:
                    nc.vector.tensor_copy(y[j % NY][:], y_ps[j % 2][:]).then_inc(y_kept, 1)
                else:
                    b = 2 * HID + CH
                    bias = wp(j)[:, b:b + D].unsqueeze(1).to_broadcast([P, S, D])
                    nc.vector.tensor_tensor(y[j % NY][:], y_ps[j % 2][:], bias, ALU.add).then_inc(y_kept, 1)

            dve.sem_inc(xT_ready, START)
            dve.sem_inc(y_kept, START)
            if gated:
                dve.sem_inc(hT_ready, START)
            def step(tile, last=False):
                if routed and not last:
                    take_turned(tile.back(-1))
                if gated:
                    multiply(tile)
                take_y(tile.back(1))

            if routed:
                take_turned(Tile(0, 0))
                take_turned(Tile(0, 1))
            if gated:
                multiply(Tile(0, 0))
            over_tiles(dve, 1, tiles - 1, step)
            step(Tile(0, tiles - 1), last=True)
            take_y(Tile(0, tiles - 1))


        @block.gpsimd
        def _(pool):
            for i in range(tiles if not routed else 0):
                if i >= UNROLL:
                    pool.wait_ge(added, i - UNROLL + 1)
                for s in range(S):
                    for k in range(TOP):
                        at = bass.IndirectOffsetOnAxis(ap=routing.slot[k][:, S * i + s:S * i + s + 1], axis=0)
                        nc.gpsimd.indirect_dma_start(got[i % UNROLL][s][k][:], None, rows_out, at).then_inc(gathered[i % UNROLL], 16)


def scatter_of(nc, xn, rows, routing, scattered):
    def scatter(pool, first, end):
        for t in range(first, end):
            for k in range(TOP):
                at = bass.IndirectOffsetOnAxis(ap=routing.slot[k][:, t:t + 1], axis=0)
                nc.gpsimd.indirect_dma_start(rows, at, xn[:, t, :], None).then_inc(scattered, 16)

    def wait_for_all(pool):
        pool.wait_ge(scattered, 16 * TOP * TILES)

    return scatter, wait_for_all


def causal_attention(nc, x, xnT, const, const_bf, w_q, w_k, w_v, b_qk, b_v, w_out, b_out, scatter,
                     scattered_all):
    ident = const[:, C_ID:C_ID + P]
    ident_bf = const_bf[:, C_ID:C_ID + P]
    causal = const_bf[:, C_MB:C_MB + P].unsqueeze(1).to_broadcast([P, 2, P])
    with ExitStack() as ctx:
        sb = lambda n, s, d=F32: ctx.enter_context(nc.sbuf_tensor(f"att_{n}", s, d))
        pb = lambda n, s, d=F32: ctx.enter_context(nc.psum_tensor(f"att_{n}", s, d))
        sem = lambda n: ctx.enter_context(nc.semaphore(f"att_{n}"))
        xT = [sb(f"xT{i}", [P, SEQ]) for i in range(2)]
        full = [sb(f"{n}_full", [P, HG, SEQ]) for n in "qk"]
        q_rows = sb("q_rows", [P, HG, SEQ], F32R)
        q_member = [sb(f"q_member{i}", [P, HG, HM, SEQ], F32R) for i in range(2)]
        k_rows = [sb(f"k_rows{i}", [P, HG, SEQ], F32R) for i in range(2)]
        v_ones = [sb(f"v_ones{i}", [P, 2, H, 32]) for i in range(2)]
        maxima = sb("maxima", [P, 2, H])
        minus_max = sb("minus_max", [P, 2, HG, 2, HM], BF16)
        max_rows = sb("max_rows", [P, HG, SEQ], BF16)
        probs_a = [sb(f"probs_a{i}", [P, HM, SEQ]) for i in range(2)]
        probs_b = [sb(f"probs_b{i}", [P, HM, P]) for i in range(2)]
        oT = sb("oT", [P, HG, SEQ])
        inv = sb("inv", [P, H])
        o_tok = [sb(f"o_tok{i}", [P, H, HS]) for i in range(2)]
        o_cols = sb("o_cols", [P, SEQ])
        with_bias = sb("with_bias", [P, 2, D])

        bank_s = [pb(f"bank_s{i}", [P, 2, SEQ]) for i in range(2)]
        bank_a = pb("bank_a", [P, HM, SEQ])
        bank_b = pb("bank_b", [P, HM, P])
        bank_m = [pb(f"bank_m{i}", [P, 512]) for i in range(3)]

        xT_in = [sem(f"xT_in{i}") for i in range(2)]
        q_filled, q_biased, q_high, q_halves, q_ready = (
            sem(n) for n in ("q_filled", "q_biased", "q_high", "q_halves", "q_ready"))
        k_filled, k_biased, k_high, k_halves, v_filled, v_ready = (
            sem(n) for n in ("k_filled", "k_biased", "k_high", "k_halves", "v_filled", "v_ready"))
        s_ready, max_ready, minus_high, minus_ready, max_turned, rows_ready = (
            sem(n) for n in ("s_ready", "max_ready", "minus_high", "minus_ready", "max_turned", "rows_ready"))
        a_ready, b_ready, exp_a, exp_b, probs_ready, weighed, oT_ready = (
            sem(n) for n in ("a_ready", "b_ready", "exp_a", "exp_b", "probs_ready", "weighed", "oT_ready"))
        back_filled, inv_ready, otok_ready, cols_filled, cols_ready, out_filled, out_taken, x_added = (
            sem(n) for n in ("back_filled", "inv_ready", "otok_ready", "cols_filled", "cols_ready", "out_filled", "out_taken",
                             "x_added"))
        zero_set, constants_set = sem("zero_set"), sem("constants_set")
        block = ctx.enter_context(nc.Block())

        def wait(eng, semaphore, value):
            if not isinstance(value, int) or value > 0:
                eng.wait_ge(semaphore, value)

        def steps(eng, step):
            step(0, 0, "A")
            step(1, 1, "AB")
            step(2, 0, "ABC")
            with eng.Fori(0, (BATCH - 4) // 2) as r:
                step(2 * r + 3, 1, "ABCD")
                step(2 * r + 4, 0, "ABCD")
            step(BATCH - 1, 1, "ABCD")
            step(BATCH, 0, "BCD")
            step(BATCH + 1, 1, "CD")
            step(BATCH + 2, 0, "D")

        @block.tensor
        def _(pe):
            def project_q(s, p, half):
                pe.wait_ge(xT_in[p], 8 * (s - p) + 16)
                wait(pe, rows_ready, 2 * s - 3 + half)
                for g in range(2):
                    last = nc.tensor.matmul(bank_m[half][:, g * SEQ:(g + 1) * SEQ], w_q[:, (2 * half + g) * P:(2 * half + g + 1) * P],
                                            xT[p][:], start=(g == 0), stop=(g == 1), skip_group_check=True)
                last.then_inc(q_filled, 1)

            def project_k(s, p, half):
                pe.wait_ge(q_biased, 2 * s + 1 + half)
                for g in range(2):
                    last = nc.tensor.matmul(bank_m[half][:, g * SEQ:(g + 1) * SEQ], w_k[:, (2 * half + g) * P:(2 * half + g + 1) * P],
                                            xT[p][:], start=(g == 0), stop=(g == 1), skip_group_check=True)
                last.then_inc(k_filled, 1)

            def bank_left(s, half, stages):
                if "A" in stages:
                    pe.wait_ge(k_biased, 2 * s + 3 + half)
                else:
                    pe.wait_ge(rows_ready, 2 * s - 1 + half)

            def project_v(s, p, stages):
                bank_left(s, 0, stages)
                for t in range(2):
                    last = nc.tensor.matmul(bank_m[0][:, t * D:(t + 1) * D], xT[p][:, t * P:(t + 1) * P], w_v[:],
                                            start=(t == 0), stop=(t == 1), skip_group_check=True)
                last.then_inc(v_filled, 1)

            def scores(s, p, first, end):
                for u in range(first, end):
                    g, t, pair = u // 4, u // 2 % 2, u % 2
                    if u % 8 == 0:
                        pe.wait_ge(q_ready, 2 * HM * s + HM * (u // 8 + 1))
                        pe.wait_ge(k_halves, 2 * s + u // 8 + 1)
                    bank = bank_s[u % 2]
                    wait(pe, max_ready, 16 * s + (u - 1))
                    for k in range(2):
                        nc.tensor.matmul(bank[:, k, :], q_member[p][:, g, 2 * pair + k, t * P:(t + 1) * P], k_rows[p][:, g, :],
                                         start=(k == 0), stop=False, skip_group_check=True)
                    nc.tensor.matmul(bank[:, :, t * P:(t + 1) * P], ident_bf, causal,
                                     start=False, stop=True, skip_group_check=True).then_inc(s_ready, 1)

            def turn_maxima(s, half, stages):
                pe.wait_ge(minus_ready, s + 1)
                if half == 0:
                    pe.wait_ge(v_ready, s + 1)
                else:
                    bank_left(s, 1, stages)
                for g in range(2):
                    for t in range(2):
                        last = nc.tensor.matmul(bank_m[half][0:2 * HM, g * SEQ + t * P:g * SEQ + (t + 1) * P],
                                                minus_max[:, t, 2 * half + g, :, :].rearrange("p a m -> p (a m)"), ident_bf,
                                                start=(g + t == 0), stop=(g + t == 2), skip_group_check=True)
                last.then_inc(max_turned, 1)

            def shifted(s, p, g):
                if g == 0:
                    pe.wait_ge(rows_ready, 2 * s + 2)
                wait(pe, exp_a, 4 * s + g)
                for m in range(HM):
                    nc.tensor.matmul(bank_a[:, m, :], k_rows[p][:, g, 0:P], q_member[p][:, g, m, :],
                                     start=(m % 2 == 0), stop=False, skip_group_check=True)
                for m in range(HM):
                    last = nc.tensor.matmul(bank_a[:, m, :], const_bf[:, C_SEL + m * P:C_SEL + (m + 1) * P], max_rows[:, g, :],
                                            start=False, stop=True, skip_group_check=True)
                last.then_inc(a_ready, 1)
                wait(pe, exp_b, 4 * s + g)
                for m in range(0, HM, 2):
                    nc.tensor.matmul(bank_b[:, m:m + 2, :], k_rows[p][:, g, P:2 * P], q_member[p][:, g, m:m + 2, P:2 * P],
                                     start=(m == 0), stop=False, skip_group_check=True)
                for m in range(HM):
                    last = nc.tensor.matmul(bank_b[:, m, :], const_bf[:, C_SEL + m * P:C_SEL + (m + 1) * P], max_rows[:, g, P:2 * P],
                                            start=False, stop=True, skip_group_check=True)
                last.then_inc(b_ready, 1)

            def weigh(s, p, g):
                pe.wait_ge(probs_ready, 8 * s + 2 * g + 2)
                if g == 0:
                    wait(pe, out_taken, s)
                if g == 2:
                    pe.wait_ge(oT_ready, 2 * s + 1)
                at = (g % 2) * SEQ
                for m in range(HM):
                    nc.tensor.matmul(bank_m[2][32 * m:32 * m + 32, at:at + SEQ], v_ones[p][:, 0, HM * g + m, :], probs_a[g % 2][:, m, :],
                                     start=True, stop=False, skip_group_check=True)
                for m in range(HM):
                    last = nc.tensor.matmul(bank_m[2][32 * m:32 * m + 32, at + P:at + SEQ], v_ones[p][:, 1, HM * g + m, :],
                                            probs_b[g % 2][:, m, :], start=False, stop=True, skip_group_check=True)
                last.then_inc(weighed, 1)

            def turn_back(s, t):
                pe.wait_ge(oT_ready, 2 * s + 2)
                if t == 1:
                    pe.wait_ge(otok_ready, 2 * s + 1)
                for g in range(HG):
                    last = nc.tensor.transpose(bank_m[2][:, g * P:(g + 1) * P], oT[:, g, t * P:(t + 1) * P], ident)
                last.then_inc(back_filled, 1)

            def to_columns(s):
                pe.wait_ge(otok_ready, 2 * s + 2)
                for t in range(2):
                    last = nc.tensor.transpose(bank_m[2][:, t * P:(t + 1) * P], o_tok[t][:].rearrange("p h d -> p (h d)"), ident)
                last.then_inc(cols_filled, 1)

            def project_out(s):
                pe.wait_ge(cols_ready, s + 1)
                for t in range(2):
                    last = nc.tensor.matmul(bank_m[2][:, t * D:(t + 1) * D], o_cols[:, t * P:(t + 1) * P], w_out[:],
                                            start=(t == 0), stop=(t == 1), skip_group_check=True)
                last.then_inc(out_filled, 1)

            def step(t, p, stages):
                a, b, c, d = (t - i for i in range(4))
                A, B, C, D_ = (n in stages for n in "ABCD")
                q = 1 - p
                if B: scores(b, q, 0, 2)
                if A: project_q(a, p, 0)
                if D_: turn_back(d, 0)
                if B: scores(b, q, 2, 3)
                if C: shifted(c, p, 0)
                if B: scores(b, q, 3, 4)
                if D_: turn_back(d, 1)
                if B: scores(b, q, 4, 5)
                if A: project_q(a, p, 1)
                if B: scores(b, q, 5, 6)
                if D_: to_columns(d)
                if B: scores(b, q, 6, 7)
                if C: shifted(c, p, 1)
                if B: scores(b, q, 7, 8)
                if D_: project_out(d)
                if B: scores(b, q, 8, 9)
                if A: project_k(a, p, 0)
                if B: scores(b, q, 9, 10)
                if C: weigh(c, p, 0)
                if B: scores(b, q, 10, 11)
                if C: shifted(c, p, 2)
                if B: scores(b, q, 11, 12)
                if C: weigh(c, p, 1)
                if A: project_k(a, p, 1)
                if B: scores(b, q, 12, 13)
                if B: project_v(b, q, stages)
                if B: scores(b, q, 13, 14)
                if C: shifted(c, p, 3)
                if B: scores(b, q, 14, 15)
                if C: weigh(c, p, 2)
                if B: scores(b, q, 15, 16)
                if C: weigh(c, p, 3)
                for half in range(2):
                    if B: turn_maxima(b, half, stages)

            pe.wait_ge(constants_set, 1)
            steps(pe, step)

        @block.sync
        def _(sp):
            def load(s, p):
                wait(sp, v_filled, s - 1)
                sp.dma_start(xT[p][:], xnT[:, bass.ds(s * SEQ, SEQ)]).then_inc(xT_in[p], 16)

            for s in range(2):
                load(s, s)
            with sp.Fori(0, BATCH // 2 - 1) as r:
                for p in range(2):
                    load(2 * r + (2 + p), p)
            for p in range(2):
                sp.wait_ge(xT_in[p], 8 * BATCH)

        @block.scalar
        def _(act):
            def add_bias(s, which, half):
                act.wait_ge((q_filled, k_filled)[which], 2 * s + half + 1)
                wait(act, (q_halves, k_halves)[which], 2 * s - 1 + half)
                for g in range(2):
                    grp = 2 * half + g
                    last = nc.scalar.activation(full[which][:, grp, :], bank_m[half][:, g * SEQ:(g + 1) * SEQ], ACT.Identity,
                                                bias=b_qk[:, HG * which + grp:HG * which + grp + 1])
                last.then_inc((q_biased, k_biased)[which], 1)

            def exponentials(s, g):
                act.wait_ge(a_ready, 4 * s + g + 1)
                wait(act, weighed, 4 * s + (g - 1))
                nc.scalar.activation(probs_a[g % 2][:], bank_a[:], ACT.Exp, scale=HS ** -0.5).then_inc(exp_a, 1)
                act.wait_ge(b_ready, 4 * s + g + 1)
                nc.scalar.activation(probs_b[g % 2][:], bank_b[:], ACT.Exp, scale=HS ** -0.5).then_inc(exp_b, 1)

            def keep_maxima(s, half):
                act.wait_ge(max_turned, 2 * s + half + 1)
                nc.scalar.activation(max_rows[0:2 * HM, 2 * half:2 * half + 2, :],
                                     bank_m[half][0:2 * HM, :].rearrange("p (g q) -> p g q", g=2), ACT.Copy).then_inc(rows_ready, 1)

            def keep_oT(s, half):
                act.wait_ge(weighed, 4 * s + 2 * half + 2)
                nc.scalar.activation(oT[:, 2 * half:2 * half + 2, :], bank_m[2][:].rearrange("p (g q) -> p g q", g=2),
                                     ACT.Copy).then_inc(oT_ready, 1)

            def keep_cols(s):
                act.wait_ge(cols_filled, s + 1)
                nc.scalar.activation(o_cols[:], bank_m[2][:, 0:SEQ], ACT.Copy).then_inc(cols_ready, 1)

            def step(t, p, stages):
                a, b, c, d = (t - i for i in range(4))
                A, B, C, D_ = (n in stages for n in "ABCD")
                if A: add_bias(a, 0, 0)
                if C: exponentials(c, 0)
                if A: add_bias(a, 0, 1)
                if D_: keep_cols(d)
                if C: exponentials(c, 1)
                if A: add_bias(a, 1, 0)
                if C: exponentials(c, 2)
                if C: keep_oT(c, 0)
                if A: add_bias(a, 1, 1)
                if C: exponentials(c, 3)
                if C: keep_oT(c, 1)
                for half in range(2):
                    if B: keep_maxima(b, half)

            steps(act, step)

        @block.vector
        def _(dve):
            def split_q(s, half):
                of = slice(2 * half, 2 * half + 2)
                dve.wait_ge(q_biased, 2 * s + half + 1)
                wait(dve, q_ready, 2 * HM * s - HM + HM * half)
                nc.vector.tensor_copy(q_rows[:, of, :], full[0][:, of, :]).then_inc(q_high, 1)
                dve.wait_ge(q_high, 2 * s + half + 1)
                low = slice(64, 128)
                nc.vector.tensor_tensor(q_rows[low, of, :], full[0][low, of, :], q_rows[low, of, :].bitcast(F32),
                                        ALU.subtract).then_inc(q_halves, 1)

            def split_k(s, p, half):
                of = slice(2 * half, 2 * half + 2)
                dve.wait_ge(k_biased, 2 * s + half + 1)
                wait(dve, b_ready, 4 * s - 6 + 2 * half)
                nc.vector.tensor_copy(k_rows[p][:, of, :], full[1][:, of, :]).then_inc(k_high, 1)
                dve.wait_ge(k_high, 2 * s + half + 1)
                for low in (slice(32, 64), slice(96, 128)):
                    last = nc.vector.tensor_tensor(k_rows[p][low, of, :], full[1][low, of, :], k_rows[p][low, of, :].bitcast(F32),
                                                   ALU.subtract)
                last.then_inc(k_halves, 1)

            def keep_v(s, p):
                dve.wait_ge(v_filled, s + 1)
                wait(dve, weighed, 4 * s - 4)
                nc.vector.tensor_tensor(v_ones[p][:, :, :, 0:HS], bank_m[0][:, 0:2 * D].rearrange("p (t h d) -> p t h d", t=2, h=H),
                                        b_v[:].rearrange("p (h d) -> p h d", h=H).unsqueeze(1).to_broadcast([P, 2, H, HS]),
                                        ALU.add).then_inc(v_ready, 1)

            def reduce(s, first, end):
                for u in range(first, end):
                    t, h = u // 2 % 2, HM * (u // 4) + 2 * (u % 2)
                    dve.wait_ge(s_ready, 16 * s + u + 1)
                    nc.vector.reduce_max(maxima[:, t, h:h + 2], bank_s[u % 2][:, :, 0:(t + 1) * P], AX.X).then_inc(max_ready, 1)

            def split_maxima(s):
                dve.wait_ge(max_ready, 16 * (s + 1))
                wait(dve, max_turned, 2 * s)
                high, low = (minus_max[:, :, :, a, :].rearrange("p t g m -> p (t g) m") for a in range(2))
                src = maxima[:].rearrange("p t (g m) -> p (t g) m", m=HM)
                nc.vector.tensor_scalar(high, src, -1.0, None, ALU.mult).then_inc(minus_high, 1)
                dve.wait_ge(minus_high, s + 1)
                nc.vector.scalar_tensor_tensor(low, src, -1.0, high, ALU.mult, ALU.subtract).then_inc(minus_ready, 1)

            def normalise(s, t):
                dve.wait_ge(back_filled, 2 * s + t + 1)
                heads = bank_m[2][:].rearrange("p (h c) -> p h c", c=32)
                nc.vector.reciprocal(inv[:], heads[:, :, HS]).then_inc(inv_ready, 1)
                dve.wait_ge(inv_ready, 2 * s + t + 1)
                nc.vector.tensor_tensor(o_tok[t][:], heads[:, :, 0:HS], inv[:].unsqueeze(2).to_broadcast([P, H, HS]),
                                        ALU.mult).then_inc(otok_ready, 1)

            def add_out(s):
                dve.wait_ge(out_filled, s + 1)
                nc.vector.tensor_tensor(with_bias[:], bank_m[2][:, 0:2 * D].rearrange("p (t d) -> p t d", t=2),
                                        b_out[:].unsqueeze(1).to_broadcast([P, 2, D]), ALU.add).then_inc(out_taken, 1)
                dve.wait_ge(out_taken, s + 1)
                at = x[:, bass.ds(2 * s, 2), :]
                nc.vector.tensor_tensor(at, at, with_bias[:], ALU.add).then_inc(x_added, 1)

            def step(t, p, stages):
                a, b, c, d = (t - i for i in range(4))
                A, B, C, D_ = (n in stages for n in "ABCD")
                q = 1 - p
                if B: reduce(b, 0, 2)
                if D_: normalise(d, 0)
                if B: reduce(b, 2, 4)
                if A: split_q(a, 0)
                if D_: normalise(d, 1)
                if B: reduce(b, 4, 7)
                if A: split_q(a, 1)
                if B: reduce(b, 7, 8)
                if D_: add_out(d)
                if B: reduce(b, 8, 11)
                if A: split_k(a, p, 0)
                if B: reduce(b, 11, 13)
                if B: keep_v(b, q)
                if B: reduce(b, 13, 16)
                if B: split_maxima(b)
                if A: split_k(a, p, 1)

            for p in range(2):
                nc.vector.memset(v_ones[p][:], 0.0)
            nc.vector.memset(max_rows[:], 0.0).then_inc(zero_set, 1)
            dve.wait_ge(zero_set, 1)
            for p in range(2):
                last = nc.vector.memset(v_ones[p][:, :, :, HS:HS + 1], 1.0)
            last.then_inc(constants_set, 1)
            dve.wait_ge(constants_set, 1)
            steps(dve, step)

        @block.gpsimd
        def _(pool):
            def member_queries(s, half):
                of = slice(2 * half, 2 * half + 2)
                pool.wait_ge(q_halves, 2 * s + half + 1)
                wait(pool, b_ready, 4 * s - 6 + 2 * half)
                for m in range(HM):
                    nc.gpsimd.tensor_scalar(q_member[s % 2][:, of, m, :], q_rows[:, of, :].bitcast(F32),
                                            const[:, C_RM + m:C_RM + m + 1], 1.0, ALU.mult, ALU.mult).then_inc(q_ready, 1)

            def keep_causal(s, g):
                for ready, block_of in ((exp_a, probs_a[g % 2][:, :, 0:P]), (exp_b, probs_b[g % 2][:])):
                    pool.wait_ge(ready, 4 * s + g + 1)
                    nc.gpsimd.affine_select(out=block_of, in_=block_of, pattern=[[0, HM], [1, P]], compare_op=ALU.is_ge,
                                            fill=0.0, base=0, channel_multiplier=-1).then_inc(probs_ready, 1)

            for t in range(BATCH + 2):
                for half in range(2):
                    if t > 1:
                        keep_causal(t - 2, 2 * half)
                        keep_causal(t - 2, 2 * half + 1)
                    if t < BATCH:
                        member_queries(t, half)
                if t < BATCH:
                    scatter(pool, 2 * t, 2 * t + 2)
            scattered_all(pool)


def attention(nc, x, xnT, const, w_q, w_k, w_v, scatter, scattered_all):
    ident = const[:, C_ID:C_ID + P]
    with ExitStack() as ctx:
        sb = lambda n, s, d=F32: ctx.enter_context(nc.sbuf_tensor(f"att1_{n}", s, d))
        pb = lambda n, s, d=F32: ctx.enter_context(nc.psum_tensor(f"att1_{n}", s, d))
        sem = lambda n: ctx.enter_context(nc.semaphore(f"att1_{n}"))
        xT = [sb(f"xT{i}", [P, SEQ]) for i in range(2)]
        qT, kT = sb("qT", [P, SEQ]), sb("kT", [P, SEQ])
        v = [sb(f"v{i}", [P, 2, D]) for i in range(2)]
        top = sb("top", [P, 2])
        minus_top = [sb(f"minus_top{i}", [P, 2]) for i in range(2)]
        total = [sb(f"total{i}", [P, 2]) for i in range(2)]
        inv = sb("inv", [P, 2])
        probs = [sb(f"probs{i}", [P, 2, SEQ]) for i in range(2)]
        probsT = sb("probsT", [P, 2, 2, P])
        qk_ps, v_ps, turned, o_ps = pb("qk_ps", [P, 2, SEQ]), pb("v_ps", [P, 2, D]), pb("turned", [P, 2, 2, P]), pb("o_ps", [P, 2, D])
        s_ps = [pb(f"s_ps{i}", [P, 2, SEQ]) for i in range(2)]
        xT_in = [sem(f"xT_in{i}") for i in range(2)]
        names = ("qk_ready", "qk_taken", "v_ready", "v_taken", "s_ready", "top_ready", "minus_ready", "probs_ready",
                 "turned_ready", "probsT_ready", "o_ready", "inv_ready", "x_added")
        (qk_ready, qk_taken, v_ready, v_taken, s_ready, top_ready, minus_ready, probs_ready,
         turned_ready, probsT_ready, o_ready, inv_ready, x_added) = (sem(n) for n in names)
        block = ctx.enter_context(nc.Block())

        def wait(eng, semaphore, value):
            if not isinstance(value, int) or value > 0:
                eng.wait_ge(semaphore, value)

        def steps(eng, new, old, both):
            new(0, 0)
            both(1, 1)
            with eng.Fori(0, BATCH // 2 - 1) as r:
                both(2 * r + 2, 0)
                both(2 * r + 3, 1)
            old(BATCH - 1, 1)

        @block.tensor
        def _(pe):
            def project(s, p):
                pe.wait_ge(xT_in[p], 8 * (s - p) + 16)
                wait(pe, qk_taken, 2 * s)
                for which, w in enumerate((w_q, w_k)):
                    last = nc.tensor.matmul(qk_ps[:, which, :], w[:], xT[p][:], start=(which == 0), stop=(which == 1),
                                            skip_group_check=True)
                last.then_inc(qk_ready, 1)

            def project_v(s, p):
                wait(pe, v_taken, s)
                for t in range(2):
                    last = nc.tensor.matmul(v_ps[:, t, :], xT[p][:, t * P:(t + 1) * P], w_v[:], start=(t == 0), stop=(t == 1),
                                            skip_group_check=True)
                last.then_inc(v_ready, 1)

            def scores(s, p):
                pe.wait_ge(qk_taken, 2 * s + 2)
                wait(pe, probs_ready, 2 * s - 2)
                for t in range(2):
                    last = nc.tensor.matmul(s_ps[p][:, t, :], qT[:, t * P:(t + 1) * P], kT[:], start=(t == 0), stop=(t == 1),
                                            skip_group_check=True)
                last.then_inc(s_ready, 1)

            def turn(s, p):
                pe.wait_ge(probs_ready, 2 * s + 2)
                wait(pe, probsT_ready, s)
                for k in range(2):
                    for t in range(2):
                        last = nc.tensor.transpose(turned[:, k, t, :], probs[p][:, t, k * P:(k + 1) * P], ident)
                last.then_inc(turned_ready, 1)

            def weigh(s, p):
                pe.wait_ge(probsT_ready, s + 1)
                pe.wait_ge(v_taken, s + 1)
                wait(pe, x_added, s)
                for t in range(2):
                    for k in range(2):
                        last = nc.tensor.matmul(o_ps[:, t, :], probsT[:, k, t, :], v[p][:, k, :], start=(k == 0), stop=(k == 1))
                last.then_inc(o_ready, 1)

            def new(s, p):
                project(s, p)
                project_v(s, p)
                scores(s, p)

            def old(s, p):
                turn(s, p)
                weigh(s, p)

            def both(s, p):
                project(s, p)
                turn(s - 1, 1 - p)
                project_v(s, p)
                scores(s, p)
                weigh(s - 1, 1 - p)

            steps(pe, new, old, both)

        @block.sync
        def _(sp):
            def load(s, p):
                wait(sp, v_ready, s - 1)
                sp.dma_start(xT[p][:], xnT[:, bass.ds(s * SEQ, SEQ)]).then_inc(xT_in[p], 16)

            for s in range(2):
                load(s, s)
            with sp.Fori(0, BATCH // 2 - 1) as r:
                for p in range(2):
                    load(2 * r + (2 + p), p)
            for p in range(2):
                sp.wait_ge(xT_in[p], 8 * BATCH)

        @block.scalar
        def _(act):
            def take_qk(s):
                act.wait_ge(qk_ready, s + 1)
                wait(act, s_ready, s)
                nc.scalar.activation(qT[:], qk_ps[:, 0, :], ACT.Copy, scale=D ** -0.5).then_inc(qk_taken, 1)
                nc.scalar.activation(kT[:], qk_ps[:, 1, :], ACT.Copy).then_inc(qk_taken, 1)

            def exponentials(s, p):
                act.wait_ge(minus_ready, s + 1)
                wait(act, turned_ready, s - 1)
                wait(act, x_added, s - 1)
                for t in range(2):
                    nc.scalar.activation(probs[p][:, t, :], s_ps[p][:, t, :], ACT.Exp, bias=minus_top[p][:, t:t + 1],
                                         accum_out=total[p][:, t:t + 1]).then_inc(probs_ready, 1)

            def take_turned(s):
                act.wait_ge(turned_ready, s + 1)
                wait(act, o_ready, s)
                nc.scalar.activation(probsT[:], turned[:], ACT.Copy).then_inc(probsT_ready, 1)

            def new(s, p):
                take_qk(s)
                exponentials(s, p)

            def old(s, p):
                take_turned(s)

            def both(s, p):
                take_qk(s)
                take_turned(s - 1)
                exponentials(s, p)

            steps(act, new, old, both)

        @block.vector
        def _(dve):
            def take_v(s, p):
                dve.wait_ge(v_ready, s + 1)
                wait(dve, o_ready, s - 1)
                nc.vector.tensor_copy(v[p][:], v_ps[:]).then_inc(v_taken, 1)

            def maxima(s, p):
                dve.wait_ge(s_ready, s + 1)
                nc.vector.reduce_max(top[:], s_ps[p][:], AX.X).then_inc(top_ready, 1)
                dve.wait_ge(top_ready, s + 1)
                wait(dve, probs_ready, 2 * s - 2)
                nc.vector.tensor_scalar(minus_top[p][:], top[:], -1.0, None, ALU.mult).then_inc(minus_ready, 1)

            def add_out(s, p):
                dve.wait_ge(probs_ready, 2 * s + 2)
                wait(dve, x_added, s)
                nc.vector.reciprocal(inv[:], total[p][:]).then_inc(inv_ready, 1)
                dve.wait_ge(inv_ready, s + 1)
                dve.wait_ge(o_ready, s + 1)
                for t in range(2):
                    at = x[:, bass.ds(2 * s + t, 1), :].squeeze(1)
                    last = nc.vector.scalar_tensor_tensor(at, o_ps[:, t, :], inv[:, t:t + 1], at, ALU.mult, ALU.add)
                last.then_inc(x_added, 1)

            def new(s, p):
                take_v(s, p)
                maxima(s, p)

            def old(s, p):
                add_out(s, p)

            def both(s, p):
                take_v(s, p)
                maxima(s, p)
                add_out(s - 1, 1 - p)

            steps(dve, new, old, both)

        @block.gpsimd
        def _(pool):
            scatter(pool, 0, TILES)
            scattered_all(pool)


def program(nc, x_in, constants, gate0, gate1, att0, att1, packs0, packs1, out):
    rows_in, rows_out = (nc.dram_tensor(n, [rows, D], F32, kind="Internal").ap() for n, rows in (("rows_in", ROWS), ("rows_out", FT * NT0)))
    with ExitStack() as ctx:
        def sb(name, shape, dt=F32):
            return ctx.enter_context(nc.sbuf_tensor(name, shape, dt))

        x, xn, xnT = sb("x", [P, TILES, D]), sb("xn", [P, TILES, D]), sb("xnT", [P, TOKENS])
        const = sb("const", [P, C_ALL])
        const_bf = sb("const_bf", [P, C_REV], BF16)
        gates = [sb("gate0", [P, E0]), sb("gate1", [P, E1])]
        routing = [Routing(ctx, nc, f"routing{l}", e, n) for l, (e, n) in enumerate(((E0, NT0), (E1, NT1)))]
        const_in, const_bf_set, zero_set, rows_zeroed = (
            ctx.enter_context(nc.semaphore(n)) for n in ("const_in", "const_bf_set", "zero_set", "rows_zeroed"))
        att_in, scattered = ([ctx.enter_context(nc.semaphore(f"{n}{l}")) for l in range(2)] for n in ("att_in", "scattered"))
        scatters = [scatter_of(nc, xn, rows_in, routing[l], scattered[l]) for l in range(2)]
        const_loaded = (const_in, 16 * 3)

        with nc.Block() as block:
            @block.sync
            def _(sp):
                for dst, src in ((const[:], constants), (gates[0][:], gate0), (gates[1][:], gate1)):
                    sp.dma_start(dst, src).then_inc(const_in, 16)

        def load_weights(pool, layer, parts, arrays):
            for dst, src in zip(parts, arrays):
                pool.dma_start(dst[:], src).then_inc(att_in[layer], 16)
            pool.wait_ge(att_in[layer], 16 * len(arrays))

        with ExitStack() as layer:
            parts = [layer.enter_context(nc.sbuf_tensor(f"att0_w{i}", list(a.shape), F32)) for i, a in enumerate(att0)]
            with nc.sbuf_tensor("zero", [P, ZEROED], F32) as zero:
                def prepare(pool, groups_ready, all_groups):
                    nc.gpsimd.memset(zero[:], 0.0).then_inc(zero_set, 1)
                    pool.wait_ge(*const_loaded)
                    nc.gpsimd.tensor_copy(const_bf[:], const[:, 0:C_REV]).then_inc(const_bf_set, 1)
                    load_weights(pool, 0, parts, att0)
                    pool.wait_ge(zero_set, 1)
                    pool.wait_ge(groups_ready, all_groups)
                    for r in range(0, ROWS, ZEROED):
                        pool.dma_start(rows_in[r:r + ZEROED, :].rearrange("(p t) d -> p (t d)", p=P), zero[:]).then_inc(rows_zeroed, 16)
                    pool.wait_ge(rows_zeroed, 16 * (ROWS // ZEROED))

                norm_and_route(nc, "route0", x, xn, xnT, const, const_bf, gates[0], routing[0], False, prepare, x_in=x_in,
                               const_loaded=const_loaded, const_bf_set=const_bf_set)
            causal_attention(nc, x, xnT, const, const_bf, *parts, *scatters[0])
        expert_tiles(nc, "experts0", NT0, const, packs0, False, True, rows_in, rows_out, routing[0])
        with ExitStack() as layer:
            parts = [layer.enter_context(nc.sbuf_tensor(f"att1_w{i}", list(a.shape), F32)) for i, a in enumerate(att1)]
            norm_and_route(nc, "route1", x, xn, xnT, const, const_bf, gates[1], routing[1], True,
                           lambda pool, *_: load_weights(pool, 1, parts, att1), results=(rows_out, routing[0]))
            attention(nc, x, xnT, const, *parts, *scatters[1])
        expert_tiles(nc, "experts1", NT1, const, packs1[0:E1], True, True, rows_in, rows_out, routing[1])
        expert_tiles(nc, "shared", TOKENS // FT, const, packs1[E1:E1 + 1], True, False, None, rows_out, routing[1],
                     x=x, xnT=xnT, out=out)


def kernel(L0_attn_encodings, L0_attn_attn_W, L0_attn_attn_b, L0_attn_out_W, L0_attn_out_b, L0_ffn_Wg, L0_ffn_W1, L0_ffn_b1,
           L0_ffn_W2, L0_ffn_b2, L1_attn_W_qkv, L1_ffn_shared_up, L1_ffn_shared_gate, L1_ffn_shared_down, L1_ffn_routed_up,
           L1_ffn_routed_gate, L1_ffn_routed_down, L1_ffn_router_w):
    import concourse.bacc as bacc
    from concourse.bass_utils import run_bass_kernel_spmd

    host = np.asarray

    def down_rows(w):
        return w.transpose(0, 2, 1).reshape(-1, CH, P, D).transpose(0, 2, 1, 3).reshape(-1, P, CH * D)

    w = host(L0_attn_attn_W).reshape(D, HG, HM, 3, HS)
    b = host(L0_attn_attn_b).reshape(HG, HM, 3, HS)
    rows = lambda k: np.broadcast_to(w[:, :, None, :, k], (D, HG, 4, HM, HS)).reshape(D, HG * P)
    bias = lambda k: np.broadcast_to(b[:, None, :, k], (HG, 4, HM, HS)).reshape(HG, P).T
    everywhere = lambda a: np.broadcast_to(a.reshape(1, -1), (P, a.size))
    att0 = [rows(0), rows(1), w[:, :, :, 2].reshape(D, D), np.concatenate([bias(0), bias(1)], 1), everywhere(b[:, :, 2]),
            host(L0_attn_out_W), everywhere(host(L0_attn_out_b))]
    w1 = host(L1_attn_W_qkv)
    att1 = [w1[i * D:(i + 1) * D].T for i in range(3)]
    E = E0
    packs0 = np.concatenate([host(L0_ffn_W1).transpose(0, 2, 1), down_rows(host(L0_ffn_W2)),
                             host(L0_ffn_b1).reshape(E, CH, P).transpose(0, 2, 1),
                             np.broadcast_to(host(L0_ffn_b2)[:, None], (E, P, D))], 2)
    experts = lambda routed, shared: np.concatenate([host(routed), host(shared)[None]])
    packs1 = np.concatenate([experts(L1_ffn_routed_gate, L1_ffn_shared_gate).transpose(0, 2, 1),
                             experts(L1_ffn_routed_up, L1_ffn_shared_up).transpose(0, 2, 1),
                             down_rows(experts(L1_ffn_routed_down, L1_ffn_shared_down))], 2)
    arrays = {"x": host(L0_attn_encodings).reshape(TOKENS, D), "constants": shape_constants(), "gate0": host(L0_ffn_Wg).T,
              "gate1": host(L1_ffn_router_w).T, "packs0": packs0, "packs1": packs1}
    arrays |= {f"att0_{i}": a for i, a in enumerate(att0)} | {f"att1_{i}": a for i, a in enumerate(att1)}
    arrays = {n: np.ascontiguousarray(a) for n, a in arrays.items()}

    nc = bacc.Bacc("TRN2", target_bir_lowering=False, num_devices=1)
    ap = {n: nc.dram_tensor(f"in_{n}", a.shape, mybir.dt.from_np(a.dtype), kind="ExternalInput").ap() for n, a in arrays.items()}
    out = nc.dram_tensor("out", [TOKENS, D], F32, kind="ExternalOutput").ap()
    program(nc, ap["x"], ap["constants"], ap["gate0"], ap["gate1"], [ap[f"att0_{i}"] for i in range(len(att0))],
            [ap[f"att1_{i}"] for i in range(len(att1))], ap["packs0"], ap["packs1"], out)
    ran = run_bass_kernel_spmd(nc, [{f"in_{n}": a for n, a in arrays.items()}], core_ids=[0])
    return ran.results[0]["out"].reshape(BATCH, SEQ, D)
```

```python
from contextlib import ExitStack

import numpy as np
import concourse.bass as bass
from concourse import mybir
from concourse.alu_op_type import AluOpType as ALU

F32 = mybir.dt.float32
F32R = mybir.dt.float32r
BF16 = mybir.dt.bfloat16
I32 = mybir.dt.int32
ACT = mybir.ActivationFunctionType
AX = mybir.AxisListType

P = 128
D = 128
BATCH, SEQ = 32, 256
TOKENS = BATCH * SEQ
TILES = TOKENS // P
H, HS = 16, D // 16
HG, HM = 4, 4
MAX_ROW = 96
HID = 512
CH = HID // P
E0, E1 = 8, 7
TOP = 2
FT = 256
NT0, NT1 = ((TOP * TOKENS + e * (FT - 1)) // FT for e in (E0, E1))
ROWS = FT * (NT0 + 1)
ZEROED = 16 * P
NEG = -1.0e30
EPS = 1e-5

C_ID, C_TRI, C_ONE, C_MB, C_RM, C_REV, C_TB = 0, 128, 256, 384, 512, 520, 528
C_ALL = C_TB + NT0


def shape_constants():
    p = np.arange(P)
    c = np.zeros((P, C_ALL), np.float32)
    c[:, C_ID:C_ID + P] = np.eye(P)
    c[:, C_TRI:C_TRI + P] = np.where(p[:, None] < p[None, :], 0.0, -1.0)
    c[:, C_ONE:C_ONE + P] = 1.0
    c[:, C_MB:C_MB + P] = np.where(p[None, :] > p[:, None], NEG, 0.0)
    c[:, C_RM:C_RM + HM] = np.where(p[:, None] < MAX_ROW, p[:, None] % 32 // HS, (p[:, None] - MAX_ROW) % HM) == np.arange(HM)[None]
    c[:, C_RM + HM] = (p >= MAX_ROW) & (p < MAX_ROW + 2 * HM)
    c[:, C_REV:C_REV + 8] = 8 - np.arange(8)
    c[:, C_TB:C_TB + NT0] = FT * np.arange(NT0)
    return c


def half_selectors():
    sel = np.zeros((P, 2, 2, HG, P), np.float32)
    for which, low_part in enumerate((2, 1)):
        for part in range(3):
            for g in range(HG):
                for n in range(HM * HS):
                    sel[HM * HS * g + n, which, int(part == low_part), g, 32 * part + n] = 1.0
    return sel.reshape(P, -1)




class Routing:

    def __init__(self, ctx, nc, name, experts, tiles):
        sb = lambda n, s, d=F32: ctx.enter_context(nc.sbuf_tensor(f"{name}_{n}", s, d))
        sem = lambda n: ctx.enter_context(nc.semaphore(f"{name}_{n}"))
        self.experts, self.tiles = experts, tiles
        self.weight = [sb(f"weight{k}", [P, TILES], F32) for k in range(TOP)]
        self.slot = [sb(f"slot{k}", [P, TILES], I32) for k in range(TOP)]
        self.expert_of_tile = sb("expert_of_tile", [1, tiles], I32)
        self.logits = sb("logits", [P, TILES, experts])
        self.top1, self.top2, self.t1, self.t2, self.t3 = (sb(n, [P, TILES]) for n in ("top1", "top2", "t1", "t2", "t3"))
        self.ends = sb("ends", [P, experts])
        self.passed, self.expert_f = sb("passed", [1, tiles, experts]), sb("expert_f", [1, tiles])
        self.finish_step, self.exp_ready = sem("finish_step"), sem("exp_ready")

    def finish_exp(self, nc, act, gated_softmax):
        act.wait_ge(self.finish_step, 2)
        if gated_softmax:
            nc.scalar.activation(self.logits[:], self.logits[:], ACT.Exp)
        nc.scalar.activation(self.t1[:], self.t1[:], ACT.Exp).then_inc(self.exp_ready, 1)

    def finish(self, nc, dve, const, gated_softmax):
        E, n, t1, t2, t3 = self.experts, self.tiles, self.t1, self.t2, self.t3
        done = [0]

        def chained(ins):
            done[0] += 1
            ins.then_inc(self.finish_step, 1)
            dve.wait_ge(self.finish_step, done[0])

        chained(nc.vector.tensor_tensor(self.logits[:], self.logits[:], self.top1[:].unsqueeze(2).to_broadcast([P, TILES, E]),
                                        ALU.subtract))
        chained(nc.vector.tensor_tensor(t1[:], self.top2[:], self.top1[:], ALU.subtract))
        chained(nc.vector.tensor_tensor(
            self.passed[:], const[0:1, C_TB:C_TB + n].unsqueeze(2).to_broadcast([1, n, E]),
            self.ends[0:1, :].unsqueeze(1).to_broadcast([1, n, E]), ALU.is_ge))
        chained(nc.vector.reduce_sum(self.expert_f[:], self.passed[:], AX.X))
        chained(nc.vector.tensor_scalar(self.expert_f[:], self.expert_f[:], float(E - 1), None, ALU.min))
        nc.vector.tensor_copy(self.expert_of_tile[:], self.expert_f[:])
        dve.wait_ge(self.exp_ready, 1)
        if gated_softmax:
            chained(nc.vector.reduce_sum(t2[:], self.logits[:], AX.X))
            chained(nc.vector.reciprocal(t2[:], t2[:]))
            chained(nc.vector.tensor_tensor(t1[:], t1[:], t2[:], ALU.mult))
            chained(nc.vector.tensor_tensor(t3[:], t2[:], t1[:], ALU.add))
            chained(nc.vector.tensor_scalar(t3[:], t3[:], 1e-9, None, ALU.add))
            chained(nc.vector.reciprocal(t3[:], t3[:]))
            nc.vector.tensor_tensor(self.weight[0][:], t2[:], t3[:], ALU.mult)
            nc.vector.tensor_tensor(self.weight[1][:], t1[:], t3[:], ALU.mult)
        else:
            chained(nc.vector.tensor_scalar(t2[:], t1[:], 1.0, None, ALU.add))
            chained(nc.vector.reciprocal(self.weight[0][:], t2[:]))
            nc.vector.tensor_tensor(self.weight[1][:], t1[:], self.weight[0][:], ALU.mult)


def weighted_add(nc, x, tile, got, weight):
    at = x[:, bass.ds(tile, 1), :].squeeze(1)
    return nc.vector.scalar_tensor_tensor(at, got, weight[:, bass.ds(tile, 1)], at, ALU.mult, ALU.add)


def norm_and_route(nc, layer, x, xn, xnT, const, const_bf, gateT, routing, size, background,
                   x_in=None, const_loaded=None, const_bf_set=None, results=None):
    E = routing.experts
    groups = TILES // size
    ident = const[:, C_ID:C_ID + P]
    with ExitStack() as ctx:
        sb = lambda n, s, d=F32: ctx.enter_context(nc.sbuf_tensor(f"{layer}_{n}", s, d))
        pb = lambda n, s, d=F32: ctx.enter_context(nc.psum_tensor(f"{layer}_{n}", s, d))
        sem = lambda n: ctx.enter_context(nc.semaphore(f"{layer}_{n}"))
        stats = [sb(f"stats{i}", [P, size, 6]) for i in range(2)]
        dmean, mean, var, root, rstd, shift, newton = (
            [sb(f"{n}{i}", [P, size]) for i in range(2)] for n in ("dmean", "mean", "var", "root", "rstd", "shift", "newton"))
        logits, top1, top2, ends = routing.logits, routing.top1, routing.top2, routing.ends
        score, hot1, hot2, base = (sb(n, [P, TILES, E]) for n in ("score", "hot1", "hot2", "base"))
        hits = sb("hits", [P, TILES, E], BF16)
        first = sb("first", [P, TILES])
        upto = sb("upto", [P, TILES, E])
        padded_i = sb("padded_i", [P, E], I32)
        padded, starts = (sb(n, [P, E]) for n in ("padded", "starts"))
        xn_now = [sb(f"xn_now{i}", [P, size, P]) for i in range(2)]
        xnT_now = [sb(f"xnT_now{i}", [P, size * P]) for i in range(2)]
        got = [[[sb(f"got{i}_{t}_{k}", [P, D]) for k in range(TOP)] for t in range(size)] for i in range(2)] if results else None
        xn_kept = [sem(f"xn_kept{i}") for i in range(2)]
        xnT_kept = [sem(f"xnT_kept{i}") for i in range(2)]
        group_in = [sem(f"group_in{i}") for i in range(2)]
        turned = [pb(f"turned{i}", [P, size * P]) for i in range(2)]
        logit_ps = [pb(f"logit_ps{i}", [P, size, E]) for i in range(2)]
        missing = pb("missing", [P, TILES * E])
        in_tile = pb("in_tile", [P, TILES * E])
        half_added, added = (sem(n) if results else None for n in ("half_added", "added"))
        moments_ready, stats_ready, xn_ready, turned_ready, xnT_ready = (
            sem(n) for n in ("moments_ready", "stats_ready", "xn_ready", "turned_ready", "xnT_ready"))
        logit_ready, logit_read, hits_ready, counts_ready = (sem(n) for n in ("logit_ready", "logit_read", "hits_ready", "counts_ready"))
        chain, var_ready, root_ready = (sem(n) for n in ("chain", "var_ready", "root_ready"))
        block = ctx.enter_context(nc.Block())

        def wait(eng, semaphore, value):
            if not isinstance(value, int) or value > 0:
                eng.wait_ge(semaphore, value)

        def steps(eng, step):
            for g in range(4):
                step(g, g % 2, g // 2, range(g + 1))
            with eng.Fori(0, (groups - 4) // 2) as r:
                for i in range(2):
                    step(2 * r + (4 + i), i, r + 2, range(4))
            for g in range(groups, groups + 3):
                step(g, g % 2, g // 2, range(g - groups + 1, 4))

        @block.vector
        def _(dve):
            done = [0]

            def chained(ins):
                done[0] += 1
                ins.then_inc(chain, 1)
                dve.wait_ge(chain, done[0])

            def take_group(g, i, turn):
                if results is None:
                    dve.wait_ge(group_in[i], 16 * turn + 16)
                    return
                dve.wait_ge(group_in[i], 16 * TOP * size * turn + 16 * TOP * size)
                for k, after in enumerate((half_added, added)):
                    if k:
                        dve.wait_ge(half_added, g + 1)
                    for t in range(size):
                        last = weighted_add(nc, x, size * g + t, got[i][t][k][:], results[1].weight[k])
                    last.then_inc(after, 1)
                dve.wait_ge(added, g + 1)

            def moments(g, i):
                for t in range(size):
                    last = nc.vector.bn_stats(stats[i][:, t, :], x[:, bass.ds(size * g + t, 1), :].squeeze(1))
                last.then_inc(moments_ready, 1)
                dve.wait_ge(moments_ready, 5 * g + 1)
                m_even, q_even, m_odd, q_odd = (stats[i][:, :, n] for n in (1, 2, 4, 5))
                nc.vector.tensor_tensor(mean[i][:], m_even, m_odd, ALU.add)
                nc.vector.tensor_tensor(dmean[i][:], m_even, m_odd, ALU.subtract).then_inc(moments_ready, 1)
                nc.vector.tensor_tensor(var[i][:], q_even, q_odd, ALU.add).then_inc(moments_ready, 1)
                dve.wait_ge(moments_ready, 5 * g + 3)
                nc.vector.tensor_tensor(dmean[i][:], dmean[i][:], dmean[i][:], ALU.mult).then_inc(moments_ready, 1)
                nc.vector.tensor_scalar(var[i][:], var[i][:], 1.0 / D, EPS, ALU.mult, ALU.add).then_inc(moments_ready, 1)
                dve.wait_ge(moments_ready, 5 * g + 5)
                nc.vector.scalar_tensor_tensor(var[i][:], dmean[i][:], 0.25, var[i][:], ALU.mult, ALU.add).then_inc(var_ready, 1)

            def inverse_root(g, i):
                dve.wait_ge(root_ready, g + 1)
                ops = (lambda: nc.vector.reciprocal(rstd[i][:], root[i][:]),
                       lambda: nc.vector.tensor_tensor(newton[i][:], rstd[i][:], rstd[i][:], ALU.mult),
                       lambda: nc.vector.tensor_tensor(newton[i][:], newton[i][:], var[i][:], ALU.mult),
                       lambda: nc.vector.tensor_scalar(newton[i][:], newton[i][:], -0.5, 1.5, ALU.mult, ALU.add),
                       lambda: nc.vector.tensor_tensor(rstd[i][:], rstd[i][:], newton[i][:], ALU.mult),
                       lambda: nc.vector.scalar_tensor_tensor(shift[i][:], mean[i][:], -0.5, rstd[i][:], ALU.mult, ALU.mult))
                for n, op in enumerate(ops):
                    op().then_inc(stats_ready, 1)
                    if n + 1 < len(ops):
                        dve.wait_ge(stats_ready, 6 * g + n + 1)

            def step(g, i, turn, stages):
                if 0 in stages:
                    take_group(g, i, turn)
                if 1 in stages:
                    inverse_root(g - 1, 1 - i)
                if 0 in stages:
                    moments(g, i)
                if 3 in stages:
                    dve.wait_ge(logit_ready, g - 2)
                    nc.vector.tensor_copy(logits[:, bass.ds(size * (g - 3), size), :], logit_ps[1 - i][:]).then_inc(logit_read, 1)

            steps(dve, step)
            if const_loaded is not None:
                dve.wait_ge(*const_loaded)
            dve.wait_ge(logit_read, groups)

            wide = lambda a: a[:].unsqueeze(2).to_broadcast([P, TILES, E])
            rev = const[:, C_REV:C_REV + E].unsqueeze(1).to_broadcast([P, TILES, E])
            for top, hot in ((top1, hot1), (top2, hot2)):
                src = logits if hot is hot1 else base
                chained(nc.vector.reduce_max(top[:], src[:], AX.X))
                chained(nc.vector.tensor_tensor(score[:], src[:], wide(top), ALU.is_ge))
                chained(nc.vector.tensor_tensor(score[:], score[:], rev, ALU.mult))
                chained(nc.vector.reduce_max(first[:], score[:], AX.X))
                chained(nc.vector.tensor_tensor(hot[:], score[:], wide(first), ALU.is_equal))
                if hot is hot1:
                    chained(nc.vector.scalar_tensor_tensor(base[:], hot1[:], -3.0e38, logits[:], ALU.mult, ALU.add))
            nc.vector.tensor_tensor(hits[:], hot1[:], hot2[:], ALU.add).then_inc(hits_ready, 1)

            dve.wait_ge(counts_ready, 1)
            here = in_tile[:].rearrange("p (t e) -> p t e", e=E)
            before = missing[:].rearrange("p (t e) -> p t e", e=E)
            ones = const[:, C_ONE:C_ONE + TILES]
            for e in range(E):
                last = nc.vector.tensor_tensor_scan(upto[:, :, e], ones, here[:, :, e], 0.0, ALU.mult, ALU.add)
            chained(last)
            chained(nc.vector.tensor_scalar(padded_i[:], upto[:, TILES - 1, :], float(FT - 1), None, ALU.add))
            chained(nc.vector.tensor_scalar(padded_i[:], padded_i[:], FT.bit_length() - 1, FT.bit_length() - 1,
                                            ALU.arith_shift_right, ALU.arith_shift_left))
            chained(nc.vector.tensor_copy(padded[:], padded_i[:]))
            chained(nc.vector.tensor_tensor_scan(ends[:], const[:, C_ONE:C_ONE + E], padded[:], 0.0, ALU.mult, ALU.add))
            chained(nc.vector.tensor_tensor(starts[:], ends[:], padded[:], ALU.subtract))
            chained(nc.vector.tensor_tensor(upto[:], upto[:], before, ALU.add))
            chained(nc.vector.tensor_tensor(base[:], upto[:], starts[:].unsqueeze(1).to_broadcast([P, TILES, E]), ALU.add))
            for k, hot in enumerate((hot1, hot2)):
                chained(nc.vector.tensor_tensor(score[:], base[:], hot[:], ALU.mult))
                chained(nc.vector.reduce_sum(first[:], score[:], AX.X))
                chained(nc.vector.tensor_copy(routing.slot[k][:], first[:]))

        @block.sync
        def _(sp):
            def step(g, i, turn, stages):
                if 1 in stages:
                    sp.wait_ge(xn_ready, g)
                    sp.dma_start(xn[:, bass.ds(size * (g - 1), size), :], xn_now[1 - i][:]).then_inc(xn_kept[1 - i], 16)
                if 2 in stages:
                    sp.wait_ge(xnT_ready, g - 1)
                    sp.dma_start(xnT[:, bass.ds(size * P * (g - 2), size * P)], xnT_now[i][:]).then_inc(xnT_kept[i], 16)

            steps(sp, step)
            for i in range(2):
                sp.wait_ge(xn_kept[i], 16 * (groups // 2))
                sp.wait_ge(xnT_kept[i], 16 * (groups // 2))

        @block.gpsimd
        def _(pool):
            def load_group(turn, i):
                wait(pool, group_in[i], 16 * turn)
                g = 2 * turn + i
                pool.dma_start(x[:, bass.ds(size * g, size), :],
                               x_in[bass.ds(size * P * g, size * P), :].rearrange("(t p) d -> p t d", p=P)).then_inc(group_in[i], 16)

            if results is None:
                for i in range(2):
                    load_group(0, i)
                with pool.Fori(1, groups // 2) as turn:
                    for i in range(2):
                        load_group(turn, i)
            else:
                for t in range(TILES):
                    g, i = t // size, t // size % 2
                    if g > 1 and t % size == 0:
                        pool.wait_ge(added, g - 1)
                    for k in range(TOP):
                        at = bass.IndirectOffsetOnAxis(ap=results[1].slot[k][:, t:t + 1], axis=0)
                        nc.gpsimd.indirect_dma_start(got[i][t % size][k][:], None, results[0], at).then_inc(group_in[i], 16)
            background(pool, xnT_ready, groups)

        @block.scalar
        def _(act):
            def normalise(g, i, turn):
                act.wait_ge(stats_ready, 6 * g + 6)
                wait(act, turned_ready, g - 1)
                wait(act, xn_kept[i], 16 * turn)
                for t in range(size):
                    last = nc.scalar.activation(xn_now[i][:, t:t + 1, :], x[:, bass.ds(size * g + t, 1), :], ACT.Identity,
                                                bias=shift[i][:, t:t + 1], scale=rstd[i][:, t:t + 1])
                last.then_inc(xn_ready, 1)

            def take_turned(g, i, turn):
                act.wait_ge(turned_ready, g + 1)
                wait(act, logit_ready, g - 1)
                wait(act, xnT_kept[i], 16 * turn)
                nc.scalar.activation(xnT_now[i][:], turned[i][:], ACT.Copy).then_inc(xnT_ready, 1)

            def step(g, i, turn, stages):
                if 1 in stages:
                    normalise(g - 1, 1 - i, turn - 1 + i)
                if 0 in stages:
                    act.wait_ge(var_ready, g + 1)
                    wait(act, stats_ready, 6 * (g - 1))
                    nc.scalar.activation(root[i][:], var[i][:], ACT.Sqrt).then_inc(root_ready, 1)
                if 2 in stages:
                    take_turned(g - 2, i, turn - 1)

            steps(act, step)

        @block.tensor
        def _(pe):
            def turn_group(g, i):
                pe.wait_ge(xn_ready, g + 1)
                wait(pe, xnT_ready, g - 1)
                for t in range(size):
                    last = nc.tensor.transpose(turned[i][:, t * P:(t + 1) * P], xn_now[i][:, t, :], ident)
                last.then_inc(turned_ready, 1)

            def score_experts(g, i):
                pe.wait_ge(xnT_ready, g + 1)
                wait(pe, logit_read, g - 1)
                for t in range(size):
                    last = nc.tensor.matmul(logit_ps[i][:, t, :], xnT_now[i][:, t * P:(t + 1) * P], gateT[:, 0:E],
                                            start=(t == 0), stop=(t == size - 1), skip_group_check=True)
                last.then_inc(logit_ready, 1)

            def step(g, i, turn, stages):
                if 1 in stages:
                    turn_group(g - 1, 1 - i)
                if 2 in stages:
                    score_experts(g - 2, i)

            if const_loaded is not None:
                pe.wait_ge(*const_loaded)
            steps(pe, step)
            if const_bf_set is not None:
                pe.wait_ge(const_bf_set, 1)
            pe.wait_ge(hits_ready, 1)
            flat = hits[:].rearrange("p t e -> p (t e)")
            nc.tensor.matmul(missing[:], const_bf[:, C_TRI:C_TRI + P], flat, start=True, stop=True)
            nc.tensor.matmul(in_tile[:], const_bf[:, C_ONE:C_ONE + P], flat, start=True, stop=True).then_inc(counts_ready, 1)


START = 16
UNROLL = 6
NY = 3


class Tile:

    def __init__(self, turn, place):
        self.turn, self.place = turn + place // UNROLL, place % UNROLL

    @property
    def i(self):
        return UNROLL * self.turn + self.place

    def back(self, n):
        return Tile(self.turn, self.place - n)

    def loaded(self):
        return START + 32 * self.turn + 32

    def gathered(self):
        return 16 * TOP * (FT // P) * (self.turn + 1)

    def stored(self):
        return START + 16 * (UNROLL // NY) * self.turn + 16 * (self.place // NY + 1)


def over_tiles(eng, first, end, body):
    turns = (end - first) // UNROLL
    if turns > 1:
        with eng.Fori(0, turns) as r:
            for u in range(UNROLL):
                body(Tile(r, first + u))
        first += turns * UNROLL
    for i in range(first, end):
        body(Tile(0, i))


def pack_cols(gated):
    return 3 * HID if gated else 2 * HID + CH + D


def expert_tiles(nc, layer, tiles, const, packs, gated, routed, rows_in, rows_out, routing, x=None, xnT=None, out=None):
    ident = const[:, C_ID:C_ID + P]
    W = pack_cols(gated)
    S = FT // P
    with ExitStack() as ctx:
        sb = lambda n, s, d=F32: ctx.enter_context(nc.sbuf_tensor(f"{layer}_{n}", s, d))
        pb = lambda n, s, d=F32: ctx.enter_context(nc.psum_tensor(f"{layer}_{n}", s, d))
        sem = lambda n: ctx.enter_context(nc.semaphore(f"{layer}_{n}"))
        pack = [sb(f"pack{i}", [P, W]) for i in range(UNROLL if routed else 1)]
        tok = [sb(f"tok{i}", [P, S, D]) for i in range(UNROLL)] if routed else None
        UP = (2 if gated else 1) * HID
        w_high, w_low = ([sb(f"{n}{i}", [P, UP], F32R) for i in range(2 if routed else 1)] for n in ("w_high", "w_low"))
        x_high, x_low = ([sb(f"{n}{i}", [P, FT], F32R) for i in range(2)] for n in ("x_high", "x_low"))
        hT = [sb(f"hT{i}", [P, CH, FT]) for i in range(2)]
        y = [sb(f"y{i}", [P, S, D]) for i in range(NY)]
        turned = pb("turned", [P, FT])
        silu = [sb(f"silu{i}", [P, 2, FT]) for i in range(2)] if gated else None
        hid_ps = [pb(f"hid_ps{i}", [P, 2, FT]) for i in range(4)]
        y_ps = [pb(f"y_ps{i}", [P, S, D]) for i in range(2)]
        got = [[[sb(f"got{i}_{s}_{k}", [P, D]) for k in range(TOP)] for s in range(S)] for i in range(UNROLL)] if not routed else None
        gathered = [sem(f"gathered{i}") for i in range(UNROLL)] if not routed else None
        half_added, added, written = (sem(n) for n in ("half_added", "added", "written")) if not routed else (None,) * 3
        tile_in = [sem(f"tile_in{i}") for i in range(UNROLL if routed else 1)]
        y_out = [sem(f"y_out{i}") for i in range(NY)] if routed else None
        w_high_set, w_ready, x_high_set = (sem(n) for n in ("w_high_set", "w_ready", "x_high_set"))
        xT_ready, hid_ready, hT_ready, y_ready, y_kept = (sem(n) for n in ("xT_ready", "hid_ready", "hT_ready", "y_ready", "y_kept"))
        turned_ready = sem("turned_ready") if routed else None
        silu_ready = sem("silu_ready") if gated else None
        block = ctx.enter_context(nc.Block())
        PER_TILE = 4 if gated else 2
        wp = lambda j: pack[j] if routed else pack[0]

        @block.sync
        def _(sp):
            def load(tile):
                i, j = tile.i, tile.place
                sp.wait_ge(y_kept, START + i - (UNROLL - 1))
                sp.dma_start(tok[j][:], rows_in[bass.ds(i * FT, FT), :].rearrange("(s p) d -> p s d", p=P)).then_inc(tile_in[j], 16)
                e = sp.value_load(routing.expert_of_tile[0:1, bass.ds(i, 1)], min_val=0, max_val=packs.shape[0] - 1)
                sp.dma_start(pack[j][:], packs[bass.ds(e, 1), :, :].rearrange("e p w -> (e p) w")).then_inc(tile_in[j], 16)

            def store(tile):
                i, j = tile.i, tile.place
                sp.wait_ge(y_kept, START + i + 1)
                sp.dma_start(rows_out[bass.ds(i * FT, FT), :].rearrange("(s p) d -> p s d", p=P), y[j % NY][:]).then_inc(y_out[j % NY], 16)

            if not routed:
                sp.dma_start(pack[0][:], packs[0, :, :]).then_inc(tile_in[0], 16)
                sp.wait_ge(tile_in[0], 16)

                def write(tile):
                    sp.wait_ge(added, tile.i + 1)
                    sp.dma_start(out[bass.ds(tile.i * FT, FT), :].rearrange("(s p) d -> p s d", p=P),
                                 x[:, bass.ds(S * tile.i, S), :]).then_inc(written, 16)

                over_tiles(sp, 0, tiles, write)
                sp.wait_ge(written, 16 * tiles)
                return
            for semaphore in tile_in + y_out:
                sp.sem_inc(semaphore, START)
            over_tiles(sp, 0, UNROLL - 1, load)

            def step(tile):
                load(tile)
                store(tile.back(UNROLL - 1))

            over_tiles(sp, UNROLL - 1, tiles, step)
            for i in range(tiles - UNROLL + 1, tiles):
                store(Tile(0, i))
            for i in range(tiles - NY, tiles):
                sp.wait_ge(y_out[i % NY], Tile(0, i).stored())

        @block.tensor
        def _(pe):
            def turn(tile):
                i, j = tile.i, tile.place
                pe.wait_ge(tile_in[j], tile.loaded())
                pe.wait_ge(xT_ready, START + i)
                for s in range(S):
                    last = nc.tensor.transpose(turned[:, s * P:(s + 1) * P], tok[j][:, s, :], ident)
                last.then_inc(turned_ready, 1)

            def hidden(tile):
                i, j = tile.i, tile.place
                pe.wait_ge(xT_ready, START + i + 1)
                pe.wait_ge(w_ready, i + 1 if routed else 1)
                w = [halves[j % 2 if routed else 0] for halves in (w_high, w_low)]
                products = ((w[0], x_high[j % 2]), (w[0], x_low[j % 2]), (w[1], x_high[j % 2]))
                for half in range(2):
                    if gated:
                        pe.wait_ge(hT_ready, START + 2 * i - 1 + half)
                        into = [hid_ps[2 * half], hid_ps[2 * half + 1]]
                    else:
                        pe.wait_ge(hT_ready, START + 2 * i - 3 + half)
                        into = [hid_ps[2 * (j % 2) + half]]
                    for k, bank in enumerate(into):
                        for c in range(2):
                            o = k * HID + (2 * half + c) * P
                            for n, (w_half, x_half) in enumerate(products):
                                last = nc.tensor.matmul(bank[:, c, :], w_half[:, o:o + P], x_half[:], start=(c + n == 0),
                                                        stop=(c == 1 and n == 2), skip_group_check=True)
                        last.then_inc(hid_ready, 1)

            def down(tile):
                i, j = tile.i, tile.place
                pe.wait_ge(hT_ready, START + 2 * i + 2)
                pe.wait_ge(y_kept, START + i - 1)
                o = (2 if gated else 1) * HID
                for s in range(S):
                    for c in range(CH):
                        last = nc.tensor.matmul(y_ps[j % 2][:, s, :], hT[j % 2][:, c, s * P:(s + 1) * P],
                                                wp(j)[:, o + c * D:o + (c + 1) * D], start=(c == 0), stop=(c == CH - 1))
                last.then_inc(y_ready, 1)

            if routed:
                pe.sem_inc(turned_ready, START)
            pe.sem_inc(y_ready, START)
            pe.sem_inc(hid_ready, START)
            if not routed:
                pe.wait_ge(tile_in[0], 16)
            def step(tile):
                if routed:
                    turn(tile.back(-1))
                hidden(tile)
                down(tile.back(1))

            if routed:
                turn(Tile(0, 0))
                turn(Tile(0, 1))
            hidden(Tile(0, 0))
            over_tiles(pe, 1, tiles - 1, step)
            hidden(Tile(0, tiles - 1))
            down(Tile(0, tiles - 2))
            down(Tile(0, tiles - 1))

        @block.scalar
        def _(act):
            def split_w(tile):
                i, j = tile.i, tile.place
                if routed:
                    act.wait_ge(tile_in[j], tile.loaded())
                    act.wait_ge(hid_ready, START + PER_TILE * (i - 1))
                else:
                    act.wait_ge(tile_in[0], 16)
                nc.scalar.activation(w_high[j % 2][:], wp(j)[:, 0:UP], ACT.Copy).then_inc(w_high_set, 1)

            def functions(tile):
                i, j = tile.i, tile.place
                if gated:
                    for half in range(2):
                        act.wait_ge(hid_ready, START + 4 * i + 2 * half + 1)
                        act.wait_ge(hT_ready, START + 2 * i - 1 + half)
                        nc.scalar.activation(silu[half][:], hid_ps[2 * half][:], ACT.Silu).then_inc(silu_ready, 1)
                else:
                    act.wait_ge(y_ready, START + i - 1)
                    for half in range(2):
                        act.wait_ge(hid_ready, START + 2 * i + half + 1)
                        for c in range(2):
                            b = 2 * HID + 2 * half + c
                            last = nc.scalar.activation(hT[j % 2][:, 2 * half + c, :], hid_ps[2 * (j % 2) + half][:, c, :],
                                                        ACT.Gelu, bias=wp(j)[:, b:b + 1])
                        last.then_inc(hT_ready, 1)

            if not gated:
                act.sem_inc(hT_ready, START)
            split_w(Tile(0, 0))
            if routed:
                def step(tile):
                    split_w(tile.back(-1))
                    functions(tile)

                split_w(Tile(0, 1))
                functions(Tile(0, 0))
                over_tiles(act, 1, tiles - 1, step)
                functions(Tile(0, tiles - 1))
            else:
                over_tiles(act, 0, tiles, functions)

        @block.vector
        def _(dve):
            def split_x(tile):
                i, j = tile.i, tile.place
                if routed:
                    dve.wait_ge(turned_ready, START + i + 1)
                dve.wait_ge(hid_ready, START + PER_TILE * (i - 1))
                src = turned[:] if routed else xnT[:, bass.ds(i * FT, FT)]
                nc.vector.tensor_copy(x_high[j % 2][:], src).then_inc(x_high_set, 1)
                dve.wait_ge(x_high_set, i + 1)
                nc.vector.tensor_tensor(x_low[j % 2][:], src, x_high[j % 2][:].bitcast(F32), ALU.subtract).then_inc(xT_ready, 1)

            def split_w(tile):
                i, j = tile.i, tile.place
                dve.wait_ge(w_high_set, i + 1)
                nc.vector.tensor_tensor(w_low[j % 2][:], wp(j)[:, 0:UP], w_high[j % 2][:].bitcast(F32), ALU.subtract).then_inc(w_ready, 1)

            def multiply(tile):
                i, j = tile.i, tile.place
                dve.wait_ge(y_ready, START + i - 1)
                for half in range(2):
                    dve.wait_ge(hid_ready, START + 4 * i + 2 * half + 2)
                    dve.wait_ge(silu_ready, 2 * i + half + 1)
                    nc.vector.tensor_tensor(hT[j % 2][:, 2 * half:2 * half + 2, :], hid_ps[2 * half + 1][:], silu[half][:],
                                            ALU.mult).then_inc(hT_ready, 1)

            def take_y(tile):
                i, j = tile.i, tile.place
                dve.wait_ge(y_ready, START + i + 1)
                if not routed:
                    at = x[:, bass.ds(S * i, S), :]
                    nc.vector.tensor_tensor(at, at, y_ps[j % 2][:], ALU.add).then_inc(y_kept, 1)
                    dve.wait_ge(y_kept, START + i + 1)
                    dve.wait_ge(gathered[j], tile.gathered())
                    for k, after in enumerate((half_added, added)):
                        if k:
                            dve.wait_ge(half_added, i + 1)
                        for s in range(S):
                            last = weighted_add(nc, x, S * i + s, got[j][s][k][:], routing.weight[k])
                        last.then_inc(after, 1)
                    return
                dve.wait_ge(y_out[j % NY], tile.back(NY).stored())
                if gated:
                    nc.vector.tensor_copy(y[j % NY][:], y_ps[j % 2][:]).then_inc(y_kept, 1)
                else:
                    b = 2 * HID + CH
                    bias = wp(j)[:, b:b + D].unsqueeze(1).to_broadcast([P, S, D])
                    nc.vector.tensor_tensor(y[j % NY][:], y_ps[j % 2][:], bias, ALU.add).then_inc(y_kept, 1)

            dve.sem_inc(xT_ready, START)
            dve.sem_inc(y_kept, START)
            if gated:
                dve.sem_inc(hT_ready, START)
            def prepare(tile):
                split_x(tile)
                if routed:
                    split_w(tile)

            def step(tile, last=False):
                if not last:
                    prepare(tile.back(-1))
                if gated:
                    multiply(tile)
                take_y(tile.back(1))

            if not routed:
                split_w(Tile(0, 0))
            prepare(Tile(0, 0))
            prepare(Tile(0, 1))
            if gated:
                multiply(Tile(0, 0))
            over_tiles(dve, 1, tiles - 1, step)
            step(Tile(0, tiles - 1), last=True)
            take_y(Tile(0, tiles - 1))


        @block.gpsimd
        def _(pool):
            for i in range(tiles if not routed else 0):
                if i >= UNROLL:
                    pool.wait_ge(added, i - UNROLL + 1)
                for s in range(S):
                    for k in range(TOP):
                        at = bass.IndirectOffsetOnAxis(ap=routing.slot[k][:, S * i + s:S * i + s + 1], axis=0)
                        nc.gpsimd.indirect_dma_start(got[i % UNROLL][s][k][:], None, rows_out, at).then_inc(gathered[i % UNROLL], 16)


def scatter_of(nc, xn, rows, routing, scattered, rows_zeroed=None):
    def scatter(pool, first, end):
        if first == 0 and rows_zeroed is not None:
            pool.wait_ge(*rows_zeroed)
        for t in range(first, end):
            for k in range(TOP):
                at = bass.IndirectOffsetOnAxis(ap=routing.slot[k][:, t:t + 1], axis=0)
                nc.gpsimd.indirect_dma_start(rows, at, xn[:, t, :], None).then_inc(scattered, 16)

    def wait_for_all(pool):
        pool.wait_ge(scattered, 16 * TOP * TILES)

    return scatter, wait_for_all


def causal_attention(nc, x, xnT, const, const_bf, w_q, w_k, w_v, b_qk, b_v, w_out, b_out, selectors, routing, scatter,
                     scattered_all):
    ident = const[:, C_ID:C_ID + P]
    ident_bf = const_bf[:, C_ID:C_ID + P]
    with ExitStack() as ctx:
        sb = lambda n, s, d=F32: ctx.enter_context(nc.sbuf_tensor(f"att_{n}", s, d))
        pb = lambda n, s, d=F32: ctx.enter_context(nc.psum_tensor(f"att_{n}", s, d))
        sem = lambda n: ctx.enter_context(nc.semaphore(f"att_{n}"))
        select = sb("select", [P, 2, 2, HG, P], F32R)
        xT = [sb(f"xT{i}", [P, SEQ]) for i in range(2)]
        full = sb("full", [P, 2, SEQ])
        high, low = (sb(n, [P, 2, SEQ], F32R) for n in ("high", "low"))
        q_rows = [sb(f"q_rows{i}", [P, HG, SEQ], F32R) for i in range(2)]
        k_rows = sb("k_rows", [P, HG, SEQ])
        k_member = [sb(f"k_member{i}", [P, HG, HM, SEQ], F32R) for i in range(2)]
        v_ones = [sb(f"v_ones{i}", [P, 2, H, 32]) for i in range(2)]
        maxima = sb("maxima", [P, 2, H])
        minus_max = sb("minus_max", [P, 2, HG, 2, HM], BF16)
        probs_a = [sb(f"probs_a{i}", [P, HM, SEQ]) for i in range(2)]
        probs_b = [sb(f"probs_b{i}", [P, HM, P]) for i in range(2)]
        oT = sb("oT", [P, HG, SEQ])
        inv = sb("inv", [P, H])
        o_tok = [sb(f"o_tok{i}", [P, H, HS]) for i in range(2)]
        o_cols = sb("o_cols", [P, SEQ])
        with_bias = sb("with_bias", [P, 2, D])

        bank_s = [pb(f"bank_s{i}", [P, 512]) for i in range(2)]
        bank_a = [pb(f"bank_a{i}", [P, 2, SEQ]) for i in range(2)]
        bank_b = pb("bank_b", [P, 2, SEQ])
        bank_m = [pb(f"bank_m{i}", [P, 512]) for i in range(3)]

        xT_in = [sem(f"xT_in{i}") for i in range(2)]
        qk_filled, qk_biased, high_set, halves, stack_q, stack_k, q_ready, k_kept, k_ready, v_filled, v_ready = (
            sem(n) for n in ("qk_filled", "qk_biased", "high_set", "halves", "stack_q", "stack_k", "q_ready", "k_kept",
                             "k_ready", "v_filled", "v_ready"))
        s_ready, max_ready, minus_high, minus_ready, max_turned, rows_ready = (
            sem(n) for n in ("s_ready", "max_ready", "minus_high", "minus_ready", "max_turned", "rows_ready"))
        a_ready, b_ready, exp_a, exp_b, probs_ready, weighed, oT_ready = (
            sem(n) for n in ("a_ready", "b_ready", "exp_a", "exp_b", "probs_ready", "weighed", "oT_ready"))
        back_filled, inv_ready, otok_ready, cols_filled, cols_ready, out_filled, out_taken = (
            sem(n) for n in ("back_filled", "inv_ready", "otok_ready", "cols_filled", "cols_ready", "out_filled", "out_taken"))
        zero_set, constants_set = sem("zero_set"), sem("constants_set")
        block = ctx.enter_context(nc.Block())

        def wait(eng, semaphore, value):
            if not isinstance(value, int) or value > 0:
                eng.wait_ge(semaphore, value)

        UNITS = 3 * HG
        BODY = 4

        def unit(u):
            return u // 3, int(u % 3 > 0), (range(HM), range(0, 2), range(2, 4))[u % 3]

        def steps(eng, step):
            step(0, 0, "A")
            step(1, 1, "AB")
            step(2, 0, "ABC")
            with eng.Fori(0, (BATCH - 4) // BODY) as r:
                for i in range(BODY):
                    step(BODY * r + (3 + i), (3 + i) % 2, "ABCD")
            step(BATCH - 1, 1, "ABCD")
            step(BATCH, 0, "BCD")
            step(BATCH + 1, 1, "CD")
            step(BATCH + 2, 0, "D")

        @block.tensor
        def _(pe):
            def project_qk(s, p):
                pe.wait_ge(xT_in[p], 8 * (s - p) + 16)
                wait(pe, rows_ready, 2 * s - 3)
                wait(pe, q_ready, 2 * s)
                for which, w in enumerate((w_q, w_k)):
                    last = nc.tensor.matmul(bank_m[0][:, which * SEQ:(which + 1) * SEQ], w[:], xT[p][:],
                                            start=(which == 0), stop=(which == 1), skip_group_check=True)
                last.then_inc(qk_filled, 1)

            def stack(s, which, half):
                if half == 0:
                    pe.wait_ge(halves, 2 * s + 2)
                    if which == 1:
                        wait(pe, v_ready, s)
                else:
                    pe.wait_ge((q_ready, k_kept)[which], 2 * s + 1)
                for g in range(2):
                    for n, part in enumerate((high, low)):
                        last = nc.tensor.matmul(bank_m[which][:, g * SEQ:(g + 1) * SEQ], select[:, which, n, 2 * half + g, :],
                                                part[:, which, :], start=(g + n == 0), stop=(g + n == 2), skip_group_check=True)
                last.then_inc((stack_q, stack_k)[which], 1)

            def project_v(s, p):
                wait(pe, rows_ready, 2 * s)
                pe.wait_ge(k_kept, 2 * s + 2)
                for t in range(2):
                    last = nc.tensor.matmul(bank_m[1][:, t * D:(t + 1) * D], xT[p][:, t * P:(t + 1) * P], w_v[:],
                                            start=(t == 0), stop=(t == 1), skip_group_check=True)
                last.then_inc(v_filled, 1)

            def scores(s, p, first, end):
                for u in range(first, end):
                    g, t, members = unit(u)
                    if u % (UNITS // 2) == 0:
                        half = u // (UNITS // 2)
                        pe.wait_ge(q_ready, 2 * s + half + 1)
                        pe.wait_ge(k_ready, 2 * HM * s + HM * (half + 1))
                    wait(pe, max_ready, UNITS * s + (u - 1))
                    bank = bank_s[u % 2][:].rearrange("p (m k) -> p m k", m=len(members))
                    nc.tensor.matmul(bank, q_rows[p][:, g, t * P:(t + 1) * P],
                                     k_member[p][:, g, members[0]:members[-1] + 1, 0:(t + 1) * P],
                                     start=True, stop=False, skip_group_check=True)
                    nc.tensor.matmul(bank[:, :, t * P:(t + 1) * P], ident_bf,
                                     const_bf[:, C_MB:C_MB + P].unsqueeze(1).to_broadcast([P, len(members), P]),
                                     start=False, stop=True, skip_group_check=True).then_inc(s_ready, 1)

            def turn_maxima(s, half, stages):
                pe.wait_ge(minus_ready, s + 1)
                if "A" in stages:
                    pe.wait_ge((q_ready, k_kept)[half], 2 * s + 4)
                elif half == 0:
                    pe.wait_ge(rows_ready, 2 * s - 1)
                else:
                    pe.wait_ge(v_ready, s + 1)
                for g in range(2):
                    for t in range(2):
                        last = nc.tensor.matmul(bank_m[half][MAX_ROW:MAX_ROW + 2 * HM, g * SEQ + t * P:g * SEQ + (t + 1) * P],
                                                minus_max[:, t, 2 * half + g, :, :].rearrange("p a m -> p (a m)"), ident_bf,
                                                start=(g + t == 0), stop=(g + t == 2), skip_group_check=True)
                last.then_inc(max_turned, 1)

            def shifted(s, p, g, pair):
                n = 2 * g + pair
                if n == 0:
                    pe.wait_ge(rows_ready, 2 * s + 1)
                if n == 4:
                    pe.wait_ge(rows_ready, 2 * s + 2)
                wait(pe, exp_a, 8 * s + n - 1)
                for k in range(2):
                    last = nc.tensor.matmul(bank_a[pair][:, k, :], k_member[p][:, g, 2 * pair + k, 0:P], q_rows[p][:, g, :],
                                            start=(k == 0), stop=(k == 1), skip_group_check=True)
                last.then_inc(a_ready, 1)
                wait(pe, exp_b, 8 * s + n)
                for k in range(2):
                    last = nc.tensor.matmul(bank_b[:, k, :], k_member[p][:, g, 2 * pair + k, P:2 * P], q_rows[p][:, g, :],
                                            start=(k == 0), stop=(k == 1), skip_group_check=True)
                last.then_inc(b_ready, 1)

            def weigh(s, p, g):
                pe.wait_ge(probs_ready, 8 * s + 2 * g + 2)
                if g == 0:
                    wait(pe, out_taken, s)
                if g == 2:
                    pe.wait_ge(oT_ready, 2 * s + 1)
                at = (g % 2) * SEQ
                for m in range(HM):
                    nc.tensor.matmul(bank_m[2][32 * m:32 * m + 32, at:at + SEQ], v_ones[p][:, 0, HM * g + m, :], probs_a[g % 2][:, m, :],
                                     start=True, stop=False, skip_group_check=True)
                for m in range(HM):
                    last = nc.tensor.matmul(bank_m[2][32 * m:32 * m + 32, at + P:at + SEQ], v_ones[p][:, 1, HM * g + m, :],
                                            probs_b[g % 2][:, m, :], start=False, stop=True, skip_group_check=True)
                last.then_inc(weighed, 1)

            def turn_back(s, t):
                pe.wait_ge(oT_ready, 2 * s + 2)
                if t == 1:
                    pe.wait_ge(otok_ready, 2 * s + 1)
                for g in range(HG):
                    last = nc.tensor.transpose(bank_m[2][:, g * P:(g + 1) * P], oT[:, g, t * P:(t + 1) * P], ident)
                last.then_inc(back_filled, 1)

            def to_columns(s):
                pe.wait_ge(otok_ready, 2 * s + 2)
                for t in range(2):
                    last = nc.tensor.transpose(bank_m[2][:, t * P:(t + 1) * P], o_tok[t][:].rearrange("p h d -> p (h d)"), ident)
                last.then_inc(cols_filled, 1)

            def project_out(s):
                pe.wait_ge(cols_ready, s + 1)
                for t in range(2):
                    last = nc.tensor.matmul(bank_m[2][:, t * D:(t + 1) * D], o_cols[:, t * P:(t + 1) * P], w_out[:],
                                            start=(t == 0), stop=(t == 1), skip_group_check=True)
                last.then_inc(out_filled, 1)

            def step(t, p, stages):
                a, b, c, d = (t - i for i in range(4))
                A, B, C, D_ = (n in stages for n in "ABCD")
                q = 1 - p
                if B: scores(b, q, 0, 1)
                if D_: turn_back(d, 0)
                if C: shifted(c, p, 0, 0)
                if A: project_qk(a, p)
                if D_: turn_back(d, 1)
                if C: shifted(c, p, 0, 1)
                if B: scores(b, q, 1, 3)
                if D_: to_columns(d)
                if B: project_v(b, q)
                if C: shifted(c, p, 1, 0)
                if B: scores(b, q, 3, 4)
                if D_: project_out(d)
                if B: scores(b, q, 4, 5)
                if C: shifted(c, p, 1, 1)
                if A: stack(a, 0, 0)
                if C: weigh(c, p, 0)
                if C: shifted(c, p, 2, 0)
                if A: stack(a, 1, 0)
                if B: scores(b, q, 5, 7)
                if C: shifted(c, p, 2, 1)
                if B: scores(b, q, 7, 8)
                if C: weigh(c, p, 1)
                if C: shifted(c, p, 3, 0)
                if B: scores(b, q, 8, 10)
                if A: stack(a, 1, 1)
                if C: shifted(c, p, 3, 1)
                if A: stack(a, 0, 1)
                if B: scores(b, q, 10, 12)
                if C: weigh(c, p, 2)
                if C: weigh(c, p, 3)
                if B: turn_maxima(b, 0, stages)
                if B: turn_maxima(b, 1, stages)

            pe.wait_ge(constants_set, 1)
            steps(pe, step)

        @block.sync
        def _(sp):
            def load(s, p):
                wait(sp, v_filled, s - 1)
                sp.dma_start(xT[p][:], xnT[:, bass.ds(s * SEQ, SEQ)]).then_inc(xT_in[p], 16)

            for s in range(2):
                load(s, s)
            with sp.Fori(0, BATCH // 2 - 1) as r:
                for p in range(2):
                    load(2 * r + (2 + p), p)
            for p in range(2):
                sp.wait_ge(xT_in[p], 8 * BATCH)

        @block.scalar
        def _(act):
            def add_bias(s):
                act.wait_ge(qk_filled, s + 1)
                wait(act, halves, 2 * s)
                for which in range(2):
                    nc.scalar.activation(full[:, which, :], bank_m[0][:, which * SEQ:(which + 1) * SEQ], ACT.Identity,
                                         bias=b_qk[:, which:which + 1]).then_inc(qk_biased, 1)

            def keep_k(s, half):
                act.wait_ge(stack_k, 2 * s + half + 1)
                wait(act, k_ready, 2 * HM * s - HM + HM * half)
                nc.scalar.activation(k_rows[:, 2 * half:2 * half + 2, :], bank_m[1][:].rearrange("p (g q) -> p g q", g=2),
                                     ACT.Identity, bias=const[:, C_RM + HM:C_RM + HM + 1]).then_inc(k_kept, 1)

            def exponentials(s, g, pair):
                n = 2 * g + pair
                act.wait_ge(a_ready, 8 * s + n + 1)
                wait(act, weighed, 4 * s + (g - 1))
                two = slice(2 * pair, 2 * pair + 2)
                nc.scalar.activation(probs_a[g % 2][:, two, :], bank_a[pair][:], ACT.Exp, scale=HS ** -0.5).then_inc(exp_a, 1)
                act.wait_ge(b_ready, 8 * s + n + 1)
                nc.scalar.activation(probs_b[g % 2][:, two, :], bank_b[:, :, P:2 * P], ACT.Exp, scale=HS ** -0.5).then_inc(exp_b, 1)

            def keep_maxima(s, p, half):
                act.wait_ge(max_turned, 2 * s + half + 1)
                at = slice(MAX_ROW, MAX_ROW + 2 * HM)
                nc.scalar.activation(q_rows[p][at, 2 * half:2 * half + 2, :], bank_m[half][at, :].rearrange("p (g q) -> p g q", g=2),
                                     ACT.Copy).then_inc(rows_ready, 1)

            def keep_oT(s, half):
                act.wait_ge(weighed, 4 * s + 2 * half + 2)
                nc.scalar.activation(oT[:, 2 * half:2 * half + 2, :], bank_m[2][:].rearrange("p (g q) -> p g q", g=2),
                                     ACT.Copy).then_inc(oT_ready, 1)

            def keep_cols(s):
                act.wait_ge(cols_filled, s + 1)
                nc.scalar.activation(o_cols[:], bank_m[2][:, 0:SEQ], ACT.Copy).then_inc(cols_ready, 1)

            def step(t, p, stages):
                a, b, c, d = (t - i for i in range(4))
                A, B, C, D_ = (n in stages for n in "ABCD")
                q = 1 - p
                if C: exponentials(c, 0, 0)
                if A: add_bias(a)
                if C: exponentials(c, 0, 1)
                if D_: keep_cols(d)
                if C: exponentials(c, 1, 0)
                if C: exponentials(c, 1, 1)
                if C: exponentials(c, 2, 0)
                if A: keep_k(a, 0)
                if C: exponentials(c, 2, 1)
                if C: keep_oT(c, 0)
                if C: exponentials(c, 3, 0)
                if C: exponentials(c, 3, 1)
                if A: keep_k(a, 1)
                if C: keep_oT(c, 1)
                if B: keep_maxima(b, q, 0)
                if B: keep_maxima(b, q, 1)

            routing.finish_exp(nc, act, False)
            steps(act, step)

        @block.vector
        def _(dve):
            def split(s, which):
                dve.wait_ge(qk_biased, 2 * s + which + 1)
                wait(dve, (stack_q, stack_k)[which], 2 * s)
                nc.vector.tensor_copy(high[:, which, :], full[:, which, :]).then_inc(high_set, 1)
                dve.wait_ge(high_set, 2 * s + which + 1)
                nc.vector.tensor_tensor(low[:, which, :], full[:, which, :], high[:, which, :].bitcast(F32),
                                        ALU.subtract).then_inc(halves, 1)

            def keep_q(s, p, half):
                dve.wait_ge(stack_q, 2 * s + half + 1)
                wait(dve, b_ready, 8 * s - 12 + 4 * half)
                nc.vector.tensor_copy(q_rows[p][:, 2 * half:2 * half + 2, :],
                                      bank_m[0][:].rearrange("p (g q) -> p g q", g=2)).then_inc(q_ready, 1)

            def keep_v(s, p):
                dve.wait_ge(v_filled, s + 1)
                wait(dve, weighed, 4 * s - 4)
                nc.vector.tensor_tensor(v_ones[p][:, :, :, 0:HS], bank_m[1][:, 0:2 * D].rearrange("p (t h d) -> p t h d", t=2, h=H),
                                        b_v[:].rearrange("p (h d) -> p h d", h=H).unsqueeze(1).to_broadcast([P, 2, H, HS]),
                                        ALU.add).then_inc(v_ready, 1)

            def reduce(s, first, end):
                for u in range(first, end):
                    g, t, members = unit(u)
                    h = HM * g + members[0]
                    dve.wait_ge(s_ready, UNITS * s + u + 1)
                    nc.vector.reduce_max(maxima[:, t, h:h + len(members)],
                                         bank_s[u % 2][:].rearrange("p (m k) -> p m k", m=len(members)), AX.X).then_inc(max_ready, 1)

            def split_maxima(s):
                dve.wait_ge(max_ready, UNITS * (s + 1))
                wait(dve, max_turned, 2 * s)
                high, low = (minus_max[:, :, :, a, :].rearrange("p t g m -> p (t g) m") for a in range(2))
                src = maxima[:].rearrange("p t (g m) -> p (t g) m", m=HM)
                nc.vector.tensor_scalar(high, src, -1.0, None, ALU.mult).then_inc(minus_high, 1)
                dve.wait_ge(minus_high, s + 1)
                nc.vector.scalar_tensor_tensor(low, src, -1.0, high, ALU.mult, ALU.subtract).then_inc(minus_ready, 1)

            def normalise(s, t):
                dve.wait_ge(back_filled, 2 * s + t + 1)
                heads = bank_m[2][:].rearrange("p (h c) -> p h c", c=32)
                nc.vector.reciprocal(inv[:], heads[:, :, HS]).then_inc(inv_ready, 1)
                dve.wait_ge(inv_ready, 2 * s + t + 1)
                nc.vector.tensor_tensor(o_tok[t][:], heads[:, :, 0:HS], inv[:].unsqueeze(2).to_broadcast([P, H, HS]),
                                        ALU.mult).then_inc(otok_ready, 1)

            def add_out(s):
                dve.wait_ge(out_filled, s + 1)
                nc.vector.tensor_tensor(with_bias[:], bank_m[2][:, 0:2 * D].rearrange("p (t d) -> p t d", t=2),
                                        b_out[:].unsqueeze(1).to_broadcast([P, 2, D]), ALU.add).then_inc(out_taken, 1)
                dve.wait_ge(out_taken, s + 1)
                at = x[:, bass.ds(2 * s, 2), :]
                nc.vector.tensor_tensor(at, at, with_bias[:], ALU.add)

            def step(t, p, stages):
                a, b, c, d = (t - i for i in range(4))
                A, B, C, D_ = (n in stages for n in "ABCD")
                q = 1 - p
                if D_: normalise(d, 0)
                if B: reduce(b, 0, 1)
                if D_: normalise(d, 1)
                if A: split(a, 0)
                if B: reduce(b, 1, 3)
                if A: split(a, 1)
                if D_: add_out(d)
                if B: keep_v(b, q)
                if B: reduce(b, 3, 5)
                if A: keep_q(a, p, 0)
                if B: reduce(b, 5, 10)
                if A: keep_q(a, p, 1)
                if B: reduce(b, 10, 12)
                if B: split_maxima(b)

            for p in range(2):
                nc.vector.memset(v_ones[p][:], 0.0)
            nc.vector.tensor_copy(select[:].rearrange("p a b g r -> p (a b g r)"), selectors[:]).then_inc(zero_set, 1)
            dve.wait_ge(zero_set, 1)
            for p in range(2):
                last = nc.vector.memset(v_ones[p][:, :, :, HS:HS + 1], 1.0)
            last.then_inc(constants_set, 1)
            dve.wait_ge(constants_set, 1)
            routing.finish(nc, dve, const, False)
            steps(dve, step)

        @block.gpsimd
        def _(pool):
            def member_keys(s, half, members):
                of = slice(2 * half, 2 * half + 2)
                if members[0] == 0:
                    pool.wait_ge(k_kept, 2 * s + half + 1)
                    wait(pool, b_ready, 8 * s - 12 + 4 * half)
                for m in members:
                    nc.gpsimd.tensor_scalar(k_member[s % 2][:, of, m, :], k_rows[:, of, :],
                                            const[:, C_RM + m:C_RM + m + 1], 1.0, ALU.mult, ALU.mult).then_inc(k_ready, 1)

            def keep_causal(s, g):
                for ready, block_of in ((exp_a, probs_a[g % 2][:, :, 0:P]), (exp_b, probs_b[g % 2][:])):
                    pool.wait_ge(ready, 8 * s + 2 * g + 2)
                    nc.gpsimd.affine_select(out=block_of, in_=block_of, pattern=[[0, HM], [1, P]], compare_op=ALU.is_ge,
                                            fill=0.0, base=0, channel_multiplier=-1).then_inc(probs_ready, 1)

            for t in range(BATCH + 2):
                a, c = t, t - 2
                A, C = t < BATCH, t > 1
                if A: scatter(pool, 2 * t, 2 * t + 1)
                if C: keep_causal(c, 0)
                if C: keep_causal(c, 1)
                if A: member_keys(a, 0, (0,))
                if C: keep_causal(c, 2)
                if A: member_keys(a, 0, (1, 2, 3))
                if C: keep_causal(c, 3)
                if A: scatter(pool, 2 * t + 1, 2 * t + 2)
                if A: member_keys(a, 1, (0, 1, 2, 3))
            scattered_all(pool)


def attention(nc, x, xnT, const, w_q, w_k, w_v, routing, scatter, scattered_all):
    ident = const[:, C_ID:C_ID + P]
    with ExitStack() as ctx:
        sb = lambda n, s, d=F32: ctx.enter_context(nc.sbuf_tensor(f"att1_{n}", s, d))
        pb = lambda n, s, d=F32: ctx.enter_context(nc.psum_tensor(f"att1_{n}", s, d))
        sem = lambda n: ctx.enter_context(nc.semaphore(f"att1_{n}"))
        xT = [sb(f"xT{i}", [P, SEQ]) for i in range(2)]
        qT, kT = sb("qT", [P, SEQ]), sb("kT", [P, SEQ])
        v = [sb(f"v{i}", [P, 2, D]) for i in range(2)]
        top = sb("top", [P, 2])
        minus_top = [sb(f"minus_top{i}", [P, 2]) for i in range(2)]
        total = [sb(f"total{i}", [P, 2]) for i in range(2)]
        inv = sb("inv", [P, 2])
        probs = [sb(f"probs{i}", [P, 2, SEQ]) for i in range(2)]
        probsT = sb("probsT", [P, 2, 2, P])
        qk_ps, v_ps, turned, o_ps = pb("qk_ps", [P, 2, SEQ]), pb("v_ps", [P, 2, D]), pb("turned", [P, 2, 2, P]), pb("o_ps", [P, 2, D])
        s_ps = [pb(f"s_ps{i}", [P, 2, SEQ]) for i in range(2)]
        xT_in = [sem(f"xT_in{i}") for i in range(2)]
        names = ("qk_ready", "qk_taken", "v_ready", "v_taken", "s_ready", "top_ready", "minus_ready", "probs_ready",
                 "turned_ready", "probsT_ready", "o_ready", "inv_ready", "x_added")
        (qk_ready, qk_taken, v_ready, v_taken, s_ready, top_ready, minus_ready, probs_ready,
         turned_ready, probsT_ready, o_ready, inv_ready, x_added) = (sem(n) for n in names)
        block = ctx.enter_context(nc.Block())

        def wait(eng, semaphore, value):
            if not isinstance(value, int) or value > 0:
                eng.wait_ge(semaphore, value)

        def steps(eng, new, old, both):
            new(0, 0)
            both(1, 1)
            with eng.Fori(0, BATCH // 2 - 1) as r:
                both(2 * r + 2, 0)
                both(2 * r + 3, 1)
            old(BATCH - 1, 1)

        @block.tensor
        def _(pe):
            def project(s, p):
                pe.wait_ge(xT_in[p], 8 * (s - p) + 16)
                wait(pe, qk_taken, 2 * s)
                for which, w in enumerate((w_q, w_k)):
                    last = nc.tensor.matmul(qk_ps[:, which, :], w[:], xT[p][:], start=(which == 0), stop=(which == 1),
                                            skip_group_check=True)
                last.then_inc(qk_ready, 1)

            def project_v(s, p):
                wait(pe, v_taken, s)
                for t in range(2):
                    last = nc.tensor.matmul(v_ps[:, t, :], xT[p][:, t * P:(t + 1) * P], w_v[:], start=(t == 0), stop=(t == 1),
                                            skip_group_check=True)
                last.then_inc(v_ready, 1)

            def scores(s, p):
                pe.wait_ge(qk_taken, 2 * s + 2)
                wait(pe, probs_ready, 2 * s - 2)
                for t in range(2):
                    last = nc.tensor.matmul(s_ps[p][:, t, :], qT[:, t * P:(t + 1) * P], kT[:], start=(t == 0), stop=(t == 1),
                                            skip_group_check=True)
                last.then_inc(s_ready, 1)

            def turn(s, p):
                pe.wait_ge(probs_ready, 2 * s + 2)
                wait(pe, probsT_ready, s)
                for k in range(2):
                    for t in range(2):
                        last = nc.tensor.transpose(turned[:, k, t, :], probs[p][:, t, k * P:(k + 1) * P], ident)
                last.then_inc(turned_ready, 1)

            def weigh(s, p):
                pe.wait_ge(probsT_ready, s + 1)
                pe.wait_ge(v_taken, s + 1)
                wait(pe, x_added, s)
                for t in range(2):
                    for k in range(2):
                        last = nc.tensor.matmul(o_ps[:, t, :], probsT[:, k, t, :], v[p][:, k, :], start=(k == 0), stop=(k == 1))
                last.then_inc(o_ready, 1)

            def new(s, p):
                project(s, p)
                project_v(s, p)
                scores(s, p)

            def old(s, p):
                turn(s, p)
                weigh(s, p)

            def both(s, p):
                project(s, p)
                turn(s - 1, 1 - p)
                project_v(s, p)
                scores(s, p)
                weigh(s - 1, 1 - p)

            steps(pe, new, old, both)

        @block.sync
        def _(sp):
            def load(s, p):
                wait(sp, v_ready, s - 1)
                sp.dma_start(xT[p][:], xnT[:, bass.ds(s * SEQ, SEQ)]).then_inc(xT_in[p], 16)

            for s in range(2):
                load(s, s)
            with sp.Fori(0, BATCH // 2 - 1) as r:
                for p in range(2):
                    load(2 * r + (2 + p), p)
            for p in range(2):
                sp.wait_ge(xT_in[p], 8 * BATCH)

        @block.scalar
        def _(act):
            def take_qk(s):
                act.wait_ge(qk_ready, s + 1)
                wait(act, s_ready, s)
                nc.scalar.activation(qT[:], qk_ps[:, 0, :], ACT.Copy, scale=D ** -0.5).then_inc(qk_taken, 1)
                nc.scalar.activation(kT[:], qk_ps[:, 1, :], ACT.Copy).then_inc(qk_taken, 1)

            def exponentials(s, p):
                act.wait_ge(minus_ready, s + 1)
                wait(act, turned_ready, s - 1)
                wait(act, x_added, s - 1)
                for t in range(2):
                    nc.scalar.activation(probs[p][:, t, :], s_ps[p][:, t, :], ACT.Exp, bias=minus_top[p][:, t:t + 1],
                                         accum_out=total[p][:, t:t + 1]).then_inc(probs_ready, 1)

            def take_turned(s):
                act.wait_ge(turned_ready, s + 1)
                wait(act, o_ready, s)
                nc.scalar.activation(probsT[:], turned[:], ACT.Copy).then_inc(probsT_ready, 1)

            def new(s, p):
                take_qk(s)
                exponentials(s, p)

            def old(s, p):
                take_turned(s)

            def both(s, p):
                take_qk(s)
                take_turned(s - 1)
                exponentials(s, p)

            routing.finish_exp(nc, act, True)
            steps(act, new, old, both)

        @block.vector
        def _(dve):
            def take_v(s, p):
                dve.wait_ge(v_ready, s + 1)
                wait(dve, o_ready, s - 1)
                nc.vector.tensor_copy(v[p][:], v_ps[:]).then_inc(v_taken, 1)

            def maxima(s, p):
                dve.wait_ge(s_ready, s + 1)
                nc.vector.reduce_max(top[:], s_ps[p][:], AX.X).then_inc(top_ready, 1)
                dve.wait_ge(top_ready, s + 1)
                wait(dve, probs_ready, 2 * s - 2)
                nc.vector.tensor_scalar(minus_top[p][:], top[:], -1.0, None, ALU.mult).then_inc(minus_ready, 1)

            def add_out(s, p):
                dve.wait_ge(probs_ready, 2 * s + 2)
                wait(dve, x_added, s)
                nc.vector.reciprocal(inv[:], total[p][:]).then_inc(inv_ready, 1)
                dve.wait_ge(inv_ready, s + 1)
                dve.wait_ge(o_ready, s + 1)
                for t in range(2):
                    at = x[:, bass.ds(2 * s + t, 1), :].squeeze(1)
                    last = nc.vector.scalar_tensor_tensor(at, o_ps[:, t, :], inv[:, t:t + 1], at, ALU.mult, ALU.add)
                last.then_inc(x_added, 1)

            def new(s, p):
                take_v(s, p)
                maxima(s, p)

            def old(s, p):
                add_out(s, p)

            def both(s, p):
                take_v(s, p)
                maxima(s, p)
                add_out(s - 1, 1 - p)

            routing.finish(nc, dve, const, True)
            steps(dve, new, old, both)

        @block.gpsimd
        def _(pool):
            scatter(pool, 0, TILES)
            scattered_all(pool)


def program(nc, x_in, constants, gate0, gate1, att0, att1, packs0, packs1, out):
    rows_in, rows_out = (nc.dram_tensor(n, [rows, D], F32, kind="Internal").ap() for n, rows in (("rows_in", ROWS), ("rows_out", FT * NT0)))
    with ExitStack() as ctx:
        def sb(name, shape, dt=F32):
            return ctx.enter_context(nc.sbuf_tensor(name, shape, dt))

        x, xn, xnT = sb("x", [P, TILES, D]), sb("xn", [P, TILES, D]), sb("xnT", [P, TOKENS])
        const = sb("const", [P, C_ALL])
        const_bf = sb("const_bf", [P, C_REV], BF16)
        gates = [sb("gate0", [P, E0]), sb("gate1", [P, E1])]
        routing0 = Routing(ctx, nc, "routing0", E0, NT0)
        const_in, const_bf_set, zero_set, rows_zeroed = (
            ctx.enter_context(nc.semaphore(n)) for n in ("const_in", "const_bf_set", "zero_set", "rows_zeroed"))
        att_in, scattered = ([ctx.enter_context(nc.semaphore(f"{n}{l}")) for l in range(2)] for n in ("att_in", "scattered"))
        const_loaded = (const_in, 16 * 3)

        with nc.Block() as block:
            @block.sync
            def _(sp):
                for dst, src in ((const[:], constants), (gates[0][:], gate0), (gates[1][:], gate1)):
                    sp.dma_start(dst, src).then_inc(const_in, 16)

        def load_weights(pool, layer, parts, arrays):
            for dst, src in zip(parts, arrays):
                pool.dma_start(dst[:], src).then_inc(att_in[layer], 16)
            pool.wait_ge(att_in[layer], 16 * len(arrays))

        with ExitStack() as layer:
            parts = [layer.enter_context(nc.sbuf_tensor(f"att0_w{i}", list(a.shape), F32)) for i, a in enumerate(att0)]
            zero = layer.enter_context(nc.sbuf_tensor("zero", [P, D], F32))
            def prepare(pool, groups_ready, all_groups):
                nc.gpsimd.memset(zero[:], 0.0).then_inc(zero_set, 1)
                pool.wait_ge(*const_loaded)
                nc.gpsimd.tensor_copy(const_bf[:], const[:, 0:C_REV]).then_inc(const_bf_set, 1)
                load_weights(pool, 0, parts, att0)
                pool.wait_ge(zero_set, 1)
                pool.wait_ge(groups_ready, all_groups)
                for r in range(0, ROWS, ZEROED):
                    pool.dma_start(rows_in[r:r + ZEROED, :].rearrange("(p t) d -> p t d", p=P),
                                   zero[:].unsqueeze(1).to_broadcast([P, ZEROED // P, D])).then_inc(rows_zeroed, 16)

            norm_and_route(nc, "route0", x, xn, xnT, const, const_bf, gates[0], routing0, 8, prepare, x_in=x_in,
                           const_loaded=const_loaded, const_bf_set=const_bf_set)
            causal_attention(nc, x, xnT, const, const_bf, *parts, routing0, *scatter_of(nc, xn, rows_in, routing0, scattered[0], (rows_zeroed, 16 * (ROWS // ZEROED))))
        expert_tiles(nc, "experts0", NT0, const, packs0, False, True, rows_in, rows_out, routing0)
        routing1 = Routing(ctx, nc, "routing1", E1, NT1)
        with ExitStack() as layer:
            parts = [layer.enter_context(nc.sbuf_tensor(f"att1_w{i}", list(a.shape), F32)) for i, a in enumerate(att1)]
            norm_and_route(nc, "route1", x, xn, xnT, const, const_bf, gates[1], routing1, 4,
                           lambda pool, *_: load_weights(pool, 1, parts, att1), results=(rows_out, routing0))
            attention(nc, x, xnT, const, *parts, routing1, *scatter_of(nc, xn, rows_in, routing1, scattered[1]))
        expert_tiles(nc, "experts1", NT1, const, packs1[0:E1], True, True, rows_in, rows_out, routing1)
        expert_tiles(nc, "shared", TOKENS // FT, const, packs1[E1:E1 + 1], True, False, None, rows_out, routing1,
                     x=x, xnT=xnT, out=out)


def kernel(L0_attn_encodings, L0_attn_attn_W, L0_attn_attn_b, L0_attn_out_W, L0_attn_out_b, L0_ffn_Wg, L0_ffn_W1, L0_ffn_b1,
           L0_ffn_W2, L0_ffn_b2, L1_attn_W_qkv, L1_ffn_shared_up, L1_ffn_shared_gate, L1_ffn_shared_down, L1_ffn_routed_up,
           L1_ffn_routed_gate, L1_ffn_routed_down, L1_ffn_router_w):
    import concourse.bacc as bacc
    from concourse.bass_utils import run_bass_kernel_spmd

    host = np.asarray

    def down_rows(w):
        return w.transpose(0, 2, 1).reshape(-1, CH, P, D).transpose(0, 2, 1, 3).reshape(-1, P, CH * D)

    w = host(L0_attn_attn_W).reshape(D, H, 3, HS)
    b = host(L0_attn_attn_b).reshape(H, 3, HS)
    everywhere = lambda a: np.broadcast_to(a.reshape(1, -1), (P, a.size))
    att0 = [*(w[:, :, k].reshape(D, D) for k in range(3)), b[:, 0:2].transpose(0, 2, 1).reshape(D, 2), everywhere(b[:, 2]),
            host(L0_attn_out_W), everywhere(host(L0_attn_out_b)), half_selectors()]
    w1 = host(L1_attn_W_qkv)
    att1 = [w1[i * D:(i + 1) * D].T for i in range(3)]
    E = E0
    packs0 = np.concatenate([host(L0_ffn_W1).transpose(0, 2, 1), down_rows(host(L0_ffn_W2)),
                             host(L0_ffn_b1).reshape(E, CH, P).transpose(0, 2, 1),
                             np.broadcast_to(host(L0_ffn_b2)[:, None], (E, P, D))], 2)
    experts = lambda routed, shared: np.concatenate([host(routed), host(shared)[None]])
    packs1 = np.concatenate([experts(L1_ffn_routed_gate, L1_ffn_shared_gate).transpose(0, 2, 1),
                             experts(L1_ffn_routed_up, L1_ffn_shared_up).transpose(0, 2, 1),
                             down_rows(experts(L1_ffn_routed_down, L1_ffn_shared_down))], 2)
    arrays = {"x": host(L0_attn_encodings).reshape(TOKENS, D), "constants": shape_constants(), "gate0": host(L0_ffn_Wg).T,
              "gate1": host(L1_ffn_router_w).T, "packs0": packs0, "packs1": packs1}
    arrays |= {f"att0_{i}": a for i, a in enumerate(att0)} | {f"att1_{i}": a for i, a in enumerate(att1)}
    arrays = {n: np.ascontiguousarray(a) for n, a in arrays.items()}

    nc = bacc.Bacc("TRN2", target_bir_lowering=False, num_devices=1)
    ap = {n: nc.dram_tensor(f"in_{n}", a.shape, mybir.dt.from_np(a.dtype), kind="ExternalInput").ap() for n, a in arrays.items()}
    out = nc.dram_tensor("out", [TOKENS, D], F32, kind="ExternalOutput").ap()
    program(nc, ap["x"], ap["constants"], ap["gate0"], ap["gate1"], [ap[f"att0_{i}"] for i in range(len(att0))],
            [ap[f"att1_{i}"] for i in range(len(att1))], ap["packs0"], ap["packs1"], out)
    ran = run_bass_kernel_spmd(nc, [{f"in_{n}": a for n, a in arrays.items()}], core_ids=[0])
    return ran.results[0]["out"].reshape(BATCH, SEQ, D)
```
